# Optimizing a Trainium2 kernel written in Bass

```python
import numpy as np
import jax
import jax.numpy as jnp

def _softmax(x, axis=-1):
    return jax.nn.softmax(x, axis=axis)

def _gelu(x):
    return jax.nn.gelu(x, approximate=True)

def _silu(x):
    return jax.nn.silu(x)

def _sigmoid(x):
    return jax.nn.sigmoid(x)

def _layernorm(x, axis=-1, eps=1e-05):
    m = jnp.mean(x, axis=axis, keepdims=True)
    v = jnp.var(x, axis=axis, keepdims=True)
    return (x - m) / jnp.sqrt(v + eps)

def _scatter_add(tgt, idx, src, axis=0):
    return tgt.at[idx].add(src)

def _segment_sum(src, seg, n):
    return jax.ops.segment_sum(src, seg, n)
kernel_name = 'mk_gps_d1_gnn_r8_cc8d86'

def setup_inputs(seed: int=0):
    np.random.seed(seed)
    _w = jnp.asarray

    def _rec_inputs():
        import jax
        import jax.numpy as jnp
        _gk = jax.random.key(seed)
        x = -7.329e-05 + 0.9999 * jax.random.normal(jax.random.fold_in(_gk, 1), (1250, 512), jnp.float32)
        _s = jax.random.randint(jax.random.fold_in(_gk, 2), (20000,), 0, 1250, jnp.int32)
        _d = jax.random.randint(jax.random.fold_in(_gk, 3), (20000,), 0, 1250, jnp.int32)
        _loop = jnp.arange(1250, dtype=jnp.int32)
        src = jnp.concatenate([_s, _d, _loop])
        dst = jnp.concatenate([_d, _s, _loop])
        _o = jnp.argsort(dst, stable=True)
        src = src[_o]
        dst = dst[_o]
        return (x, src, dst)
    x, src, dst = _rec_inputs()

    def _L0_gnn_setup():
        import jax, jax.numpy as jnp
        import numpy as np
        N, D, E, L = (12500, 512, 400000, 2)
        BN_EPS = 1e-05

        def _prelu(x, a):
            return jnp.where(x > 0, x, a * x)
        key = jax.random.key(seed)
        ks = jax.random.split(key, 12)
        s = 1.0 / np.sqrt(D)
        return {'x': jax.random.normal(ks[0], (N, D), dtype=jnp.float32), 'edge_index': jax.random.randint(ks[1], (2, E), 0, N, dtype=jnp.int64), 'lin_W': jax.random.uniform(ks[2], (D, D), jnp.float32, -s, s), 'lin_b': jax.random.uniform(ks[3], (D,), jnp.float32, -s, s), 'lin_a': jnp.full((D,), 0.25, dtype=jnp.float32), 'conv_W1': jax.random.uniform(ks[4], (L, D, D), jnp.float32, -s, s), 'conv_b1': jax.random.uniform(ks[5], (L, D), jnp.float32, -s, s), 'conv_a': jnp.full((L,), 0.25, dtype=jnp.float32), 'conv_W2': jax.random.uniform(ks[6], (L, D, D), jnp.float32, -s, s), 'conv_b2': jax.random.uniform(ks[7], (L, D), jnp.float32, -s, s), 'bn_gamma': jnp.ones((L, D), dtype=jnp.float32), 'bn_beta': jnp.zeros((L, D), dtype=jnp.float32)}
    _L0_gnn_all = _L0_gnn_setup()
    _L0_gnn_in = {k: v for k, v in _L0_gnn_all.items() if k in ('lin_W', 'lin_b', 'lin_a', 'conv_W1', 'conv_b1', 'conv_a', 'conv_W2', 'conv_b2', 'bn_gamma', 'bn_beta')}
    del _L0_gnn_all

    def _L0_mix_setup():
        import jax, jax.numpy as jnp
        import numpy as np
        HEADS = 8
        DIM_HEAD = 64
        LN_EPS = 1e-05
        key = jax.random.key(seed)
        k1, k2, k3, k4, k5 = jax.random.split(key, 5)
        B, N, C = (8, 512, 512)
        dim = HEADS * DIM_HEAD
        x = jax.random.normal(k1, (B, N, C), dtype=jnp.float32)
        w_qkv = jax.random.normal(k2, (C, dim * 3), dtype=jnp.float32) * (1.0 / np.sqrt(C))
        w_out = jax.random.normal(k3, (dim, C), dtype=jnp.float32) * (1.0 / np.sqrt(dim))
        b_out = jax.random.normal(k4, (C,), dtype=jnp.float32) * 0.01
        ln_scale = jnp.ones((C,), dtype=jnp.float32) + 0.02 * jax.random.normal(k5, (C,), dtype=jnp.float32)
        return {'x': x, 'w_qkv': w_qkv, 'w_out': w_out, 'b_out': b_out, 'ln_scale': ln_scale}
    _L0_mix_all = _L0_mix_setup()
    _L0_mix_in = {k: v for k, v in _L0_mix_all.items() if k in ('w_qkv', 'w_out', 'b_out', 'ln_scale')}
    del _L0_mix_all

    def _L0_ffn_setup():
        import jax, jax.numpy as jnp
        import numpy as np
        B, S, D, F, E = (8, 512, 512, 256, 8)
        INIT_LAMBDA = 0.2
        LN_EPS = 1e-05
        LN_MERGE = 0.03
        key = jax.random.key(seed)
        ks = jax.random.split(key, 12)
        n = lambda k, shp, s=1.0: jax.random.normal(k, shp, dtype=jnp.float32) * s
        return {'hidden_states': n(ks[0], (B, S, D)), 'gfc1_w': n(ks[1], (D, D), 0.01), 'gfc1_b': jnp.zeros((D,), jnp.float32), 'gfc2_w': n(ks[2], (E, D), 0.01), 'gfc2_b': jnp.full((E,), INIT_LAMBDA, dtype=jnp.float32), 'W1': n(ks[3], (F, D), 0.02), 'b1': jnp.zeros((F,), jnp.float32), 'W2': n(ks[4], (D, F), 0.02), 'b2': jnp.zeros((D,), jnp.float32), 'ln_g': jnp.ones((D,), jnp.float32), 'ln_b': jnp.zeros((D,), jnp.float32), 'tv_W1': n(ks[5], (E, F, D), 0.02), 'tv_b1': n(ks[6], (E, F), 0.02), 'tv_W2': n(ks[7], (E, D, F), 0.02), 'tv_b2': n(ks[8], (E, D), 0.02), 'tv_ln_g': n(ks[9], (E, D), 0.02), 'tv_ln_b': n(ks[10], (E, D), 0.02)}
    _L0_ffn_all = _L0_ffn_setup()
    _L0_ffn_in = {k: v for k, v in _L0_ffn_all.items() if k in ('gfc1_w', 'gfc1_b', 'gfc2_w', 'gfc2_b', 'W1', 'b1', 'W2', 'b2', 'ln_g', 'ln_b', 'tv_W1', 'tv_b1', 'tv_W2', 'tv_b2', 'tv_ln_g', 'tv_ln_b')}
    del _L0_ffn_all
    return {'x': x, 'src': src, 'dst': dst, 'L0_gnn_lin_W': _L0_gnn_in['lin_W'], 'L0_gnn_lin_b': _L0_gnn_in['lin_b'], 'L0_gnn_lin_a': _L0_gnn_in['lin_a'], 'L0_gnn_conv_W1': _L0_gnn_in['conv_W1'], 'L0_gnn_conv_b1': _L0_gnn_in['conv_b1'], 'L0_gnn_conv_a': _L0_gnn_in['conv_a'], 'L0_gnn_conv_W2': _L0_gnn_in['conv_W2'], 'L0_gnn_conv_b2': _L0_gnn_in['conv_b2'], 'L0_gnn_bn_gamma': _L0_gnn_in['bn_gamma'], 'L0_gnn_bn_beta': _L0_gnn_in['bn_beta'], 'L0_mix_w_qkv': _L0_mix_in['w_qkv'], 'L0_mix_w_out': _L0_mix_in['w_out'], 'L0_mix_b_out': _L0_mix_in['b_out'], 'L0_mix_ln_scale': _L0_mix_in['ln_scale'], 'L0_ffn_gfc1_w': _L0_ffn_in['gfc1_w'], 'L0_ffn_gfc1_b': _L0_ffn_in['gfc1_b'], 'L0_ffn_gfc2_w': _L0_ffn_in['gfc2_w'], 'L0_ffn_gfc2_b': _L0_ffn_in['gfc2_b'], 'L0_ffn_W1': _L0_ffn_in['W1'], 'L0_ffn_b1': _L0_ffn_in['b1'], 'L0_ffn_W2': _L0_ffn_in['W2'], 'L0_ffn_b2': _L0_ffn_in['b2'], 'L0_ffn_ln_g': _L0_ffn_in['ln_g'], 'L0_ffn_ln_b': _L0_ffn_in['ln_b'], 'L0_ffn_tv_W1': _L0_ffn_in['tv_W1'], 'L0_ffn_tv_b1': _L0_ffn_in['tv_b1'], 'L0_ffn_tv_W2': _L0_ffn_in['tv_W2'], 'L0_ffn_tv_b2': _L0_ffn_in['tv_b2'], 'L0_ffn_tv_ln_g': _L0_ffn_in['tv_ln_g'], 'L0_ffn_tv_ln_b': _L0_ffn_in['tv_ln_b']}

def reference(x, src, dst, L0_gnn_lin_W, L0_gnn_lin_b, L0_gnn_lin_a, L0_gnn_conv_W1, L0_gnn_conv_b1, L0_gnn_conv_a, L0_gnn_conv_W2, L0_gnn_conv_b2, L0_gnn_bn_gamma, L0_gnn_bn_beta, L0_mix_w_qkv, L0_mix_w_out, L0_mix_b_out, L0_mix_ln_scale, L0_ffn_gfc1_w, L0_ffn_gfc1_b, L0_ffn_gfc2_w, L0_ffn_gfc2_b, L0_ffn_W1, L0_ffn_b1, L0_ffn_W2, L0_ffn_b2, L0_ffn_ln_g, L0_ffn_ln_b, L0_ffn_tv_W1, L0_ffn_tv_b1, L0_ffn_tv_W2, L0_ffn_tv_b2, L0_ffn_tv_ln_g, L0_ffn_tv_ln_b):
    import jax
    import jax.numpy as jnp

    def _L0_gnn_ref(x, edge_index, lin_W, lin_b, lin_a, conv_W1, conv_b1, conv_a, conv_W2, conv_b2, bn_gamma, bn_beta):
        import jax, jax.numpy as jnp
        import numpy as np
        N, D, E, L = (12500, 512, 400000, 2)
        BN_EPS = 1e-05

        def _prelu(x, a):
            return jnp.where(x > 0, x, a * x)
        n = x.shape[0]
        src, dst = (edge_index[0], edge_index[1])
        x = _prelu(x @ lin_W.T + lin_b, lin_a)
        for l in range(L):
            agg = jax.ops.segment_sum(x[src], dst, num_segments=n)
            h = x + agg
            h = _prelu(h @ conv_W1[l].T + conv_b1[l], conv_a[l])
            h = h @ conv_W2[l].T + conv_b2[l]
            mean = h.mean(axis=0)
            var = ((h - mean) ** 2).mean(axis=0)
            h = (h - mean) * jax.lax.rsqrt(var + BN_EPS) * bn_gamma[l] + bn_beta[l]
            x = jax.nn.relu(h)
        return x

    def _L0_mix_ref(x, w_qkv, w_out, b_out, ln_scale):
        import jax, jax.numpy as jnp
        import numpy as np
        HEADS = 8
        DIM_HEAD = 64
        LN_EPS = 1e-05
        B, N, C = x.shape
        H, D = (HEADS, DIM_HEAD)
        qkv = jnp.einsum('bnc,cf->bnf', x, w_qkv)
        q, k, v = jnp.split(qkv, 3, axis=-1)
        q = q.reshape(B, N, H, D)
        k = k.reshape(B, N, H, D)
        v = v.reshape(B, N, H, D)
        q = jax.nn.softmax(q, axis=-1)
        k = jax.nn.softmax(k, axis=1)
        q = q / jnp.sqrt(jnp.asarray(D, dtype=q.dtype))
        v = v / N
        context = jnp.einsum('bnhd,bnhe->bhde', k, v)
        out = jnp.einsum('bhde,bnhd->bhen', context, q)
        out = out.transpose(0, 3, 1, 2).reshape(B, N, H * D)
        out = jnp.einsum('bnf,fc->bnc', out, w_out) + b_out
        mu = jnp.mean(out, axis=-1, keepdims=True)
        var = jnp.mean(jnp.square(out - mu), axis=-1, keepdims=True)
        out = (out - mu) * jax.lax.rsqrt(var + LN_EPS) * ln_scale
        return out

    def _L0_ffn_ref(hidden_states, gfc1_w, gfc1_b, gfc2_w, gfc2_b, W1, b1, W2, b2, ln_g, ln_b, tv_W1, tv_b1, tv_W2, tv_b2, tv_ln_g, tv_ln_b):
        import jax, jax.numpy as jnp
        import numpy as np
        B, S, D, F, E = (8, 512, 512, 256, 8)
        INIT_LAMBDA = 0.2
        LN_EPS = 1e-05
        LN_MERGE = 0.03
        x = hidden_states
        gh = jax.nn.relu(jnp.einsum('bsd,hd->bsh', x, gfc1_w) + gfc1_b)
        g = (jnp.einsum('bsh,eh->bse', gh, gfc2_w) + gfc2_b).mean(axis=1)
        W1m = W1 + jnp.einsum('be,efd->bfd', g, tv_W1)
        b1m = b1 + g @ tv_b1
        W2m = W2 + jnp.einsum('be,edf->bdf', g, tv_W2)
        b2m = b2 + g @ tv_b2
        lng = ln_g + LN_MERGE * (tv_ln_g - ln_g).sum(axis=0)
        lnb = ln_b + LN_MERGE * (tv_ln_b - ln_b).sum(axis=0)
        h = jax.nn.relu(jnp.einsum('bsd,bfd->bsf', x, W1m) + b1m[:, None, :])
        out = jnp.einsum('bsf,bdf->bsd', h, W2m) + b2m[:, None, :]
        res = x + out
        mu = res.mean(axis=-1, keepdims=True)
        var = res.var(axis=-1, keepdims=True)
        return (res - mu) * jax.lax.rsqrt(var + LN_EPS) * lng + lnb
    edge_index = jnp.stack([src, dst])
    xn = _layernorm(x, axis=-1)
    x = x + _L0_gnn_ref(xn, edge_index, L0_gnn_lin_W, L0_gnn_lin_b, L0_gnn_lin_a, L0_gnn_conv_W1, L0_gnn_conv_b1, L0_gnn_conv_a, L0_gnn_conv_W2, L0_gnn_conv_b2, L0_gnn_bn_gamma, L0_gnn_bn_beta) + _L0_mix_ref(xn[None], L0_mix_w_qkv, L0_mix_w_out, L0_mix_b_out, L0_mix_ln_scale)[0]
    x = x + _L0_ffn_ref(_layernorm(x, axis=-1)[None], L0_ffn_gfc1_w, L0_ffn_gfc1_b, L0_ffn_gfc2_w, L0_ffn_gfc2_b, L0_ffn_W1, L0_ffn_b1, L0_ffn_W2, L0_ffn_b2, L0_ffn_ln_g, L0_ffn_ln_b, L0_ffn_tv_W1, L0_ffn_tv_b1, L0_ffn_tv_W2, L0_ffn_tv_b2, L0_ffn_tv_ln_g, L0_ffn_tv_ln_b)[0]
    return x

_drawn_inputs = setup_inputs


def setup_inputs(seed=0):
    import zlib

    import numpy as np

    out = dict(_drawn_inputs(seed))
    spreads = {'L0_gnn_lin_a': (0.25, 0.2),
     'L0_gnn_conv_a': (0.25, 0.2),
     'L0_gnn_bn_gamma': (1.0, 0.2),
     'L0_gnn_bn_beta': (0.0, 0.1),
     'L0_ffn_gfc1_b': (0.0, 0.1),
     'L0_ffn_gfc2_b': (0.20000000298023224, 0.2),
     'L0_ffn_b1': (0.0, 0.1),
     'L0_ffn_b2': (0.0, 0.1),
     'L0_ffn_ln_g': (1.0, 0.2),
     'L0_ffn_ln_b': (0.0, 0.1)}
    factors = {}
    for name, (base, spread) in spreads.items():
        noise = np.random.default_rng([zlib.crc32(name.encode()), seed]).standard_normal(out[name].shape)
        drawn = base * np.exp(spread * noise) if base else spread * noise
        out[name] = jnp.asarray(drawn.astype(out[name].dtype))
    for name, factor in factors.items():
        out[name] = (out[name] * factor).astype(out[name].dtype)
    return out
```

```python
from contextlib import ExitStack

import concourse.bass as bass
from concourse import mybir

F32 = mybir.dt.float32
F16 = mybir.dt.float16
I32 = mybir.dt.int32
ALU = mybir.AluOpType
ACT = mybir.ActivationFunctionType
AX = mybir.AxisListType

N, D, H, F, E, L, EDGES = 1250, 512, 8, 256, 8, 2, 41250
DH = D // H
P = 125
T = N // P
KB = D // 128
FB = F // 128
CH = 2 * P
J = N // CH
COLS = EDGES // P
WIN = 25
NW = N // WIN
WC = 9
KEYS = COLS + WC
WK = T * WIN
OHS = 2 * (WC * (P + WK) + 1)
HT = T // 2
LN_EPS, BN_EPS, LN_MERGE = 1e-5, 1e-5, 0.03
F16_EXACT = 2048.0
LO_TILES = 8

S_X, S_W, S_H, S_K, S_Q, S_M = 16.0, 256.0, 1 / 16, 256.0, 1024.0, 256.0
S_XW = 1 / (S_X * S_W)

COL = {}
for _name, _n in (("lin_b", 4), ("lin_a", 4), ("b1", 8), ("b2", 8), ("gamma", 8), ("beta", 8), ("conv_a", 2),
                  ("gfc1_b", 4), ("ffn_b1", 2), ("tv_b1", 16), ("gfc2_b", 8), ("gfc2_bc", 1)):
    COL[_name] = (sum(n for _, n in COL.values()), _n)
NCOL = sum(n for _, n in COL.values())

WEIGHTS = ["lin", "k", "q", "v", "out", "up0", "down0", "up1", "down1", "gate"]
SLOTS = 3
WINDOWS = {"lin": 2, "k": 2, "q": 0, "v": 4, "mix": 2}

USES = {
    "n": [("q", T, "dve", 0), ("v", T, "dve", 1), ("m", KB, "dve", 1), ("mix", T, "dve", 0), ("ffn2", T, "dve", 0)],
    "t": [("lin", 20, "act", 0), ("k", 20, "dve", 0), ("agg0", 20, "dve", 1), ("up0", 20, "act", 0),
          ("down0", 20, "act", 0), ("agg1", 20, "dve", 1), ("up1", 20, "act", 0), ("down1", 20, "act", 0),
          ("gate", 20, "act", 0), ("ffn1", 10, "act", 0)],
    "x": [("xn", T, "dve", 1), ("x0", T, "dve", 1), ("kn", T, "dve", 1),
          ("qt", T, "dve", 1), ("ctx", 2, "dve", 1), ("x1", T, "dve", 1), ("gnn", T, "dve", 0),
          ("x2", T, "dve", 1), ("rows", 2, "dve", 0), ("g", 2, "dve", 0)],
}
RING = {"n": 2, "t": 4, "x": 2}
BANKS_FROM = {"q": ("t", "k", 17), "agg0": ("n", "mix", 9), "ffn2": ("t", "ffn1", 9)}


def before(family, phase, who=None, high=False):
    total = 0
    for name, uses, by, hi in USES[family]:
        if name == phase:
            return total
        if (who is None or by == who) and (hi or not high):
            total += uses
    raise KeyError(phase)


def entry(family, phase):
    return next(u for u in USES[family] if u[0] == phase)


def first_window(phase):
    at = 0
    for name, per in WINDOWS.items():
        if name == phase:
            return at
        at += per * J
    raise KeyError(phase)


def window_list(phase, i, part=0, parts=1):
    n = WINDOWS.get(phase, 0) // parts
    return [((n * parts) * i + (first_window(phase) + n * part + c), (n * part + c) % 2) for c in range(n)]


assert sum(WINDOWS.values()) * J == NW and J == HT

READER = {"lin": ("t", "lin"), "k": ("t", "k"), "q": ("n", "q"), "v": ("n", "v"), "out": ("n", "m"), "up0": ("t", "up0"),
          "down0": ("t", "down0"), "up1": ("t", "up1"), "down1": ("t", "down1"), "gate": ("t", "gate")}


def gps_block(nc, dram):
    with ExitStack() as ctx:
        def sb(name, shape, dt=F32):
            return ctx.enter_context(nc.sbuf_tensor(name, shape, dt))

        def sem(name):
            return ctx.enter_context(nc.semaphore(name))

        ps = ctx.enter_context(nc.psum_tensor("ps", [128, 8, 512], F32))

        def bank(family, slot):
            if family == "t":
                return ps[:, slot, 0:CH]
            return ps[:, {"n": 0, "x": 4}[family] + slot, :]

        x = sb("x", [P, T, D])
        r1 = sb("r1", [128, T * D])
        r2 = sb("r2", [128, T * D])
        r3 = sb("r3", [128, T * D])
        late = sb("late", [128, 2 * T * D + N * T // 2])
        r4, r5 = late[:, 0:T * D], late[:, T * D:2 * T * D]
        adj = late[0:P, 2 * T * D:].bitcast(F16).rearrange("p (h d) -> p h d", h=T)

        def nat32(r):
            return r[0:P].rearrange("p (t c) -> p t c", t=T)

        def nat16(r):
            return r[0:P].bitcast(F16).rearrange("p (h t c) -> p h t c", h=2, t=T)

        def tr32(r):
            return r[:, 0:KB * N].rearrange("p (k n) -> p k n", k=KB)

        def tr16(r, blocks=KB):
            return r[:, 0:blocks * N].bitcast(F16).rearrange("p (h k n) -> p h k n", h=2, k=blocks)

        xn_nat, xn_t = nat32(r5), tr16(r1)
        gnn_t, gnn_nat = tr32(r3), nat16(r2)
        k_t, k_nat = tr32(r4), nat16(r5)
        q_nat, q_t = nat32(r3), tr16(r1)
        v_nat = nat16(r4)
        mm = r5[:, 0:KB * D].bitcast(F16).rearrange("p (h k n) -> p h k n", h=2, k=KB)
        mix_nat = nat32(r3)
        h_t, a_t = tr16(r4), tr16(r5)
        x2_nat, x2_t = nat32(r2), tr16(r1)
        hid_t = tr16(r3, FB)
        tv = late[:, 0:2 * E * KB * F].rearrange("p (w e n) -> p w e n", w=2, e=E)

        stage = sb("stage", [128, KB * D])
        wm32 = stage[:, :].rearrange("p (w n) -> p w n", w=2)
        wslot = sb("wslot", [128, SLOTS, 2, KB, D], F16)
        wm16 = wslot[:, 2].rearrange("p h k n -> p (h k n)").rearrange("p (w h n) -> p w h n", w=2, h=2)
        w1m = wm16[:, 0].rearrange("p h (k f) -> p h k f", k=KB)
        w2m = wm16[:, 1].rearrange("p h (k c) -> p h k c", k=FB)
        assert WEIGHTS.index("gate") % SLOTS == 0

        ohs = sb("ohs", [128, OHS], F16)
        oh_s = ohs[0:P, 0:2 * (WC * P + 1)].rearrange("p (b n) -> p b n", b=2)[:, :, 0:WC * P].rearrange(
            "p b (s w) -> p b s w", w=WC)
        oh_d = ohs[0:P, 2 * (WC * P + 1):].rearrange("p (b d w h) -> p b d w h", b=2, w=WC, h=T)
        act_tmp = ohs[:, 0:2 * KB * CH].bitcast(F32).rearrange("p (m n) -> p m n", m=KB)
        negative = ohs[:, 2 * KB * CH:4 * KB * CH].bitcast(F32).rearrange("p (m n) -> p m n", m=KB)
        tvrow = ohs[0:E, 2 * KB * CH:2 * KB * CH + 6 * D].bitcast(F32).rearrange("e (r c) -> e r c", r=3)
        lo_a = r1[0:P, 0:LO_TILES * N // 2].bitcast(F16).rearrange("p (h d) -> p h d", h=LO_TILES)
        lo_b = ohs[0:P, OHS - (T - LO_TILES) * N:].rearrange("p (h d) -> p h d", h=T - LO_TILES)

        ident = sb("ident", [128, 128])
        cols = sb("cols", [128, NCOL])
        rows = sb("rows", [P, 2, D])
        keys = sb("keys", [P, KEYS])
        sources = sb("sources", [P, KEYS], F16)
        iota_mem = sb("iota", [P, WK + P * WC + 1], F16)
        iota_d = iota_mem[:, 0:WK].rearrange("p (d h) -> p d h", h=T)
        iota_s = iota_mem[:, WK:WK + P * WC].rearrange("p (s w) -> p s w", w=WC)
        b2_row = iota_mem[:, 0:2 * D].bitcast(F32)
        win_key = sb("win_key", [P, NW])
        rel = sb("rel", [P, 2, WC, T], F16)
        window_at = sb("window_at", [1, NW], I32)
        adj_sum = sb("adj_sum", [P, NW])
        chk = sb("chk", [P, 4])
        ones = sb("ones", [128, 128])
        rare = sb("rare", [1, 2], I32)
        stat = sb("stat", [128, KB * J * 6])
        mv = sb("mv", [128, T, 2])
        std = sb("std", [128, T])
        eps = sb("eps", [128, 2])
        rstd = sb("rstd", [128, T])
        shift = sb("shift", [128, T])
        kmax = sb("kmax", [128, KB, J])
        kneg = sb("kneg", [128, KB])
        ksum = sb("ksum", [128, KB])
        krec = sb("krec", [128, KB])
        qmax = sb("qmax", [P, T, H])
        qsum = sb("qsum", [P, T, H])
        ctx16 = sb("ctx16", [128, 2, KB, 128], F16)
        bias_a = sb("bias_a", [128, 2 * KB])
        gsum = sb("gsum", [128, KB, J])
        gmean = sb("gmean", [128, KB])
        gbc = ctx16[:, :, :, :].rearrange("p h k n -> p (h k n)").bitcast(F32).rearrange("p (k n) -> p k n", k=KB)
        gcol = sb("gcol", [128, E])
        grow = sb("grow", [E, P])
        b1m = sb("b1m", [128, FB])
        gfc2 = sb("gfc2", [128, KB, E])

        ints = r2[0:P, 0:2 * COLS].bitcast(I32).rearrange("p (a c) -> p a c", a=2)
        heads_i = r2[0:NW, 700:700 + COLS].bitcast(I32)
        heads = r2[0:NW, 1100:1100 + COLS]
        heads_lt = r2[0:NW, 1500:1500 + COLS]
        iota_i = r2[0:P, 1900:1900 + WK + NW].bitcast(I32)
        src_tile = r2[0:P, 2400:2400 + COLS]
        first = r2[0:NW, 2800:2802]
        lin_neg = r2[:, 3000:3000 + KB * CH].rearrange("p (m n) -> p m n", m=KB)
        first_i = r2[0:NW, 2802:2803].bitcast(I32)

        def col(name, i=0, n=1):
            return cols[:, COL[name][0] + i:COL[name][0] + i + n]

        got_edges, got_cols, got_rows, got_w = sem("got_edges"), sem("got_cols"), sem("got_rows"), sem("got_w")
        got_x = [sem(f"got_x{i}") for i in range(2)]
        got_tvrow, got_wm, got_tv, got_ln = sem("got_tvrow"), sem("got_wm"), sem("got_tv"), sem("got_ln")
        stored = sem("stored")
        full = {f: sem(f"{f}_full") for f in USES}
        high = {f: sem(f"{f}_high") for f in USES}
        free = {(f, e): sem(f"{f}_free_{e}") for f in USES for e in ("act", "dve")}
        w_scaled, w_high, w_split = sem("w_scaled"), sem("w_high"), sem("w_split")
        consts, iotas = sem("consts"), sem("iotas")
        dve_step, act_step, pool_step = sem("dve_step"), sem("act_step"), sem("pool_step")
        firsts, firsts_row, window_ready = sem("firsts"), sem("firsts_row"), sem("window_ready")
        rel_ready, oh_ready, adj_full, adj_freed = sem("rel_ready"), sem("oh_ready"), sem("adj_full"), sem("adj_freed")
        chk_ready, chk_sum, rare_ready = sem("chk_ready"), sem("chk_sum"), sem("rare_ready")
        g_oh, g_used, g_full, g_high, g_low = sem("g_oh"), sem("g_used"), sem("g_full"), sem("g_high"), sem("g_low")
        adj_ready = sem("adj_ready")
        var_ready, std_ready, norm_ready, ln_done = sem("var_ready"), sem("std_ready"), sem("norm_ready"), sem("ln_done")
        k_max, k_exp, q_sub, q_exp, q_rec, q_soft = (sem(n) for n in ("k_max", "k_exp", "q_sub", "q_exp", "q_rec", "q_soft"))
        mix_scaled, mixed = sem("mix_scaled"), sem("mixed")
        z_ready, z_norm, layer_out = sem("z_ready"), sem("z_norm"), sem("layer_out")
        g_acc, g_bc, g_mm, g_vec, b2_ready = sem("g_acc"), sem("g_bc"), sem("g_mm"), sem("g_vec"), sem("b2_ready")
        wm_done, wm_high, wm_split, x2b_ready, xb_ready = (sem(n) for n in ("wm_done", "wm_high", "wm_split", "x2b_ready", "xb_ready"))
        gnn_added, res_ready, out_ready = sem("gnn_added"), sem("res_ready"), sem("out_ready")
        x2_done, b2_sum = sem("x2_done"), sem("b2_sum")
        lin_out, prelu_out, hid_high = sem("lin_out"), sem("prelu_out"), sem("hid_high")
        tmp_free, bias_ready = sem("tmp_free"), sem("bias_ready")

        def wait_full(eng, family, phase, i):
            eng.wait_ge(full[family], before(family, phase) + i + 1)

        def wait_high(eng, family, phase, i):
            eng.wait_ge(high[family], before(family, phase, high=True) + i + 1)

        def wait_done(eng, family, phase, n):
            who = entry(family, phase)[2]
            eng.wait_ge(free[family, who], RING[family] + before(family, phase, who) + n)

        def wait_bank(pe, family, phase, i, slot, ring=None):
            names = [u[0] for u in USES[family]]
            _, _, who, _ = entry(family, phase)
            ring_ = RING[family]
            pe.wait_ge(free[family, who], before(family, phase, who) + i + 1 + ring_ - (ring or ring_))
            if names.index(phase):
                last, uses, by, _ = USES[family][names.index(phase) - 1]
                if by != who:
                    pe.wait_ge(free[family, by], before(family, last, by) + uses + slot + 1)
            if phase in BANKS_FROM and slot < 2:
                family, last, uses = BANKS_FROM[phase]
                wait_done(pe, family, last, uses + slot)

        def weight(name):
            return wslot[:, WEIGHTS.index(name) % SLOTS]

        def wait_weight(pe, name):
            pe.wait_ge(w_split, WEIGHTS.index(name) + 1)

        block = ctx.enter_context(nc.Block())

        @block.sync
        def _(sp):
            sp.dma_start(ints, dram["edges"]).then_inc(got_edges, 16)
            sp.dma_start(heads_i, dram["heads"]).then_inc(got_edges, 16)
            sp.dma_start(stage[:, :], dram["w_lin"]).then_inc(got_w, 16)
            sp.dma_start(cols[:, :], dram["cols"]).then_inc(got_cols, 16)
            sp.dma_start(rows[:, 0:2, :], dram["mix_rows"]).then_inc(got_rows, 16)
            sp.dma_start(gfc2[:, :, :], dram["gfc2"]).then_inc(got_tvrow, 16)
            for i, name in enumerate(WEIGHTS[1:], 1):
                sp.wait_ge(w_split, i)
                sp.dma_start(stage[:, :], dram["w_" + name]).then_inc(got_w, 16)
            sp.wait_ge(mixed, T)
            sp.dma_start(rows[:, :, :], dram["ln_rows"][:, 0:2]).then_inc(got_ln, 16)
            sp.wait_ge(adj_ready, 1)
            sp.dma_start(b2_row, dram["ln_rows"][:, 2]).then_inc(got_ln, 16)
            sp.wait_ge(w_split, len(WEIGHTS))
            sp.dma_start(stage[:, :], dram["w_ffn"]).then_inc(got_wm, 16)
            sp.wait_ge(full["t"], before("t", "gate"))
            sp.dma_start(tvrow, dram["tv_rows"]).then_inc(got_tvrow, 16)
            for w in range(2):
                sp.dma_start(tv[:, w], dram["tv"][:, w]).then_inc(got_tv, 16)
            for t in range(T):
                sp.wait_ge(out_ready, t + 1)
                sp.dma_start(dram["out"][:, t, :], x2_nat[:, t, :]).then_inc(stored, 16)
            sp.wait_ge(stored, 16 * T)

        @block.tensor
        def _(pe):
            for f in USES:
                pe.sem_inc(free[f, "act"], RING[f])
                pe.sem_inc(free[f, "dve"], RING[f])
            pe.sem_inc(adj_full, 2)
            pe.sem_inc(adj_freed, 2)
            pe.sem_inc(g_used, 1)
            pe.sem_inc(tmp_free, KB)

            def window(w, slot):
                pe.wait_ge(oh_ready, w + 1)
                pe.wait_ge(adj_freed, w + 1)
                for c in range(WC):
                    mm_ = nc.tensor.matmul(ps[0:P, 6 + slot, 0:WK], oh_s[:, slot, :, c], oh_d[:, slot, :, c, :],
                                           start=(c == 0), stop=(c == WC - 1))
                mm_.then_inc(adj_full, 1)

            def windows(phase, i, part=0, parts=1):
                for w, slot in window_list(phase, i, part, parts):
                    window(w, slot)

            def passes(out, stat_, mov, blocks, start=True, stop=True):
                n = 0
                for b in range(blocks):
                    for hs, hm in ((0, 0), (0, 1), (1, 0)):
                        last = nc.tensor.matmul(out, stat_(hs, b), mov(hm, b), start=start and n == 0,
                                                stop=stop and n == 3 * blocks - 1)
                        n += 1
                return last

            def transposed(phase, w, mov, blocks=KB, outs=KB, ready=None):
                with pe.Fori(0, J) as j:
                    if ready:
                        ready(j)
                    for m in range(outs):
                        wait_bank(pe, "t", phase, outs * j + m, m, ring=outs)
                        passes(bank("t", m), lambda h, b: w[:, h, b, m * 128:(m + 1) * 128],
                               lambda h, b: mov[:, h, b, bass.ts(j, CH)], blocks).then_inc(full["t"], 1)
                    windows(phase, j)

            def natural(phase, mov, w, blocks=KB, ready=None):
                with pe.Fori(0, HT) as i:
                    if ready:
                        ready(i)
                    for c in range(2):
                        wait_bank(pe, "n", phase, 2 * i + c, c)
                        passes(bank("n", c)[0:P, :], lambda h, b: mov[:, h, b, bass.ts(2 * i + c, P)],
                               lambda h, b: w[:, h, b, :], blocks).then_inc(full["n"], 1)
                        windows(phase, i, c, 2)

            def flip_to_t(phase, src, ready):
                for t in range(T):
                    ready(t)
                    wait_bank(pe, "x", phase, t, t % 2)
                    for m in range(KB):
                        mm_ = nc.tensor.transpose(bank("x", t % 2)[:, m * P:(m + 1) * P],
                                                  src[:, t, m * 128:(m + 1) * 128], ident[0:P, 0:P])
                    mm_.then_inc(full["x"], 1)

            def flip_to_nat(phase, src, ready):
                for t in range(T):
                    ready(t)
                    wait_bank(pe, "x", phase, t, t % 2)
                    for m in range(KB):
                        mm_ = nc.tensor.transpose(bank("x", t % 2)[0:P, m * 128:(m + 1) * 128],
                                                  src[:, m, t * P:(t + 1) * P], ident[:, :])
                    mm_.then_inc(full["x"], 1)

            pe.wait_ge(consts, 1)
            pe.wait_ge(firsts, 1)
            nc.tensor.matmul(ps[0:1, 7, 0:NW], first[:, 1:2], ident[0:NW, 0:NW], start=True, stop=True).then_inc(firsts_row, 1)

            flip_to_t("xn", xn_nat, lambda t: pe.wait_ge(ln_done, t + 1))
            wait_weight(pe, "lin")
            transposed("lin", weight("lin"), xn_t, ready=lambda j: wait_done(pe, "x", "xn", 2 * j + 2))
            flip_to_nat("x0", gnn_t, lambda t: pe.wait_ge(lin_out, KB * (t // 2) + KB))
            wait_weight(pe, "k")
            transposed("k", weight("k"), xn_t)
            wait_weight(pe, "q")
            natural("q", xn_t, weight("q"))
            flip_to_nat("kn", k_t, lambda t: pe.wait_ge(k_exp, KB))
            wait_weight(pe, "v")
            natural("v", xn_t, weight("v"))
            flip_to_t("qt", q_nat, lambda t: pe.wait_ge(q_soft, t + 1))
            wait_done(pe, "n", "v", T)
            wait_done(pe, "x", "kn", T)
            for b in range(2):
                wait_bank(pe, "x", "ctx", b, b)
                for q in range(2):
                    part = slice((2 * b + q) * 128, (2 * b + q + 1) * 128)
                    last = passes(bank("x", b)[:, q * 128:(q + 1) * 128], lambda h, t: v_nat[:, h, t, part],
                                  lambda h, t: k_nat[:, h, t, part], T)
                last.then_inc(full["x"], 1)
            wait_weight(pe, "out")
            wait_done(pe, "x", "ctx", 2)
            for p in range(KB):
                wait_bank(pe, "n", "m", p, p % 2)
                passes(bank("n", p % 2), lambda h, b: ctx16[:, h, p, :], lambda h, b: weight("out")[:, h, p, :], 1
                       ).then_inc(full["n"], 1)
            wait_done(pe, "n", "m", KB)
            natural("mix", q_t, mm, ready=lambda i: wait_done(pe, "x", "qt", 2 * i + 2))

            pe.wait_ge(chk_ready, 1)
            nc.tensor.matmul(ps[0:1, 6, 0:2], ones[0:P, 0:1], chk[:, 0:2], start=True, stop=True).then_inc(chk_sum, 1)
            pe.wait_ge(rare_ready, 1)
            is_rare = pe.value_load(rare[0:1, 0:1], min_val=0, max_val=1)

            with pe.If(is_rare):
                with pe.Fori(0, NW) as w:
                    pe.wait_ge(g_low, w + 1)
                    nc.tensor.matmul(ps[0:P, 6, 0:WK], oh_s[:, 1, :, 0], oh_d[:, 0, :, 7, :], start=True, stop=False)
                    with pe.Fori(0, COLS // 2) as c:
                        pe.wait_ge(g_oh, w * (COLS // 2) + c + 2)
                        for b in range(2):
                            mm_ = nc.tensor.matmul(ps[0:P, 6, 0:WK], oh_s[:, 0, :, b], oh_d[:, 0, :, b, :],
                                                   start=False, stop=False)
                        mm_.then_inc(g_used, 1)
                    nc.tensor.matmul(ps[0:P, 6, 0:WK], oh_s[:, 1, :, 0], oh_d[:, 0, :, 7, :], start=False, stop=True
                                     ).then_inc(g_full, 1)

            def gather(phase, general):
                with pe.Fori(0, J) as j:
                    for m in range(KB):
                        wait_bank(pe, "t", phase, KB * j + m, m)
                        for h in range(T):
                            for p in range(2):
                                last = nc.tensor.matmul(bank("t", m), gnn_nat[:, p, h, m * 128:(m + 1) * 128],
                                                        adj[:, h, bass.ts(j, CH)], start=(h == 0 and p == 0),
                                                        stop=(not general and h == T - 1 and p == 1))
                        if general:
                            for h in range(T):
                                low = lo_a[:, h] if h < LO_TILES else lo_b[:, h - LO_TILES]
                                for p in range(2):
                                    last = nc.tensor.matmul(bank("t", m), gnn_nat[:, p, h, m * 128:(m + 1) * 128],
                                                            low[:, bass.ts(j, CH)], start=False,
                                                            stop=(h == T - 1 and p == 1))
                        last.then_inc(full["t"], 1)

            for layer in range(L):
                pe.wait_ge(adj_ready, 1)
                wait_done(pe, "x", "x1" if layer else "x0", T)
                with pe.If(is_rare):
                    gather(f"agg{layer}", True)
                with pe.Else():
                    gather(f"agg{layer}", False)
                wait_weight(pe, f"up{layer}")
                transposed(f"up{layer}", weight(f"up{layer}"), h_t,
                           ready=lambda j: wait_done(pe, "t", f"agg{layer}", KB * j + KB))
                wait_weight(pe, f"down{layer}")
                transposed(f"down{layer}", weight(f"down{layer}"), a_t,
                           ready=lambda j: pe.wait_ge(tmp_free, KB + 20 * layer + KB * j + KB))
                if layer == 0:
                    flip_to_nat("x1", gnn_t, lambda t: pe.wait_ge(layer_out, KB))
            flip_to_nat("gnn", gnn_t, lambda t: pe.wait_ge(layer_out, 2 * KB))

            flip_to_t("x2", x2_nat, lambda t: pe.wait_ge(ln_done, T + T + t + 1))
            wait_weight(pe, "gate")
            transposed("gate", weight("gate"), x2_t, ready=lambda j: wait_done(pe, "x", "x2", 2 * j + 2))
            pe.wait_ge(got_tvrow, 32)
            for r in range(2):
                wait_bank(pe, "x", "rows", r, r)
                nc.tensor.matmul(bank("x", r)[0:P, :], ones[0:E, 0:P], tvrow[:, r, :], start=True, stop=True
                                 ).then_inc(full["x"], 1)
            pe.wait_ge(g_bc, 1)
            wait_bank(pe, "x", "g", 0, 0)
            for m in range(KB):
                mm_ = nc.tensor.matmul(bank("x", 0)[:, 0:E], gbc[:, m, :], gfc2[:, m, :], start=(m == 0), stop=(m == KB - 1))
            mm_.then_inc(full["x"], 1)
            wait_bank(pe, "x", "g", 1, 1)
            for m in range(KB):
                mm_ = nc.tensor.matmul(bank("x", 1)[0:E, 0:P], gfc2[:, m, :], gbc[:, m, 0:P], start=(m == 0), stop=(m == KB - 1))
            mm_.then_inc(full["x"], 1)
            pe.wait_ge(g_vec, 1)
            nc.tensor.matmul(ps[0:P, 7, :], grow[:, :], tvrow[:, 2, :], start=True, stop=True).then_inc(b2_sum, 1)
            pe.wait_ge(wm_split, 1)
            transposed("ffn1", w1m, x2_t, outs=FB)
            pe.wait_ge(wm_split, 2)
            natural("ffn2", hid_t, w2m, blocks=FB,
                    ready=lambda i: pe.wait_ge(tmp_free, KB + 40 + FB * i + FB))

        @block.scalar
        def _(act):
            nc.scalar.preload_act_table(ACT.Sqrt)
            act.dma_start(x[:, HT:T, :], dram["x"][:, HT:T, :]).then_inc(got_x[1], 16)

            def split_weight(name):
                i = WEIGHTS.index(name)
                act.wait_ge(w_scaled, i + 1)
                if i >= SLOTS:
                    family, phase = READER[WEIGHTS[i - SLOTS]]
                    act.wait_ge(full[family], before(family, phase) + entry(family, phase)[1])
                nc.scalar.activation(wslot[:, i % SLOTS, 0].rearrange("p k n -> p (k n)"), stage[:, :], ACT.Copy
                                     ).then_inc(w_high, 1)

            def windows(phase, i, part=0, parts=1):
                for w, slot in window_list(phase, i, part, parts):
                    act.wait_ge(adj_full, w + 3)
                    nc.scalar.activation(adj[:, :, bass.ts(w, WIN)], ps[0:P, 6 + slot, 0:WK].rearrange("p (d h) -> p h d", h=T),
                                         ACT.Copy, accum_out=adj_sum[:, bass.ds(w, 1)]).then_inc(adj_freed, 1)

            def deviations(lo, hi, turn, rows_=P, scaled=False):
                act.wait_ge(var_ready, turn + 1)
                nc.scalar.activation(std[0:rows_, lo:hi], mv[0:rows_, lo:hi, 1], ACT.Sqrt,
                                     bias=eps[0:rows_, scaled:scaled + 1], scale=S_X ** -2 if scaled else 1.0
                                     ).then_inc(std_ready, 1)

            def high_t(phase, dst, scale):
                with act.Fori(0, HT) as i:
                    for c in range(2):
                        wait_full(act, "x", phase, 2 * i + c)
                        nc.scalar.activation(dst[:, 0, :, bass.ts(2 * i + c, P)],
                                             bank("x", c)[:, 0:KB * P].rearrange("p (k n) -> p k n", k=KB),
                                             ACT.Copy, scale=scale).then_inc(high["x"], 1)

            def high_nat(family, phase, dst, scale):
                with act.Fori(0, HT) as i:
                    for c in range(2):
                        wait_full(act, family, phase, 2 * i + c)
                        nc.scalar.activation(dst[:, 0, 2 * i + c, :], bank(family, c)[0:P, :], ACT.Copy, scale=scale
                                             ).then_inc(high[family], 1)
                        windows(phase, i, c, 2)

            split_weight("lin")
            for half in range(2):
                deviations(half * HT, half * HT + HT, half, scaled=True)
                act.wait_ge(norm_ready, half + 1)
                for t_ in range(half * HT, half * HT + HT):
                    nc.scalar.activation(xn_nat[:, t_, :], x[:, t_, :], ACT.Identity, bias=shift[0:P, t_:t_ + 1],
                                         scale=rstd[0:P, t_:t_ + 1]).then_inc(ln_done, 1)
            high_t("xn", xn_t, 1.0)
            split_weight("k")
            act.wait_ge(got_cols, 16)
            nc.scalar.preload_act_table(ACT.Exp)
            with act.Fori(0, J) as j:
                for m in range(KB):
                    wait_full(act, "t", "lin", KB * j + m)
                    nc.scalar.activation(gnn_t[:, m, bass.ts(j, CH)], bank("t", m), ACT.Identity, bias=col("lin_b", m),
                                         scale=S_XW).then_inc(free["t", "act"], 1)
                windows("lin", j)
            high_nat("x", "x0", gnn_nat, S_X)
            split_weight("q")
            with act.Fori(0, J) as j:
                windows("k", j)
            act.wait_ge(k_max, 1)
            for m in range(KB):
                nc.scalar.activation(k_t[:, m, :], k_t[:, m, :], ACT.Exp, bias=kneg[:, m:m + 1],
                                     accum_out=ksum[:, m:m + 1]).then_inc(k_exp, 1)
            split_weight("v")
            with act.Fori(0, HT) as i:
                for c in range(2):
                    wait_done(act, "n", "q", 2 * i + c + 1)
                    nc.scalar.activation(q_nat[:, 2 * i + c, :], q_nat[:, 2 * i + c, :], ACT.Exp, scale=S_XW).then_inc(q_exp, 1)
            high_nat("x", "kn", k_nat, S_K)
            split_weight("out")
            high_nat("n", "v", v_nat, 1 / S_W)
            split_weight("up0")
            high_t("qt", q_t, S_Q)
            split_weight("down0")
            act.wait_ge(consts, 1)
            for b in range(2):
                wait_full(act, "x", "ctx", b)
                for hh in range(2):
                    part = slice(hh * DH, hh * DH + DH)
                    last = nc.scalar.activation(ctx16[part, 0, 2 * b:2 * b + 2, part],
                                                bank("x", b)[part, 0:256].rearrange("p (q d) -> p q d", q=2)[:, :, part],
                                                ACT.Copy, scale=1 / (S_X * S_K))
                last.then_inc(high["x"], 1)
            act.wait_ge(k_max, 2)
            for p in range(KB):
                wait_full(act, "n", "m", p)
                nc.scalar.activation(mm[:, 0, p, :], bank("n", p % 2), ACT.Identity, scale=krec[:, p:p + 1]).then_inc(high["n"], 1)
            with act.Fori(0, HT) as i:
                for c in range(2):
                    windows("mix", i, c, 2)
            deviations(0, T, 2)
            act.wait_ge(norm_ready, 3)
            with act.Fori(0, T) as t_:
                nc.scalar.activation(mix_nat[:, t_, :], mix_nat[:, t_, :], ACT.Identity, bias=shift[0:P, bass.ds(t_, 1)],
                                     scale=rstd[0:P, bass.ds(t_, 1)]).then_inc(ln_done, 1)

            act.wait_ge(rare_ready, 1)
            is_rare = act.value_load(rare[0:1, 0:1], min_val=0, max_val=1)
            with act.If(is_rare):
                with act.Fori(0, NW) as w:
                    act.wait_ge(g_full, w + 1)
                    nc.scalar.activation(adj[:, :, bass.ts(w, WIN)], ps[0:P, 6, 0:WK].rearrange("p (d h) -> p h d", h=T),
                                         ACT.Copy).then_inc(g_high, 1)

            act.wait_ge(bias_ready, 1)
            nc.scalar.preload_act_table(ACT.Sqrt)

            def prelu(phase, turn, dst, bias):
                def product(i, m):
                    wait_full(act, "t", phase, i + m)
                    act.wait_ge(tmp_free, i + (turn + m + 1))
                    nc.scalar.activation(act_tmp[:, m, :], bank("t", m), ACT.Identity, bias=bias(m), scale=1 / S_W
                                         ).then_inc(free["t", "act"], 1)

                def top(j, m):
                    act.wait_ge(prelu_out, KB * j + (turn + m + 1))
                    nc.scalar.activation(dst[:, 0, m, bass.ts(j, CH)], act_tmp[:, m, :], ACT.Copy).then_inc(hid_high, 1)

                with act.Fori(0, J) as j:
                    for m in range(KB):
                        product(KB * j, m)
                        if m:
                            top(j, m - 1)
                    top(j, KB - 1)

            def hidden(phase, turn, dst, outs, scale, bias, **func):
                with act.Fori(0, J) as j:
                    for m in range(outs):
                        wait_full(act, "t", phase, outs * j + m)
                        act.wait_ge(tmp_free, turn + outs * j + m + 1 + KB - outs)
                        nc.scalar.activation(dst[:, 0, m, bass.ts(j, CH)], bank("t", m), bias=bias(m), scale=scale, **func)
                        nc.scalar.activation(act_tmp[:, m, :], bank("t", m), bias=bias(m), scale=scale, **func
                                             ).then_inc(free["t", "act"], 1)

            for layer in range(L):
                with act.Fori(0, J) as j:
                    for m in range(KB):
                        wait_full(act, "t", f"agg{layer}", KB * j + m)
                        nc.scalar.activation(h_t[:, 0, m, bass.ts(j, CH)], bank("t", m), ACT.Copy, scale=S_H / S_X
                                             ).then_inc(high["t"], 1)
                split_weight("gate" if layer else "up1")
                prelu(f"up{layer}", 20 * layer, a_t, lambda m: bias_a[:, KB * layer + m:KB * layer + m + 1])
                if layer == 0:
                    act.wait_ge(mixed, T)
                with act.Fori(0, J) as j:
                    for m in range(KB):
                        wait_full(act, "t", f"down{layer}", KB * j + m)
                        nc.scalar.activation(gnn_t[:, m, bass.ts(j, CH)], bank("t", m), ACT.Identity,
                                             bias=col("b2", KB * layer + m), scale=1 / (S_W * S_H)).then_inc(free["t", "act"], 1)
                deviations(0, KB, 3 + layer, rows_=128)
                if layer == 0:
                    split_weight("down1")
                act.wait_ge(norm_ready, 4 + layer)
                for m in range(KB):
                    nc.scalar.activation(gnn_t[:, m, :], gnn_t[:, m, :], ACT.Relu, bias=shift[:, m:m + 1],
                                         scale=rstd[:, m:m + 1]).then_inc(layer_out, 1)
                if layer == 0:
                    high_nat("x", "x1", gnn_nat, S_X)

            for half in range(2):
                deviations(half * HT, half * HT + HT, 5 + half, scaled=True)
                act.wait_ge(norm_ready, 6 + half)
                for t_ in range(half * HT, half * HT + HT):
                    nc.scalar.activation(x2_nat[:, t_, :], x[:, t_, :], ACT.Identity, bias=shift[0:P, t_:t_ + 1],
                                         scale=rstd[0:P, t_:t_ + 1]).then_inc(ln_done, 1)
            high_t("x2", x2_t, 1.0)
            with act.Fori(0, J) as j:
                for m in range(KB):
                    wait_full(act, "t", "gate", KB * j + m)
                    nc.scalar.activation(bank("t", m), bank("t", m), ACT.Relu, bias=col("gfc1_b", m), scale=S_XW,
                                         accum_out=gsum[:, m, bass.ds(j, 1)]).then_inc(free["t", "act"], 1)
            for w in range(2):
                act.wait_ge(wm_done, w + 1)
                nc.scalar.activation(wm16[:, w, 0, :], wm32[:, w, :], ACT.Copy, scale=S_W).then_inc(wm_high, 1)
            hidden("ffn1", 40, hid_t, FB, 1 / S_W, lambda m: b1m[:, m:m + 1], func=ACT.Relu)
            deviations(0, T, 7)
            act.wait_ge(norm_ready, 8)
            for t_ in range(T):
                nc.scalar.activation(x2_nat[:, t_, :], x2_nat[:, t_, :], ACT.Identity, bias=shift[0:P, t_:t_ + 1],
                                     scale=rstd[0:P, t_:t_ + 1]).then_inc(ln_done, 1)

        @block.vector
        def _(dve):
            steps = [0]

            def chain(ins, times=1):
                ins.then_inc(dve_step, 1)
                steps[0] += times
                return steps[0]

            def then(ins):
                dve.wait_ge(dve_step, chain(ins))

            def windows(phase, i, part=0, parts=1):
                for w, slot in window_list(phase, i, part, parts):
                    at = dve.value_load(window_at[0:1, bass.ds(w, 1)], min_val=0, max_val=COLS)
                    dve.wait_ge(adj_full, w + 1)
                    nc.vector.tensor_tensor(rel[:, slot], keys[:, bass.ds(at, WC)].unsqueeze(2).to_broadcast([P, WC, T]),
                                            win_key[:, bass.ds(w, 1)].unsqueeze(2).to_broadcast([P, WC, T]),
                                            ALU.subtract).then_inc(rel_ready, 1)
                    nc.vector.tensor_tensor(oh_s[:, slot], iota_s, sources[:, bass.ds(at, WC)].unsqueeze(1)
                                            .to_broadcast([P, P, WC]), ALU.is_equal)
                    dve.wait_ge(rel_ready, w + 1)
                    last = nc.vector.tensor_tensor(oh_d[:, slot], iota_d.unsqueeze(2).to_broadcast([P, WIN, WC, T]),
                                                   rel[:, slot].unsqueeze(1).to_broadcast([P, WIN, WC, T]), ALU.is_equal)
                    last.then_inc(oh_ready, 1)

            def low(out, src, hi, scale=1.0):
                if isinstance(scale, float) and scale == 1.0:
                    return nc.vector.tensor_tensor(out, src, hi, ALU.subtract)
                return nc.vector.scalar_tensor_tensor(out, src, scale, hi, ALU.mult, ALU.subtract)

            def low_t(phase, dst, scale=1.0):
                with dve.Fori(0, HT) as i:
                    for c in range(2):
                        tile = bass.ts(2 * i + c, P)
                        wait_high(dve, "x", phase, 2 * i + c)
                        if scale == 1.0:
                            ins = nc.vector.tensor_tensor(dst[:, 1, :, tile], bank("x", c)[:, 0:KB * P].rearrange(
                                "p (k n) -> p k n", k=KB), dst[:, 0, :, tile], ALU.subtract)
                        else:
                            ins = nc.vector.scalar_tensor_tensor(dst[:, 1, :, tile], bank("x", c)[:, 0:KB * P].rearrange(
                                "p (k n) -> p k n", k=KB), scale, dst[:, 0, :, tile], ALU.mult, ALU.subtract)
                        ins.then_inc(free["x", "dve"], 1)

            def low_nat(family, phase, dst, scale):
                with dve.Fori(0, HT) as i:
                    for c in range(2):
                        windows(phase, i, c, 2)
                        wait_high(dve, family, phase, 2 * i + c)
                        low(dst[:, 1, 2 * i + c, :], bank(family, c)[0:P, :], dst[:, 0, 2 * i + c, :], scale
                            ).then_inc(free[family, "dve"], 1)

            def aggregate(lo, hi):
                for t_ in range(lo, hi):
                    last = nc.vector.bn_aggr(mv[0:P, t_, :], stat[0:P, 6 * t_:6 * t_ + 6])
                last.then_inc(var_ready, 1)

            def normalizer(lo, hi, turn):
                dve.wait_ge(std_ready, turn + 1)
                then(nc.vector.reciprocal(rstd[0:P, lo:hi], std[0:P, lo:hi]))
                nc.vector.scalar_tensor_tensor(shift[0:P, lo:hi], mv[0:P, lo:hi, 0], -1.0, rstd[0:P, lo:hi], ALU.mult,
                                               ALU.mult).then_inc(norm_ready, 1)

            def layer_norm(src, lo, hi, turn):
                for t_ in range(lo, hi):
                    last = nc.vector.bn_stats(stat[0:P, 6 * t_:6 * t_ + 6], src[:, t_, :])
                then(last)
                aggregate(lo, hi)
                normalizer(lo, hi, turn)

            dve.wait_ge(got_edges, 32)
            then(nc.vector.tensor_scalar(src_tile, ints[:, 0, :], float(P), None, ALU.is_ge))
            for h in range(2, T):
                then(nc.vector.scalar_tensor_tensor(src_tile, ints[:, 0, :], float(P * h), src_tile, ALU.is_ge, ALU.add))
            dve.wait_ge(iotas, 1)
            nc.vector.scalar_tensor_tensor(keys[:, 0:COLS], ints[:, 1, :], float(T), src_tile, ALU.mult, ALU.add)
            nc.vector.scalar_tensor_tensor(sources[:, 0:COLS], src_tile, -float(P), ints[:, 0, :], ALU.mult, ALU.add)
            nc.vector.tensor_copy(iota_mem[:, 0:WK], iota_i[:, 0:WK])
            nc.vector.tensor_copy(iota_s, iota_i[:, 0:P].unsqueeze(2).to_broadcast([P, P, WC]))
            nc.vector.tensor_copy(win_key[:, :], iota_i[:, WK:])
            nc.vector.tensor_copy(heads, heads_i)
            then(nc.vector.tensor_copy(first[:, 0:1], first_i))
            then(nc.vector.tensor_scalar(heads_lt, heads, first[:, 0:1], None, ALU.is_lt, ALU.add, accum_out=first[:, 1:2]))
            nc.vector.tensor_scalar(first[:, 1:2], first[:, 1:2], -1.0, 0.0, ALU.add, ALU.max).then_inc(firsts, 1)
            dve.wait_ge(firsts_row, 1)
            nc.vector.tensor_copy(window_at[:, :], ps[0:1, 7, 0:NW]).then_inc(window_ready, 1)

            for half in range(2):
                dve.wait_ge(got_x[half], 16)
                layer_norm(x, half * HT, half * HT + HT, half)
            low_t("xn", xn_t)
            dve.wait_ge(window_ready, 1)

            def prelu(phase, base, src, neg, alpha, done):
                with dve.Fori(0, J) as j:
                    windows(phase, j)
                    for m in range(0, KB, 2):
                        for q in (m, m + 1):
                            wait_done(dve, "t", phase, KB * j + q + 1)
                            nc.vector.tensor_scalar(neg[:, q, :], src(q, j), 0.0, alpha(q), ALU.min, ALU.mult
                                                    ).then_inc(dve_step, 1)
                        for q in (m, m + 1):
                            dve.wait_ge(dve_step, KB * j + (base + q + 1))
                            nc.vector.scalar_tensor_tensor(src(q, j), src(q, j), 0.0, neg[:, q, :], ALU.max, ALU.add
                                                           ).then_inc(done, 1)
                steps[0] += KB * J

            dve.wait_ge(got_cols, 16)
            prelu("lin", steps[0], lambda m, j: gnn_t[:, m, bass.ts(j, CH)], lin_neg, lambda m: col("lin_a", m), lin_out)
            low_nat("x", "x0", gnn_nat, S_X)
            with dve.Fori(0, J) as j:
                windows("k", j)
                for m in range(KB):
                    wait_full(dve, "t", "k", KB * j + m)
                    nc.vector.tensor_scalar(k_t[:, m, bass.ts(j, CH)], bank("t", m), S_XW, None, ALU.mult, ALU.max,
                                            accum_out=kmax[:, m, bass.ds(j, 1)]).then_inc(free["t", "dve"], 1)
            wait_done(dve, "t", "k", 20)
            nc.vector.tensor_reduce(kneg[:, :], kmax[:, :, :], AX.X, ALU.max, negate=True).then_inc(k_max, 1)
            def heads_of(ap):
                return ap.rearrange("p (h d) -> p h d", h=H)

            def per_head(ap):
                return ap.unsqueeze(2).to_broadcast([P, H, DH])

            for i in range(HT):
                for t_ in (2 * i, 2 * i + 1):
                    wait_full(dve, "n", "q", t_)
                    then(nc.vector.tensor_reduce(qmax[:, t_, :], heads_of(bank("n", t_ % 2)[0:P, :]), AX.X, ALU.max))
                    nc.vector.tensor_tensor(heads_of(q_nat[:, t_, :]), heads_of(bank("n", t_ % 2)[0:P, :]),
                                            per_head(qmax[:, t_, :]), ALU.subtract).then_inc(free["n", "dve"], 1)
                for t_ in (2 * i, 2 * i + 1):
                    dve.wait_ge(q_exp, t_ + 1)
                    then(nc.vector.tensor_reduce(qsum[:, t_, :], heads_of(q_nat[:, t_, :]), AX.X, ALU.add))
                    nc.vector.reciprocal(qsum[:, t_, :], qsum[:, t_, :]).then_inc(q_rec, 1)
            low_nat("x", "kn", k_nat, S_K)
            low_nat("n", "v", v_nat, 1 / S_W)
            low_t("qt", q_t, S_Q)
            dve.wait_ge(k_exp, KB)
            nc.vector.reciprocal(krec[:, :], ksum[:, :]).then_inc(k_max, 1)
            dve.wait_ge(k_max, 2)
            for b in range(2):
                wait_high(dve, "x", "ctx", b)
                for hh in range(2):
                    part = slice(hh * DH, hh * DH + DH)
                    last = low(ctx16[part, 1, 2 * b:2 * b + 2, part],
                               bank("x", b)[part, 0:256].rearrange("p (q d) -> p q d", q=2)[:, :, part],
                               ctx16[part, 0, 2 * b:2 * b + 2, part], 1 / (S_X * S_K))
                last.then_inc(free["x", "dve"], 1)
            for p in range(KB):
                wait_high(dve, "n", "m", p)
                low(mm[:, 1, p, :], bank("n", p % 2), mm[:, 0, p, :], krec[:, p:p + 1]).then_inc(free["n", "dve"], 1)
            dve.wait_ge(got_rows, 16)
            with dve.Fori(0, HT) as i:
                for c in range(2):
                    windows("mix", i, c, 2)
                    wait_full(dve, "n", "mix", 2 * i + c)
                    nc.vector.scalar_tensor_tensor(mix_nat[:, 2 * i + c, :], bank("n", c)[0:P, :],
                                                   1 / (S_Q * S_M * DH ** 0.5 * N), rows[:, 0, :], ALU.mult, ALU.add
                                                   ).then_inc(free["n", "dve"], 1)
            wait_done(dve, "n", "mix", T)
            layer_norm(mix_nat, 0, T, 2)

            dve.wait_ge(adj_freed, 2 + NW)
            nc.vector.tensor_reduce(chk[:, 0:1], adj_sum[:, :], AX.X, ALU.add)
            nc.vector.tensor_scalar(stat[0:P, 64:64 + NW], adj_sum[:, :], F16_EXACT, None, ALU.is_ge, ALU.add,
                                    accum_out=chk[:, 1:2]).then_inc(chk_ready, 1)
            dve.wait_ge(chk_sum, 1)
            then(nc.vector.tensor_copy(chk[0:1, 2:4], ps[0:1, 6, 0:2]))
            then(nc.vector.scalar_tensor_tensor(chk[0:1, 2:3], chk[0:1, 2:3], float(EDGES), chk[0:1, 3:4], ALU.not_equal, ALU.add))
            nc.vector.tensor_scalar(rare[:, 0:1], chk[0:1, 2:3], 0.0, None, ALU.is_gt).then_inc(rare_ready, 1)
            dve.wait_ge(rare_ready, 1)
            is_rare = dve.value_load(rare[0:1, 0:1], min_val=0, max_val=1)
            with dve.If(is_rare):
                nc.vector.memset(oh_s[:, 1, :, 0], 0.0).then_inc(g_oh, 1)
                nc.vector.memset(oh_d[:, 0, :, 7, :], 0.0).then_inc(g_low, 1)
                with dve.Fori(0, NW) as w:
                    with dve.Fori(0, COLS // 2) as c:
                        dve.wait_ge(g_used, w * (COLS // 2) + c + 1)
                        for b in range(2):
                            e = 2 * c + b
                            nc.vector.tensor_scalar(oh_d[:, 0, :, b, :], iota_d, win_key[:, bass.ds(w, 1)],
                                                    keys[:, bass.ds(e, 1)], ALU.add, ALU.is_equal)
                            last = nc.vector.tensor_tensor(oh_s[:, 0, :, b], iota_s[:, :, 0], sources[:, bass.ds(e, 1)]
                                                           .to_broadcast([P, P]), ALU.is_equal)
                        last.then_inc(g_oh, 1)
                    dve.wait_ge(g_high, w + 1)
                    counts = ps[0:P, 6, 0:WK].rearrange("p (d h) -> p h d", h=T)
                    part = bass.ts(w, WIN)
                    nc.vector.tensor_tensor(lo_a[:, :, part], counts[:, 0:LO_TILES, :], adj[:, 0:LO_TILES, part], ALU.subtract)
                    nc.vector.tensor_tensor(lo_b[:, :, part], counts[:, LO_TILES:T, :], adj[:, LO_TILES:T, part], ALU.subtract
                                            ).then_inc(g_low, 1)
                dve.wait_ge(g_low, NW + 1)
                for h in range(T):
                    low_ = lo_a[:, h] if h < LO_TILES else lo_b[:, h - LO_TILES]
                    last = nc.vector.tensor_tensor(low_[:, h * P:(h + 1) * P], low_[:, h * P:(h + 1) * P], ident[0:P, 0:P], ALU.add)
                last.then_inc(adj_ready, 1)
            with dve.Else():
                for h in range(T):
                    diagonal = adj[:, h, h * P:(h + 1) * P]
                    last = nc.vector.tensor_tensor(diagonal, diagonal, ident[0:P, 0:P], ALU.add)
                last.then_inc(adj_ready, 1)

            nc.vector.tensor_scalar(bias_a[:, :], col("b1", 0, 2 * KB), S_H, None, ALU.mult).then_inc(bias_ready, 1)

            def low_hidden(phase, dst, outs):
                with dve.Fori(0, J) as j:
                    for m in range(outs):
                        chunk = bass.ts(j, CH)
                        wait_done(dve, "t", phase, outs * j + m + 1)
                        nc.vector.tensor_tensor(dst[:, 1, m, chunk], act_tmp[:, m, :], dst[:, 0, m, chunk], ALU.subtract
                                                ).then_inc(tmp_free, 1)

            for layer in range(L):
                with dve.Fori(0, J) as j:
                    for m in range(KB):
                        chunk = bass.ts(j, CH)
                        wait_high(dve, "t", f"agg{layer}", KB * j + m)
                        low(h_t[:, 1, m, chunk], bank("t", m), h_t[:, 0, m, chunk], S_H / S_X).then_inc(free["t", "dve"], 1)
                prelu(f"up{layer}", steps[0], lambda m, j: act_tmp[:, m, :], negative, lambda m: col("conv_a", layer), prelu_out)
                with dve.Fori(0, J) as j:
                    for m in range(KB):
                        wait_done(dve, "t", f"down{layer}", KB * j + m + 1)
                        ins = nc.vector.bn_stats(stat[:, :].rearrange("p (m j s) -> p m (j s)", m=KB, j=J)[:, m, bass.ts(j, 6)],
                                                 gnn_t[:, m, bass.ts(j, CH)])
                    ins.then_inc(dve_step, 1)
                steps[0] += J
                dve.wait_ge(dve_step, steps[0])
                for m in range(KB):
                    last = nc.vector.bn_aggr(mv[:, m, :], stat[:, 6 * J * m:6 * J * (m + 1)])
                last.then_inc(var_ready, 1)
                dve.wait_ge(std_ready, 4 + layer)
                then(nc.vector.reciprocal(rstd[:, 0:KB], std[:, 0:KB]))
                then(nc.vector.tensor_tensor(rstd[:, 0:KB], rstd[:, 0:KB], col("gamma", KB * layer, KB), ALU.mult))
                then(nc.vector.tensor_tensor(shift[:, 0:KB], mv[:, 0:KB, 0], rstd[:, 0:KB], ALU.mult))
                nc.vector.tensor_tensor(shift[:, 0:KB], col("beta", KB * layer, KB), shift[:, 0:KB], ALU.subtract
                                        ).then_inc(norm_ready, 1)
                if layer == 0:
                    low_nat("x", "x1", gnn_nat, S_X)

            dve.wait_ge(mixed, T)
            with dve.Fori(0, HT) as i:
                for c in range(2):
                    wait_full(dve, "x", "gnn", 2 * i + c)
                    nc.vector.tensor_tensor(x[:, 2 * i + c, :], bank("x", c)[0:P, :], x[:, 2 * i + c, :], ALU.add
                                            ).then_inc(free["x", "dve"], 1)
            for half in range(2):
                wait_done(dve, "x", "gnn", half * HT + HT)
                layer_norm(x, half * HT, half * HT + HT, 5 + half)
            low_t("x2", x2_t)
            dve.wait_ge(got_ln, 32)
            then(nc.vector.tensor_scalar(rows[:, 0:2, :], rows[:, 0:2, :], 1 - LN_MERGE * E, None, ALU.mult))
            for r in range(2):
                wait_full(dve, "x", "rows", r)
                nc.vector.scalar_tensor_tensor(rows[:, r, :], bank("x", r)[0:P, :], LN_MERGE, rows[:, r, :], ALU.mult, ALU.add
                                               ).then_inc(free["x", "dve"], 1)
            wait_done(dve, "t", "gate", 20)
            then(nc.vector.tensor_reduce(gmean[:, :], gsum[:, :, :], AX.X, ALU.add))
            nc.vector.tensor_scalar(gbc[:, :, :], gmean[:, :].unsqueeze(2).to_broadcast([128, KB, 128]), 1 / N, None, ALU.mult
                                    ).then_inc(g_bc, 1)
            wait_full(dve, "x", "g", 0)
            nc.vector.tensor_tensor(gcol[:, :], bank("x", 0)[:, 0:E], col("gfc2_b", 0, E), ALU.add).then_inc(free["x", "dve"], 1)
            wait_full(dve, "x", "g", 1)
            nc.vector.tensor_scalar(grow[:, :], bank("x", 1)[0:E, 0:P], cols[0:E, COL["gfc2_bc"][0]:COL["gfc2_bc"][0] + 1], None,
                                    ALU.add).then_inc(g_vec, 1)
            wait_done(dve, "x", "g", 1)
            dve.wait_ge(got_wm, 16)
            dve.wait_ge(got_tv, 32)
            for w in range(2):
                for e in range(E):
                    ins = nc.vector.scalar_tensor_tensor(wm32[:, w, :], tv[:, w, e, :], gcol[:, e:e + 1], wm32[:, w, :],
                                                         ALU.mult, ALU.add)
                    if e < E - 1:
                        then(ins)
                ins.then_inc(wm_done, 1)
                if w == 0:
                    scratch = stat[:, 0:FB * E].rearrange("p (f e) -> p f e", f=FB)
                    then(nc.vector.tensor_tensor(scratch, col("tv_b1", 0, FB * E).rearrange("p (f e) -> p f e", f=FB),
                                                 gcol[:, :].unsqueeze(1).to_broadcast([128, FB, E]), ALU.mult))
                    then(nc.vector.tensor_reduce(b1m[:, :], scratch, AX.X, ALU.add))
                    then(nc.vector.tensor_tensor(b1m[:, :], b1m[:, :], col("ffn_b1", 0, FB), ALU.add))
                    then(nc.vector.tensor_scalar(b1m[:, :], b1m[:, :], S_X, None, ALU.mult))
                dve.wait_ge(wm_high, w + 1)
                low(wm16[:, w, 1, :], wm32[:, w, :], wm16[:, w, 0, :], S_W).then_inc(wm_split, 1)
            dve.wait_ge(b2_sum, 1)
            then(nc.vector.tensor_tensor(b2_row, ps[0:P, 7, :], b2_row, ALU.add))
            low_hidden("ffn1", hid_t, FB)
            with dve.Fori(0, T) as t_:
                nc.vector.scalar_tensor_tensor(x2_nat[:, t_, :], x2_nat[:, t_, :], 1 / S_X, b2_row, ALU.mult, ALU.add
                                               ).then_inc(dve_step, 1)
            steps[0] += T
            dve.wait_ge(dve_step, steps[0])
            with dve.Fori(0, HT) as i:
                for c in range(2):
                    wait_full(dve, "n", "ffn2", 2 * i + c)
                    nc.vector.scalar_tensor_tensor(x2_nat[:, 2 * i + c, :], bank("n", c)[0:P, :], S_XW, x2_nat[:, 2 * i + c, :],
                                                   ALU.mult, ALU.add).then_inc(free["n", "dve"], 1)
            wait_done(dve, "n", "ffn2", T)
            layer_norm(x2_nat, 0, T, 7)
            dve.wait_ge(xb_ready, T)
            for t_ in range(T):
                dve.wait_ge(ln_done, 3 * T + t_ + 1)
                then(nc.vector.tensor_tensor(x2_nat[:, t_, :], x2_nat[:, t_, :], rows[:, 0, :], ALU.mult))
                nc.vector.tensor_tensor(x2_nat[:, t_, :], x2_nat[:, t_, :], x[:, t_, :], ALU.add).then_inc(out_ready, 1)

        @block.gpsimd
        def _(pool):
            steps = [0]

            def then(ins):
                ins.then_inc(pool_step, 1)
                steps[0] += 1
                pool.wait_ge(pool_step, steps[0])

            pool.dma_start(x[:, 0:HT, :], dram["x"][:, 0:HT, :]).then_inc(got_x[0], 16)
            nc.gpsimd.memset(keys[:, COLS:KEYS], -1.0)
            nc.gpsimd.memset(sources[:, COLS:KEYS], 0.0)
            nc.gpsimd.iota(iota_i[:, 0:WK], pattern=[[1, WK]], base=0, channel_multiplier=0)
            nc.gpsimd.iota(iota_i[:, WK:], pattern=[[WK, NW]], base=0, channel_multiplier=0)
            nc.gpsimd.iota(first_i, pattern=[[0, 1]], base=0, channel_multiplier=WIN).then_inc(iotas, 1)
            nc.gpsimd.memset(eps[:, 0:1], LN_EPS)
            nc.gpsimd.memset(eps[:, 1:2], LN_EPS / (S_X * S_X))
            nc.gpsimd.memset(ones[:, :], 1.0)
            nc.gpsimd.memset(ctx16[:, :, :, :], 0.0)
            then(nc.gpsimd.memset(ident[:, :], 0.0))
            nc.gpsimd.affine_select(out=ident[:, :], in_=ident[:, :], compare_op=ALU.not_equal, fill=1.0, base=0,
                                    pattern=[[-1, 128]], channel_multiplier=1).then_inc(consts, 1)

            def split_weight(name):
                i = WEIGHTS.index(name)
                pool.wait_ge(got_w, 16 * (i + 1))
                nc.gpsimd.tensor_scalar(stage[:, :], stage[:, :], S_W, 1.0, ALU.mult, ALU.mult).then_inc(w_scaled, 1)
                pool.wait_ge(w_high, i + 1)
                nc.gpsimd.tensor_tensor(wslot[:, i % SLOTS, 1].rearrange("p k n -> p (k n)"), stage[:, :],
                                        wslot[:, i % SLOTS, 0].rearrange("p k n -> p (k n)"), ALU.subtract).then_inc(w_split, 1)

            for name in ("lin", "k", "q", "v"):
                split_weight(name)
            with pool.Fori(0, T) as t_:
                pool.wait_ge(q_rec, t_ + 1)
                tile = q_nat[:, bass.ds(t_, 1), :].rearrange("p o (h d) -> p (o h) d", h=H)
                nc.gpsimd.tensor_tensor(tile, tile, qsum[:, bass.ds(t_, 1), :].rearrange("p o h -> p (o h)").unsqueeze(2)
                                        .to_broadcast([P, H, DH]), ALU.mult).then_inc(q_soft, 1)
            for name in ("out", "up0", "down0"):
                split_weight(name)
            base = steps[0]
            with pool.Fori(0, T) as t_:
                pool.wait_ge(ln_done, T + t_ + 1)
                tile = mix_nat[:, t_, :]
                nc.gpsimd.tensor_tensor(tile, tile, rows[:, 1, :], ALU.mult).then_inc(pool_step, 1)
                pool.wait_ge(pool_step, t_ + (base + 1))
                nc.gpsimd.tensor_tensor(x[:, t_, :], x[:, t_, :], tile, ALU.add).then_inc(mixed, 1)

            def low_prelu(layer):
                with pool.Fori(0, J) as j:
                    for m in range(KB):
                        pool.wait_ge(hid_high, KB * j + (KB * J * layer + m + 1))
                        nc.gpsimd.tensor_tensor(a_t[:, 1, m, bass.ts(j, CH)], act_tmp[:, m, :], a_t[:, 0, m, bass.ts(j, CH)],
                                                ALU.subtract).then_inc(tmp_free, 1)

            split_weight("up1")
            low_prelu(0)
            split_weight("down1")
            split_weight("gate")
            low_prelu(1)
            pool.wait_ge(ln_done, 3 * T)
            wait_done(pool, "x", "rows", 2)
            with pool.Fori(0, T) as t_:
                nc.gpsimd.tensor_tensor(x[:, t_, :], x[:, t_, :], rows[:, 1, :], ALU.add).then_inc(xb_ready, 1)


def kernel(**inputs):
    import numpy as np
    import concourse.bacc as bacc
    from concourse.bass_utils import run_bass_kernel_spmd

    def arr(name):
        return np.asarray(inputs[name])

    def blocks(w):
        return np.ascontiguousarray(w.reshape(-1, 128, w.shape[-1]).transpose(1, 0, 2).reshape(128, -1))

    def columns(v):
        return v.reshape(-1, 128).T

    def spread(v, n):
        return np.broadcast_to(v, (n,) + v.shape)

    g, m, f = "L0_gnn_", "L0_mix_", "L0_ffn_"
    qkv = arr(m + "w_qkv")
    src, dst = (arr(n).reshape(COLS, P) for n in ("src", "dst"))
    gfc2_b = arr(f + "gfc2_b")
    gfc2_col = np.zeros((128, 1), gfc2_b.dtype)
    gfc2_col[:E, 0] = gfc2_b
    weights = {
        "lin": arr(g + "lin_W").T, "q": qkv[:, 0:D], "k": qkv[:, D:2 * D], "v": qkv[:, 2 * D:], "out": arr(m + "w_out"),
        "up0": arr(g + "conv_W1")[0].T, "up1": arr(g + "conv_W1")[1].T, "down0": arr(g + "conv_W2")[0].T,
        "down1": arr(g + "conv_W2")[1].T, "gate": arr(f + "gfc1_w").T,
    }
    arrays = {"w_" + n: blocks(w) for n, w in weights.items()}
    arrays["x"] = np.ascontiguousarray(arr("x").reshape(T, P, D).transpose(1, 0, 2))
    arrays["edges"] = np.ascontiguousarray(np.stack([src.T, dst.T], 1))
    arrays["heads"] = np.ascontiguousarray(spread(dst[:, 0], NW))
    arrays["cols"] = np.ascontiguousarray(np.concatenate([
        columns(arr(g + "lin_b")), columns(arr(g + "lin_a")), columns(arr(g + "conv_b1")), columns(arr(g + "conv_b2")),
        columns(arr(g + "bn_gamma")), columns(arr(g + "bn_beta")), spread(arr(g + "conv_a"), 128),
        columns(arr(f + "gfc1_b")), columns(arr(f + "b1")),
        arr(f + "tv_b1").reshape(E, FB, 128).transpose(2, 1, 0).reshape(128, FB * E), spread(gfc2_b, 128), gfc2_col], 1))
    arrays["mix_rows"] = np.ascontiguousarray(spread(np.stack([arr(m + "b_out"), arr(m + "ln_scale")]), P))
    arrays["ln_rows"] = np.ascontiguousarray(spread(np.stack([arr(f + "ln_g"), arr(f + "ln_b"), arr(f + "b2")]), P))
    arrays["tv_rows"] = np.ascontiguousarray(np.stack([arr(f + "tv_ln_g"), arr(f + "tv_ln_b"), arr(f + "tv_b2")], 1))
    arrays["gfc2"] = blocks(arr(f + "gfc2_w").T).reshape(128, KB, E)
    arrays["w_ffn"] = np.concatenate([blocks(arr(f + "W1").T), blocks(arr(f + "W2").T)], 1)
    arrays["tv"] = np.ascontiguousarray(np.stack(
        [np.stack([blocks(w.T) for w in arr(f + n)], 1) for n in ("tv_W1", "tv_W2")], 1))

    nc = bacc.Bacc("TRN2", target_bir_lowering=False, num_devices=1)
    dram = {n: nc.dram_tensor("in_" + n, a.shape, mybir.dt.from_np(a.dtype), kind="ExternalInput").ap()
            for n, a in arrays.items()}
    dram["out"] = nc.dram_tensor("out_0", (P, T, D), F32, kind="ExternalOutput").ap()
    gps_block(nc, dram)
    result = run_bass_kernel_spmd(nc, [{"in_" + n: a for n, a in arrays.items()}], core_ids=[0])
    return np.ascontiguousarray(result.results[0]["out_0"].transpose(1, 0, 2)).reshape(N, D)
```

```python
from contextlib import ExitStack

import concourse.bass as bass
from concourse import mybir

F32 = mybir.dt.float32
F16 = mybir.dt.float16
I32 = mybir.dt.int32
ALU = mybir.AluOpType
ACT = mybir.ActivationFunctionType
AX = mybir.AxisListType

N, D, H, F, E, L, EDGES = 1250, 512, 8, 256, 8, 2, 41250
DH = D // H
P = 125
T = N // P
KB = D // 128
FB = F // 128
CH = 2 * P
J = N // CH
COLS = EDGES // P
WIN = 25
NW = N // WIN
WC = 9
KEYS = COLS + WC
WK = T * WIN
OHS = 2 * (WC * (P + WK) + 1)
HT = T // 2
LN_EPS, BN_EPS, LN_MERGE = 1e-5, 1e-5, 0.03
F16_EXACT = 2048.0
LO_TILES = 8

TURN = {"xn": 0, "mix": HT, "bn": HT + 1, "x2": HT + 1 + L, "out": 2 * HT + 1 + L}

S_X, S_W, S_H, S_K, S_Q, S_M = 16.0, 256.0, 1 / 16, 256.0, 1024.0, 256.0
S_XW = 1 / (S_X * S_W)

COL = {}
for _name, _n in (("lin_b", 4), ("lin_a", 4), ("b1", 8), ("b2", 8), ("gamma", 8), ("beta", 8), ("conv_a", 2),
                  ("gfc1_b", 4), ("ffn_b1", 2), ("tv_b1", 16), ("gfc2_b", 8), ("gfc2_bc", 1)):
    COL[_name] = (sum(n for _, n in COL.values()), _n)
NCOL = sum(n for _, n in COL.values())

WEIGHTS = ["lin", "k", "q", "v", "out", "up0", "down0", "up1", "down1", "gate"]
SLOTS = 3
WINDOWS = {"k": 4, "v": 4, "mix": 2}

USES = {
    "n": [("q", T, "dve", 0), ("v", T, "dve", 1), ("m", KB, "dve", 1), ("mix", T, "dve", 0), ("ffn2", T, "dve", 0)],
    "t": [("lin", 20, "act", 0), ("k", 20, "dve", 0), ("agg0", 20, "dve", 1), ("up0", 20, "act", 0),
          ("down0", 20, "act", 0), ("agg1", 20, "dve", 1), ("up1", 20, "act", 0), ("down1", 20, "act", 0),
          ("gate", 20, "act", 0), ("ffn1", 10, "act", 0)],
    "x": [("xn", T, "dve", 1), ("x0", T, "dve", 1), ("kn", T, "dve", 1),
          ("ctx", 2, "dve", 1), ("qt", T, "dve", 1), ("x1", T, "dve", 1), ("x2", T, "dve", 1),
          ("rows", 2, "dve", 0), ("g", 2, "dve", 0)],
    "y": [("gnn", T, "dve", 0)],
}
RING = {"n": 2, "t": 4, "x": 2, "y": 2}
BANKS_FROM = {"q": ("t", "k", 17), "agg0": ("n", "mix", 9), "ffn2": ("t", "ffn1", 9)}


def before(family, phase, who=None, high=False):
    total = 0
    for name, uses, by, hi in USES[family]:
        if name == phase:
            return total
        if (who is None or by == who) and (hi or not high):
            total += uses
    raise KeyError(phase)


def entry(family, phase):
    return next(u for u in USES[family] if u[0] == phase)


def first_window(phase):
    at = 0
    for name, per in WINDOWS.items():
        if name == phase:
            return at
        at += per * J
    raise KeyError(phase)


DONE_EARLY = first_window("mix") * WIN // P


def window_list(phase, i, part=0, parts=1):
    n = WINDOWS.get(phase, 0) // parts
    return [((n * parts) * i + (first_window(phase) + n * part + c), (n * part + c) % 2) for c in range(n)]


assert sum(WINDOWS.values()) * J == NW and J == HT

READER = {"lin": ("t", "lin"), "k": ("t", "k"), "q": ("n", "q"), "v": ("n", "v"), "out": ("n", "m"), "up0": ("t", "up0"),
          "down0": ("t", "down0"), "up1": ("t", "up1"), "down1": ("t", "down1"), "gate": ("t", "gate")}


def gps_block(nc, dram):
    with ExitStack() as ctx:
        def sb(name, shape, dt=F32):
            return ctx.enter_context(nc.sbuf_tensor(name, shape, dt))

        def sem(name):
            return ctx.enter_context(nc.semaphore(name))

        ps = ctx.enter_context(nc.psum_tensor("ps", [128, 8, 512], F32))

        def bank(family, slot):
            if family == "t":
                return ps[:, slot, 0:CH]
            return ps[:, {"n": 0, "x": 4, "y": 6}[family] + slot, :]

        x = sb("x", [P, T, D])
        r1 = sb("r1", [128, T * D])
        r2 = sb("r2", [128, T * D])
        r3 = sb("r3", [128, T * D])
        late = sb("late", [128, 2 * T * D + N * T // 2])
        r4, r5 = late[:, 0:T * D], late[:, T * D:2 * T * D]
        adj = late[0:P, 2 * T * D:].bitcast(F16).rearrange("p (h d) -> p h d", h=T)

        def nat32(r):
            return r[0:P].rearrange("p (t c) -> p t c", t=T)

        def nat16(r):
            return r[0:P].bitcast(F16).rearrange("p (h t c) -> p h t c", h=2, t=T)

        def tr32(r):
            return r[:, 0:KB * N].rearrange("p (k n) -> p k n", k=KB)

        def tr16(r, blocks=KB):
            return r[:, 0:blocks * N].bitcast(F16).rearrange("p (h k n) -> p h k n", h=2, k=blocks)

        xn_nat, xn_t = nat32(r5), tr16(r1)
        gnn_t, gnn_nat = tr32(r3), nat16(r2)
        k_t, k_nat = tr32(r4), nat16(r5)
        q_nat, q_t = nat32(r3), tr16(r1)
        v_nat = nat16(r4)
        mm = r5[:, 0:KB * D].bitcast(F16).rearrange("p (h k n) -> p h k n", h=2, k=KB)
        mix_nat = nat32(r3)
        h_t, a_t = tr16(r4), tr16(r5)
        x2_nat, x2_t = nat32(r2), tr16(r1)
        hid_t = tr16(r3, FB)
        tv = late[:, 0:2 * E * KB * F].rearrange("p (w e n) -> p w e n", w=2, e=E)

        stage = sb("stage", [128, KB * D])
        wm32 = stage[:, :].rearrange("p (w n) -> p w n", w=2)
        wslot = sb("wslot", [128, SLOTS, 2, KB, D], F16)
        wm16 = wslot[:, 2].rearrange("p h k n -> p (h k n)").rearrange("p (w h n) -> p w h n", w=2, h=2)
        w1m = wm16[:, 0].rearrange("p h (k f) -> p h k f", k=KB)
        w2m = wm16[:, 1].rearrange("p h (k c) -> p h k c", k=FB)
        assert WEIGHTS.index("gate") % SLOTS == 0

        ohs = sb("ohs", [128, OHS], F16)
        oh_s = ohs[0:P, 0:2 * (WC * P + 1)].rearrange("p (b n) -> p b n", b=2)[:, :, 0:WC * P].rearrange(
            "p b (s w) -> p b s w", w=WC)
        oh_d = ohs[0:P, 2 * (WC * P + 1):].rearrange("p (b d w h) -> p b d w h", b=2, w=WC, h=T)
        act_tmp = ohs[:, 0:2 * KB * CH].bitcast(F32).rearrange("p (m n) -> p m n", m=KB)
        negative = ohs[:, 2 * KB * CH:4 * KB * CH].bitcast(F32).rearrange("p (m n) -> p m n", m=KB)
        tvrow = ohs[0:E, 2 * KB * CH:2 * KB * CH + 6 * D].bitcast(F32).rearrange("e (r c) -> e r c", r=3)
        general = ohs[0:P, 0:3 * (P + WK)].rearrange("p (b n) -> p b n", b=3)
        lo_a = r1[0:P, 0:LO_TILES * N // 2].bitcast(F16).rearrange("p (h d) -> p h d", h=LO_TILES)
        lo_b = ohs[0:P, OHS - (T - LO_TILES) * N:].rearrange("p (h d) -> p h d", h=T - LO_TILES)

        ident = sb("ident", [128, 128])
        cols = sb("cols", [128, NCOL])
        rows = sb("rows", [P, 2, D])
        keys = sb("keys", [P, KEYS])
        sources = sb("sources", [P, KEYS], F16)
        iota_mem = sb("iota", [P, WK + P * WC + 1], F16)
        iota_d = iota_mem[:, 0:WK].rearrange("p (d h) -> p d h", h=T)
        iota_s = iota_mem[:, WK:WK + P * WC].rearrange("p (s w) -> p s w", w=WC)
        b2_row = iota_mem[:, 0:2 * D].bitcast(F32)
        win_key = sb("win_key", [P, NW])
        rel = sb("rel", [P, 2, WC, T], F16)
        window_at = sb("window_at", [1, NW], I32)
        adj_sum = sb("adj_sum", [P, NW])
        chk = sb("chk", [P, 4])
        ones = sb("ones", [128, 128])
        rare = sb("rare", [1, 2], I32)
        stat = sb("stat", [128, KB * J * 6])
        mv = sb("mv", [128, T, 2])
        std = sb("std", [128, T])
        eps = sb("eps", [128, 2])
        rstd = sb("rstd", [128, T])
        shift = sb("shift", [128, T])
        bn_scale, bn_shift = sb("bn_scale", [128, KB]), sb("bn_shift", [128, KB])
        kmax = sb("kmax", [128, KB, J])
        kneg = sb("kneg", [128, KB])
        ksum = sb("ksum", [128, KB])
        krec = sb("krec", [128, KB])
        qmax = sb("qmax", [P, T, H])
        qsum = sb("qsum", [P, T, H])
        ctx16 = sb("ctx16", [128, 2, KB, 128], F16)
        bias_a = sb("bias_a", [128, 2 * KB])
        gsum = sb("gsum", [128, KB, J])
        gmean = sb("gmean", [128, KB])
        gbc = ctx16[:, :, :, :].rearrange("p h k n -> p (h k n)").bitcast(F32).rearrange("p (k n) -> p k n", k=KB)
        gcol = sb("gcol", [128, E])
        grow = sb("grow", [E, P])
        b1m = sb("b1m", [128, FB])
        gfc2 = sb("gfc2", [128, KB, E])

        ints = r2[0:P, 0:2 * COLS].bitcast(I32).rearrange("p (a c) -> p a c", a=2)
        heads_i = r2[0:NW, 700:700 + COLS].bitcast(I32)
        heads = r2[0:NW, 1100:1100 + COLS]
        heads_lt = r2[0:NW, 1500:1500 + COLS]
        iota_i = r2[0:P, 1900:1900 + WK + NW].bitcast(I32)
        src_tile = r2[0:P, 2400:2400 + COLS]
        first = r2[0:NW, 2800:2802]
        lin_neg = r2[:, 3000:3000 + KB * CH].rearrange("p (m n) -> p m n", m=KB)
        first_i = r2[0:NW, 2802:2803].bitcast(I32)

        def col(name, i=0, n=1):
            return cols[:, COL[name][0] + i:COL[name][0] + i + n]

        got_edges, got_cols, got_rows, got_w = sem("got_edges"), sem("got_cols"), sem("got_rows"), sem("got_w")
        got_x = [sem(f"got_x{i}") for i in range(HT)]
        got_tvrow, got_wm, got_tv, got_ln = sem("got_tvrow"), sem("got_wm"), sem("got_tv"), sem("got_ln")
        stored = sem("stored")
        full = {f: sem(f"{f}_full") for f in USES}
        high = {f: sem(f"{f}_high") for f in USES}
        free = {(f, e): sem(f"{f}_free_{e}") for f in USES for e in ("act", "dve")}
        w_scaled, w_high, w_split = sem("w_scaled"), sem("w_high"), sem("w_split")
        consts, iotas = sem("consts"), sem("iotas")
        dve_step, act_step, pool_step = sem("dve_step"), sem("act_step"), sem("pool_step")
        firsts, firsts_row, window_ready = sem("firsts"), sem("firsts_row"), sem("window_ready")
        rel_ready, oh_ready, adj_full, adj_freed = sem("rel_ready"), sem("oh_ready"), sem("adj_full"), sem("adj_freed")
        chk_ready, chk_sum, rare_ready = sem("chk_ready"), sem("chk_sum"), sem("rare_ready")
        g_oh, g_used, g_full, g_high, g_low = sem("g_oh"), sem("g_used"), sem("g_full"), sem("g_high"), sem("g_low")
        adj_ready = sem("adj_ready")
        var_ready, std_ready, norm_ready, ln_done = sem("var_ready"), sem("std_ready"), sem("norm_ready"), sem("ln_done")
        k_max, k_exp, q_sub, q_exp, q_rec, q_soft = (sem(n) for n in ("k_max", "k_exp", "q_sub", "q_exp", "q_rec", "q_soft"))
        mix_scaled, mixed = sem("mix_scaled"), sem("mixed")
        z_ready, z_norm, layer_out = sem("z_ready"), sem("z_norm"), sem("layer_out")
        g_acc, g_bc, g_mm, g_vec, b2_ready = sem("g_acc"), sem("g_bc"), sem("g_mm"), sem("g_vec"), sem("b2_ready")
        wm_done, wm_high, wm_split, x2b_ready, xb_ready = (sem(n) for n in ("wm_done", "wm_high", "wm_split", "x2b_ready", "xb_ready"))
        gnn_added, res_ready, out_ready = sem("gnn_added"), sem("res_ready"), sem("out_ready")
        x2_done, b2_sum = sem("x2_done"), sem("b2_sum")
        scaled, merged, b1_done = sem("scaled"), sem("merged"), sem("b1_done")
        lin_out, prelu_out, hid_high = sem("lin_out"), sem("prelu_out"), sem("hid_high")
        tmp_free, bias_ready = sem("tmp_free"), sem("bias_ready")

        def wait_full(eng, family, phase, i):
            eng.wait_ge(full[family], before(family, phase) + i + 1)

        def wait_high(eng, family, phase, i):
            eng.wait_ge(high[family], before(family, phase, high=True) + i + 1)

        def wait_done(eng, family, phase, n):
            who = entry(family, phase)[2]
            eng.wait_ge(free[family, who], RING[family] + before(family, phase, who) + n)

        def wait_bank(pe, family, phase, i, slot):
            names = [u[0] for u in USES[family]]
            _, _, who, _ = entry(family, phase)
            pe.wait_ge(free[family, who], before(family, phase, who) + i + 1)
            if names.index(phase):
                last, uses, by, _ = USES[family][names.index(phase) - 1]
                if by != who:
                    pe.wait_ge(free[family, by], before(family, last, by) + uses + slot + 1)
            if phase in BANKS_FROM and slot < 2:
                family, last, uses = BANKS_FROM[phase]
                wait_done(pe, family, last, uses + slot)

        def weight(name):
            return wslot[:, WEIGHTS.index(name) % SLOTS]

        def wait_weight(pe, name):
            pe.wait_ge(w_split, WEIGHTS.index(name) + 1)

        block = ctx.enter_context(nc.Block())

        @block.sync
        def _(sp):
            for pair in (0, 2):
                sp.dma_start(x[:, 2 * pair:2 * pair + 2, :], dram["x"][:, 2 * pair:2 * pair + 2, :]).then_inc(got_x[pair], 16)
            sp.dma_start(stage[:, :], dram["w_lin"]).then_inc(got_w, 16)
            sp.dma_start(x[:, 8:10, :], dram["x"][:, 8:10, :]).then_inc(got_x[4], 16)
            sp.dma_start(ints, dram["edges"]).then_inc(got_edges, 16)
            sp.dma_start(heads_i, dram["heads"]).then_inc(got_edges, 16)
            sp.dma_start(cols[:, :], dram["cols"]).then_inc(got_cols, 16)
            sp.dma_start(rows[:, 0:2, :], dram["mix_rows"]).then_inc(got_rows, 16)
            sp.dma_start(gfc2[:, :, :], dram["gfc2"]).then_inc(got_tvrow, 16)
            for i, name in enumerate(WEIGHTS[1:], 1):
                sp.wait_ge(w_split, i)
                sp.dma_start(stage[:, :], dram["w_" + name]).then_inc(got_w, 16)
            sp.wait_ge(mixed, T)
            sp.dma_start(rows[:, :, :], dram["ln_rows"][:, 0:2]).then_inc(got_ln, 16)
            sp.wait_ge(adj_ready, 1)
            sp.dma_start(b2_row, dram["ln_rows"][:, 2]).then_inc(got_ln, 16)
            sp.wait_ge(w_split, len(WEIGHTS))
            sp.dma_start(stage[:, :], dram["w_ffn"]).then_inc(got_wm, 16)
            sp.wait_ge(full["t"], before("t", "gate"))
            sp.dma_start(tvrow, dram["tv_rows"]).then_inc(got_tvrow, 16)
            for w in range(2):
                sp.dma_start(tv[:, w], dram["tv"][:, w]).then_inc(got_tv, 16)
            for t in range(T):
                sp.wait_ge(out_ready, t + 1)
                sp.dma_start(dram["out"][:, t, :], x2_nat[:, t, :]).then_inc(stored, 16)
            sp.wait_ge(stored, 16 * T)

        @block.tensor
        def _(pe):
            for f in USES:
                pe.sem_inc(free[f, "act"], RING[f])
                pe.sem_inc(free[f, "dve"], RING[f])
            pe.sem_inc(adj_full, 2)
            pe.sem_inc(adj_freed, 2)
            pe.sem_inc(g_used, 1)
            pe.sem_inc(tmp_free, KB)

            def window(w, slot):
                pe.wait_ge(oh_ready, w + 1)
                pe.wait_ge(adj_freed, w + 1)
                for c in range(WC):
                    mm_ = nc.tensor.matmul(ps[0:P, 6 + slot, 0:WK], oh_s[:, slot, :, c], oh_d[:, slot, :, c, :],
                                           start=(c == 0), stop=(c == WC - 1))
                mm_.then_inc(adj_full, 1)

            def windows(phase, i, part=0, parts=1):
                for w, slot in window_list(phase, i, part, parts):
                    window(w, slot)

            def passes(out, stat_, mov, blocks, start=True, stop=True):
                n = 0
                for b in range(blocks):
                    for hs, hm in ((0, 0), (0, 1), (1, 0)):
                        last = nc.tensor.matmul(out, stat_(hs, b), mov(hm, b), start=start and n == 0,
                                                stop=stop and n == 3 * blocks - 1)
                        n += 1
                return last

            def product(phase, i, slot, w, m, mov, chunk):
                wait_bank(pe, "t", phase, i, slot)
                passes(bank("t", slot), lambda h, b: w[:, h, b, m * 128:(m + 1) * 128],
                       lambda h, b: mov[:, h, b, chunk], KB).then_inc(full["t"], 1)

            def product_chunk(phase, w, mov, j, chunk):
                for m in range(KB):
                    product(phase, KB * j + m, m, w, m, mov, chunk)
                    windows(phase, j, m, KB)

            def transposed(phase, w, mov, ready=None):
                with pe.Fori(0, J) as j:
                    if ready:
                        ready(j)
                    product_chunk(phase, w, mov, j, bass.ts(j, CH))

            def natural_tile(phase, mov, w, t):
                wait_bank(pe, "n", phase, t, t % 2)
                passes(bank("n", t % 2)[0:P, :], lambda h, b: mov[:, h, b, t * P:(t + 1) * P], lambda h, b: w[:, h, b, :], KB
                       ).then_inc(full["n"], 1)

            def natural(phase, mov, w, blocks=KB, ready=None):
                with pe.Fori(0, HT) as i:
                    if ready:
                        ready(i)
                    for c in range(2):
                        wait_bank(pe, "n", phase, 2 * i + c, c)
                        passes(bank("n", c)[0:P, :], lambda h, b: mov[:, h, b, bass.ts(2 * i + c, P)],
                               lambda h, b: w[:, h, b, :], blocks).then_inc(full["n"], 1)

            def flip_tile_to_t(family, phase, src, t):
                wait_bank(pe, family, phase, t, t % 2)
                for m in range(KB):
                    mm_ = nc.tensor.transpose(bank(family, t % 2)[:, m * P:(m + 1) * P],
                                              src[:, t, m * 128:(m + 1) * 128], ident[0:P, 0:P])
                mm_.then_inc(full[family], 1)

            def flip_tile_to_nat(family, phase, src, t):
                wait_bank(pe, family, phase, t, t % 2)
                for m in range(KB):
                    mm_ = nc.tensor.transpose(bank(family, t % 2)[0:P, m * 128:(m + 1) * 128],
                                              src[:, m, t * P:(t + 1) * P], ident[:, :])
                mm_.then_inc(full[family], 1)

            def flip_to_t(phase, src, ready):
                for t in range(T):
                    ready(t)
                    flip_tile_to_t("x", phase, src, t)

            pe.wait_ge(consts, 1)
            flip_to_t("xn", xn_nat, lambda t: pe.wait_ge(ln_done, t + 1))
            wait_weight(pe, "lin")
            transposed("lin", weight("lin"), xn_t, ready=lambda j: wait_done(pe, "x", "xn", 2 * j + 2))
            pe.wait_ge(firsts, 1)
            nc.tensor.matmul(ps[0:1, 7, 0:NW], first[:, 1:2], ident[0:NW, 0:NW], start=True, stop=True).then_inc(firsts_row, 1)
            wait_weight(pe, "k")
            for j in range(J):
                for m in range(KB):
                    product("k", KB * j + m, m, weight("k"), m, xn_t, slice(j * CH, (j + 1) * CH))
                    windows("k", j, m, KB)
                    if m % 2 == 0:
                        pe.wait_ge(lin_out, KB * j + KB)
                        flip_tile_to_nat("x", "x0", gnn_t, 2 * j + m // 2)
            wait_weight(pe, "q")
            for t in range(T + 2):
                if t < T:
                    natural_tile("q", xn_t, weight("q"), t)
                if t >= 2:
                    pe.wait_ge(k_exp, KB)
                    flip_tile_to_nat("x", "kn", k_t, t - 2)
            wait_weight(pe, "v")
            for t in range(T):
                natural_tile("v", xn_t, weight("v"), t)
                windows("v", t // 2, t % 2, 2)
            wait_done(pe, "n", "v", T)
            wait_done(pe, "x", "kn", T)
            for b in range(2):
                wait_bank(pe, "x", "ctx", b, b)
                for q in range(2):
                    part = slice((2 * b + q) * 128, (2 * b + q + 1) * 128)
                    last = passes(bank("x", b)[:, q * 128:(q + 1) * 128], lambda h, t: v_nat[:, h, t, part],
                                  lambda h, t: k_nat[:, h, t, part], T)
                last.then_inc(full["x"], 1)

            def flip_q(t):
                pe.wait_ge(q_soft, t + 1)
                flip_tile_to_t("x", "qt", q_nat, t)

            flip_q(0)
            flip_q(1)
            wait_weight(pe, "out")
            wait_done(pe, "x", "ctx", 2)
            for p in range(KB):
                wait_bank(pe, "n", "m", p, p % 2)
                passes(bank("n", p % 2), lambda h, b: ctx16[:, h, p, :], lambda h, b: weight("out")[:, h, p, :], 1
                       ).then_inc(full["n"], 1)
            flip_q(2)
            flip_q(3)
            wait_done(pe, "n", "m", KB)
            for t in range(T):
                if t + 4 < T:
                    flip_q(t + 4)
                wait_done(pe, "x", "qt", t + 1)
                natural_tile("mix", q_t, mm, t)
                windows("mix", t // 2, t % 2, 2)

            pe.wait_ge(chk_ready, 1)
            nc.tensor.matmul(ps[0:1, 6, 0:2], ones[0:P, 0:1], chk[:, 0:2], start=True, stop=True).then_inc(chk_sum, 1)
            pe.wait_ge(rare_ready, 1)
            is_rare = pe.value_load(rare[0:1, 0:1], min_val=0, max_val=1)

            with pe.If(is_rare):
                with pe.Fori(0, NW) as w:
                    pe.wait_ge(g_low, w + 1)
                    nc.tensor.matmul(ps[0:P, 6, 0:WK], general[:, 2, 0:P], general[:, 2, P:], start=True, stop=False)
                    with pe.Fori(0, COLS // 2) as c:
                        pe.wait_ge(g_oh, w * (COLS // 2) + c + 2)
                        for b in range(2):
                            mm_ = nc.tensor.matmul(ps[0:P, 6, 0:WK], general[:, b, 0:P], general[:, b, P:],
                                                   start=False, stop=False)
                        mm_.then_inc(g_used, 1)
                    nc.tensor.matmul(ps[0:P, 6, 0:WK], general[:, 2, 0:P], general[:, 2, P:], start=False, stop=True
                                     ).then_inc(g_full, 1)

            def low_count(h):
                return lo_a[:, h] if h < LO_TILES else lo_b[:, h - LO_TILES]

            def add_tiles(m, tiles, counts, chunk, start=False, stop=False):
                for h in tiles:
                    for p in range(2):
                        last = nc.tensor.matmul(bank("t", m), gnn_nat[:, p, h, m * 128:(m + 1) * 128], counts(h)[:, chunk],
                                                start=(start and h == 0 and p == 0), stop=(stop and h == T - 1 and p == 1))
                return last

            def gather(phase, general, first_done):
                def chunk_sums(j, chunk, tiles):
                    for m in range(KB):
                        if len(tiles) == T:
                            wait_bank(pe, "t", phase, KB * j + m, m)
                        last = add_tiles(m, tiles, lambda h: adj[:, h], chunk, start=True, stop=not general)
                        if general:
                            last = add_tiles(m, range(T), low_count, chunk, stop=True)
                        last.then_inc(full["t"], 1)

                if first_done:
                    chunk_sums(0, slice(0, CH), [T - 1])
                with pe.Fori(int(first_done), J) as j:
                    chunk_sums(j, bass.ts(j, CH), range(T))

            for layer in range(L):
                if layer == 0:
                    pe.wait_ge(adj_ready, 1)
                    wait_done(pe, "x", "x0", T)
                else:
                    for t in range(T + 2):
                        if t < T:
                            if t % 2 == 0:
                                pe.wait_ge(layer_out, KB * (t // 2) + KB)
                            flip_tile_to_nat("x", "x1", gnn_t, t)
                        if t >= 2:
                            wait_done(pe, "x", "x1", t - 1)
                            for m in range(KB if t < T + 1 else 0):
                                if t == 2:
                                    wait_bank(pe, "t", "agg1", m, m)
                                add_tiles(m, [t - 2], lambda h: adj[:, h], slice(0, CH), start=True)
                with pe.If(is_rare):
                    gather(f"agg{layer}", True, layer > 0)
                with pe.Else():
                    gather(f"agg{layer}", False, layer > 0)
                wait_weight(pe, f"up{layer}")
                transposed(f"up{layer}", weight(f"up{layer}"), h_t,
                           ready=lambda j: wait_done(pe, "t", f"agg{layer}", KB * j + KB))
                wait_weight(pe, f"down{layer}")
                transposed(f"down{layer}", weight(f"down{layer}"), a_t,
                           ready=lambda j: pe.wait_ge(tmp_free, KB + 20 * layer + KB * j + KB))

            wait_weight(pe, "gate")
            for g in range(HT + 2):
                for t in (2 * g, 2 * g + 1):
                    if g < HT:
                        if t % 2 == 0:
                            pe.wait_ge(layer_out, KB * J + KB * g + KB)
                        flip_tile_to_nat("y", "gnn", gnn_t, t)
                for t in (2 * g - 2, 2 * g - 1):
                    if 1 <= g <= HT:
                        pe.wait_ge(ln_done, T + T + t + 1)
                        flip_tile_to_t("x", "x2", x2_nat, t)
                if g >= 2:
                    wait_done(pe, "x", "x2", 2 * g - 2)
                    product_chunk("gate", weight("gate"), x2_t, g - 2, slice((g - 2) * CH, (g - 1) * CH))
            pe.wait_ge(got_tvrow, 32)
            for r in range(2):
                wait_bank(pe, "x", "rows", r, r)
                nc.tensor.matmul(bank("x", r)[0:P, :], ones[0:E, 0:P], tvrow[:, r, :], start=True, stop=True
                                 ).then_inc(full["x"], 1)
            pe.wait_ge(g_bc, 1)
            wait_bank(pe, "x", "g", 0, 0)
            for m in range(KB):
                mm_ = nc.tensor.matmul(bank("x", 0)[:, 0:E], gbc[:, m, :], gfc2[:, m, :], start=(m == 0), stop=(m == KB - 1))
            mm_.then_inc(full["x"], 1)
            wait_bank(pe, "x", "g", 1, 1)
            for m in range(KB):
                mm_ = nc.tensor.matmul(bank("x", 1)[0:E, 0:P], gfc2[:, m, :], gbc[:, m, 0:P], start=(m == 0), stop=(m == KB - 1))
            mm_.then_inc(full["x"], 1)
            pe.wait_ge(g_vec, 1)
            nc.tensor.matmul(ps[0:P, 7, :], grow[:, :], tvrow[:, 2, :], start=True, stop=True).then_inc(b2_sum, 1)
            for m in range(FB):
                pe.wait_ge(wm_split, m + 1)
                for j in range(J):
                    product("ffn1", J * m + j, (J * m + j) % 4, w1m, m, x2_t, slice(j * CH, (j + 1) * CH))
            pe.wait_ge(wm_split, FB + 1)
            natural("ffn2", hid_t, w2m, blocks=FB, ready=lambda i: pe.wait_ge(tmp_free, KB + 2 * KB * J + J + i + 1))

        @block.scalar
        def _(act):
            nc.scalar.preload_act_table(ACT.Sqrt)
            for pair in (1, 3):
                act.dma_start(x[:, 2 * pair:2 * pair + 2, :], dram["x"][:, 2 * pair:2 * pair + 2, :]).then_inc(got_x[pair], 16)

            def split_weight(name):
                i = WEIGHTS.index(name)
                act.wait_ge(w_scaled, i)
                if i >= SLOTS:
                    family, phase = READER[WEIGHTS[i - SLOTS]]
                    act.wait_ge(full[family], before(family, phase) + entry(family, phase)[1])
                nc.scalar.activation(wslot[:, i % SLOTS, 0].rearrange("p k n -> p (k n)"), stage[:, :], ACT.Copy
                                     ).then_inc(w_high, 1)

            def windows(phase, i, part=0, parts=1):
                for w, slot in window_list(phase, i, part, parts):
                    act.wait_ge(adj_full, w + 3)
                    nc.scalar.activation(adj[:, :, bass.ts(w, WIN)], ps[0:P, 6 + slot, 0:WK].rearrange("p (d h) -> p h d", h=T),
                                         ACT.Copy, accum_out=adj_sum[:, bass.ds(w, 1)]).then_inc(adj_freed, 1)

            def deviations(lo, hi, turn, rows_=P, scaled=False):
                act.wait_ge(var_ready, turn + 1)
                nc.scalar.activation(std[0:rows_, lo:hi], mv[0:rows_, lo:hi, 1], ACT.Sqrt,
                                     bias=eps[0:rows_, scaled:scaled + 1], scale=S_X ** -2 if scaled else 1.0
                                     ).then_inc(std_ready, 1)

            def high_tile_nat(family, phase, dst, scale, t, slot):
                wait_full(act, family, phase, t)
                nc.scalar.activation(dst[:, 0, t, :], bank(family, slot)[0:P, :], ACT.Copy, scale=scale
                                     ).then_inc(high[family], 1)

            def normalize(dst, src, t, scale_shift=True):
                nc.scalar.activation(dst[:, t, :], src[:, t, :], ACT.Identity, bias=shift[0:P, t:t + 1],
                                     scale=rstd[0:P, t:t + 1]).then_inc(ln_done, 1)

            def high_tile_t(phase, dst, t, scale=1.0):
                wait_full(act, "x", phase, t)
                nc.scalar.activation(dst[:, 0, :, t * P:(t + 1) * P],
                                     bank("x", t % 2)[:, 0:KB * P].rearrange("p (k n) -> p k n", k=KB), ACT.Copy,
                                     scale=scale).then_inc(high["x"], 1)

            act.wait_ge(consts, 1)
            for g in range(HT + 1):
                if g < HT:
                    deviations(2 * g, 2 * g + 2, TURN["xn"] + g, scaled=True)
                if g:
                    for t in (2 * g - 2, 2 * g - 1):
                        high_tile_t("xn", xn_t, t)
                if g < HT:
                    act.wait_ge(norm_ready, TURN["xn"] + g + 1)
                    for t in (2 * g, 2 * g + 1):
                        normalize(xn_nat, x, t)
                if g == 1:
                    act.wait_ge(got_w, 16)
                    nc.scalar.activation(wslot[:, 0, 0].rearrange("p k n -> p (k n)"), stage[:, :], ACT.Copy, scale=S_W
                                         ).then_inc(w_high, 1)
            split_weight("k")
            act.wait_ge(got_cols, 16)
            nc.scalar.preload_act_table(ACT.Exp)
            with act.Fori(0, J) as j:
                for m in range(KB):
                    wait_full(act, "t", "lin", KB * j + m)
                    nc.scalar.activation(gnn_t[:, m, bass.ts(j, CH)], bank("t", m), ACT.Identity, bias=col("lin_b", m),
                                         scale=S_XW).then_inc(free["t", "act"], 1)
            split_weight("q")
            with act.Fori(0, J) as j:
                for m in range(KB):
                    windows("k", j, m, KB)
                    if m % 2 == 0:
                        high_tile_nat("x", "x0", gnn_nat, S_X, 2 * j + m // 2, m // 2)
            act.wait_ge(k_max, 1)
            for m in range(KB):
                nc.scalar.activation(k_t[:, m, :], k_t[:, m, :], ACT.Exp, bias=kneg[:, m:m + 1],
                                     accum_out=ksum[:, m:m + 1]).then_inc(k_exp, 1)
            split_weight("v")
            for t in range(T + 2):
                if t < T:
                    wait_done(act, "n", "q", t + 1)
                    nc.scalar.activation(q_nat[:, t, :], q_nat[:, t, :], ACT.Exp, scale=S_XW).then_inc(q_exp, 1)
                if t >= 2:
                    high_tile_nat("x", "kn", k_nat, S_K, t - 2, t % 2)
            split_weight("out")
            with act.Fori(0, HT) as i:
                for c in range(2):
                    high_tile_nat("n", "v", v_nat, 1 / S_W, 2 * i + c, c)
                    windows("v", i, c, 2)
            split_weight("up0")
            act.wait_ge(consts, 1)
            for b in range(2):
                wait_full(act, "x", "ctx", b)
                for hh in range(2):
                    part = slice(hh * DH, hh * DH + DH)
                    last = nc.scalar.activation(ctx16[part, 0, 2 * b:2 * b + 2, part],
                                                bank("x", b)[part, 0:256].rearrange("p (q d) -> p q d", q=2)[:, :, part],
                                                ACT.Copy, scale=1 / (S_X * S_K))
                last.then_inc(high["x"], 1)
            high_tile_t("qt", q_t, 0, S_Q)
            high_tile_t("qt", q_t, 1, S_Q)
            act.wait_ge(k_max, 2)
            for p in range(KB):
                wait_full(act, "n", "m", p)
                nc.scalar.activation(mm[:, 0, p, :], bank("n", p % 2), ACT.Identity, scale=krec[:, p:p + 1]).then_inc(high["n"], 1)
            high_tile_t("qt", q_t, 2, S_Q)
            high_tile_t("qt", q_t, 3, S_Q)
            for t in range(T):
                if t + 4 < T:
                    high_tile_t("qt", q_t, t + 4, S_Q)
                windows("mix", t // 2, t % 2, 2)
            split_weight("down0")
            act.wait_ge(rare_ready, 1)
            is_rare = act.value_load(rare[0:1, 0:1], min_val=0, max_val=1)
            with act.If(is_rare):
                with act.Fori(0, NW) as w:
                    act.wait_ge(g_full, w + 1)
                    nc.scalar.activation(adj[:, :, bass.ts(w, WIN)], ps[0:P, 6, 0:WK].rearrange("p (d h) -> p h d", h=T),
                                         ACT.Copy).then_inc(g_high, 1)
            deviations(0, T, TURN["mix"])
            act.wait_ge(norm_ready, TURN["mix"] + 1)
            with act.Fori(0, T) as t_:
                nc.scalar.activation(mix_nat[:, t_, :], mix_nat[:, t_, :], ACT.Identity, bias=shift[0:P, bass.ds(t_, 1)],
                                     scale=rstd[0:P, bass.ds(t_, 1)]).then_inc(ln_done, 1)

            act.wait_ge(bias_ready, 1)
            nc.scalar.preload_act_table(ACT.Sqrt)

            def prelu(phase, turn, dst, bias):
                def product(i, m):
                    wait_full(act, "t", phase, i + m)
                    act.wait_ge(tmp_free, i + (turn + m + 1))
                    nc.scalar.activation(act_tmp[:, m, :], bank("t", m), ACT.Identity, bias=bias(m), scale=1 / S_W
                                         ).then_inc(free["t", "act"], 1)

                def top(j, m):
                    act.wait_ge(prelu_out, KB * j + (turn + m + 1))
                    nc.scalar.activation(dst[:, 0, m, bass.ts(j, CH)], act_tmp[:, m, :], ACT.Copy).then_inc(hid_high, 1)

                with act.Fori(0, J) as j:
                    for m in range(KB):
                        product(KB * j, m)
                        if m:
                            top(j, m - 1)
                    top(j, KB - 1)

            def hidden(i):
                m, j = divmod(i, J)
                wait_full(act, "t", "ffn1", i)
                act.wait_ge(tmp_free, 2 * KB * J + i + 1)
                for out in (hid_t[:, 0, m, j * CH:(j + 1) * CH], act_tmp[:, i % KB, :]):
                    last = nc.scalar.activation(out, bank("t", i % KB), ACT.Relu, bias=b1m[:, m:m + 1], scale=1 / S_W)
                last.then_inc(free["t", "act"], 1)

            def relu_chunk(layer, chunk):
                for m in range(KB):
                    nc.scalar.activation(gnn_t[:, m, chunk], gnn_t[:, m, chunk], ACT.Relu, bias=bn_shift[:, m:m + 1],
                                         scale=bn_scale[:, m:m + 1]).then_inc(layer_out, 1)

            for layer in range(L):
                with act.Fori(0, J) as j:
                    for m in range(KB):
                        wait_full(act, "t", f"agg{layer}", KB * j + m)
                        nc.scalar.activation(h_t[:, 0, m, bass.ts(j, CH)], bank("t", m), ACT.Copy, scale=S_H / S_X
                                             ).then_inc(high["t"], 1)
                split_weight("gate" if layer else "up1")
                prelu(f"up{layer}", 20 * layer, a_t, lambda m: bias_a[:, KB * layer + m:KB * layer + m + 1])
                if layer == 0:
                    act.wait_ge(mixed, T)
                with act.Fori(0, J) as j:
                    for m in range(KB):
                        wait_full(act, "t", f"down{layer}", KB * j + m)
                        nc.scalar.activation(gnn_t[:, m, bass.ts(j, CH)], bank("t", m), ACT.Identity,
                                             bias=col("b2", KB * layer + m), scale=1 / (S_W * S_H)).then_inc(free["t", "act"], 1)
                deviations(0, KB, TURN["bn"] + layer, rows_=128)
                if layer == 0:
                    split_weight("down1")
                act.wait_ge(norm_ready, TURN["bn"] + layer + 1)
                relu_chunk(layer, slice(0, CH))
                if layer == 0:
                    with act.Fori(0, J - 1) as j:
                        relu_chunk(layer, bass.ts(j + 1, CH))
                        for c in range(2):
                            high_tile_nat("x", "x1", gnn_nat, S_X, 2 * j + c, c)
                    for t in (T - 2, T - 1):
                        high_tile_nat("x", "x1", gnn_nat, S_X, t, t % 2)

            def gate_chunk(j):
                for m in range(KB):
                    wait_full(act, "t", "gate", KB * j + m)
                    nc.scalar.activation(bank("t", m), bank("t", m), ACT.Relu, bias=col("gfc1_b", m), scale=S_XW,
                                         accum_out=gsum[:, m, j:j + 1]).then_inc(free["t", "act"], 1)

            for g in range(HT + 2):
                if g + 1 < HT:
                    relu_chunk(L - 1, slice((g + 1) * CH, (g + 2) * CH))
                if g < HT:
                    deviations(2 * g, 2 * g + 2, TURN["x2"] + g, scaled=True)
                if 1 <= g <= HT:
                    for t in (2 * g - 2, 2 * g - 1):
                        high_tile_t("x2", x2_t, t)
                if g < HT:
                    act.wait_ge(norm_ready, TURN["x2"] + g + 1)
                    for t in (2 * g, 2 * g + 1):
                        normalize(x2_nat, x, t)
                if g >= 2:
                    gate_chunk(g - 2)

            for part in range(FB):
                act.wait_ge(merged, 2 * E * (part + 1))
                nc.scalar.activation(w1m[:, 0, :, part * 128:(part + 1) * 128], wm32[:, 0, :].rearrange("p (k f) -> p k f", k=KB)
                                     [:, :, part * 128:(part + 1) * 128], ACT.Copy, scale=S_W).then_inc(wm_high, 1)
            act.wait_ge(b1_done, 1)
            for i in range(FB * J - 2):
                hidden(i)
            act.wait_ge(merged, 2 * E * (FB + 1))
            nc.scalar.activation(wm16[:, 1, 0, :], wm32[:, 1, :], ACT.Copy, scale=S_W).then_inc(wm_high, 1)
            for i in range(FB * J - 2, FB * J):
                hidden(i)
            for g in range(HT):
                deviations(2 * g, 2 * g + 2, TURN["out"] + g)
                act.wait_ge(norm_ready, TURN["out"] + g + 1)
                for t in (2 * g, 2 * g + 1):
                    normalize(x2_nat, x2_nat, t)

        @block.vector
        def _(dve):
            steps = [0]

            def chain(ins, times=1):
                ins.then_inc(dve_step, 1)
                steps[0] += times
                return steps[0]

            def then(ins):
                dve.wait_ge(dve_step, chain(ins))

            def first_column(phase, i, n=0):
                return [dve.value_load(window_at[0:1, bass.ds(w, 1)], min_val=0, max_val=COLS)
                        for w, _ in window_list(phase, i)[n:n + 1]]

            def windows(phase, i, part, parts, columns):
                for w, slot in window_list(phase, i, part, parts):
                    at = columns[-1]
                    dve.wait_ge(adj_full, w + 1)
                    nc.vector.tensor_tensor(rel[:, slot], keys[:, bass.ds(at, WC)].unsqueeze(2).to_broadcast([P, WC, T]),
                                            win_key[:, bass.ds(w, 1)].unsqueeze(2).to_broadcast([P, WC, T]),
                                            ALU.subtract).then_inc(rel_ready, 1)
                    nc.vector.tensor_tensor(oh_s[:, slot], iota_s, sources[:, bass.ds(at, WC)].unsqueeze(1)
                                            .to_broadcast([P, P, WC]), ALU.is_equal)
                    dve.wait_ge(rel_ready, w + 1)
                    last = nc.vector.tensor_tensor(oh_d[:, slot], iota_d.unsqueeze(2).to_broadcast([P, WIN, WC, T]),
                                                   rel[:, slot].unsqueeze(1).to_broadcast([P, WIN, WC, T]), ALU.is_equal)
                    last.then_inc(oh_ready, 1)
                    columns += first_column(phase, i, len(columns))

            def low(out, src, hi, scale=1.0):
                if isinstance(scale, float) and scale == 1.0:
                    return nc.vector.tensor_tensor(out, src, hi, ALU.subtract)
                return nc.vector.scalar_tensor_tensor(out, src, scale, hi, ALU.mult, ALU.subtract)

            def low_tile_nat(family, phase, dst, scale, t, slot):
                wait_high(dve, family, phase, t)
                low(dst[:, 1, t, :], bank(family, slot)[0:P, :], dst[:, 0, t, :], scale).then_inc(free[family, "dve"], 1)

            def aggregate(lo, hi):
                for t_ in range(lo, hi):
                    last = nc.vector.bn_aggr(mv[0:P, t_, :], stat[0:P, 6 * t_:6 * t_ + 6])
                last.then_inc(var_ready, 1)

            def normalizer(lo, hi, turn):
                dve.wait_ge(std_ready, turn + 1)
                then(nc.vector.reciprocal(rstd[0:P, lo:hi], std[0:P, lo:hi]))
                nc.vector.scalar_tensor_tensor(shift[0:P, lo:hi], mv[0:P, lo:hi, 0], -1.0, rstd[0:P, lo:hi], ALU.mult,
                                               ALU.mult).then_inc(norm_ready, 1)

            def pair_statistics(src, g):
                for t in (2 * g, 2 * g + 1):
                    last = nc.vector.bn_stats(stat[0:P, 6 * t:6 * t + 6], src[:, t, :])
                then(last)
                aggregate(2 * g, 2 * g + 2)

            def low_tile_t(phase, dst, t, scale=1.0):
                wait_high(dve, "x", phase, t)
                tile = slice(t * P, (t + 1) * P)
                low(dst[:, 1, :, tile], bank("x", t % 2)[:, 0:KB * P].rearrange("p (k n) -> p k n", k=KB), dst[:, 0, :, tile],
                    scale).then_inc(free["x", "dve"], 1)

            def layer_norm(src, lo, hi, turn):
                for t_ in range(lo, hi):
                    last = nc.vector.bn_stats(stat[0:P, 6 * t_:6 * t_ + 6], src[:, t_, :])
                then(last)
                aggregate(lo, hi)
                normalizer(lo, hi, turn)

            for g in range(HT + 1):
                if g < HT:
                    dve.wait_ge(got_x[g], 16)
                    pair_statistics(x, g)
                if g:
                    for t in (2 * g - 2, 2 * g - 1):
                        low_tile_t("xn", xn_t, t)
                if g < HT:
                    normalizer(2 * g, 2 * g + 2, TURN["xn"] + g)
                if g == 2:
                    dve.wait_ge(w_high, 1)
                    low(wslot[:, 0, 1].rearrange("p k n -> p (k n)"), stage[:, :], wslot[:, 0, 0].rearrange("p k n -> p (k n)"), S_W
                        ).then_inc(w_split, 1)

            def prelu(phase, base, src, neg, alpha, done):
                with dve.Fori(0, J) as j:
                    for m in range(0, KB, 2):
                        for q in (m, m + 1):
                            wait_done(dve, "t", phase, KB * j + q + 1)
                            nc.vector.tensor_scalar(neg[:, q, :], src(q, j), 0.0, alpha(q), ALU.min, ALU.mult
                                                    ).then_inc(dve_step, 1)
                        for q in (m, m + 1):
                            dve.wait_ge(dve_step, KB * j + (base + q + 1))
                            nc.vector.scalar_tensor_tensor(src(q, j), src(q, j), 0.0, neg[:, q, :], ALU.max, ALU.add
                                                           ).then_inc(done, 1)
                steps[0] += KB * J

            dve.wait_ge(got_edges, 32)
            then(nc.vector.tensor_scalar(src_tile, ints[:, 0, :], float(P), None, ALU.is_ge))
            for h in range(2, T):
                then(nc.vector.scalar_tensor_tensor(src_tile, ints[:, 0, :], float(P * h), src_tile, ALU.is_ge, ALU.add))
            dve.wait_ge(iotas, 1)
            nc.vector.scalar_tensor_tensor(keys[:, 0:COLS], ints[:, 1, :], float(T), src_tile, ALU.mult, ALU.add)
            nc.vector.scalar_tensor_tensor(sources[:, 0:COLS], src_tile, -float(P), ints[:, 0, :], ALU.mult, ALU.add)
            nc.vector.tensor_copy(iota_mem[:, 0:WK], iota_i[:, 0:WK])
            nc.vector.tensor_copy(iota_s, iota_i[:, 0:P].unsqueeze(2).to_broadcast([P, P, WC]))
            nc.vector.tensor_copy(win_key[:, :], iota_i[:, WK:])
            nc.vector.tensor_copy(heads, heads_i)
            then(nc.vector.tensor_copy(first[:, 0:1], first_i))
            then(nc.vector.tensor_scalar(heads_lt, heads, first[:, 0:1], None, ALU.is_lt, ALU.add, accum_out=first[:, 1:2]))
            nc.vector.tensor_scalar(first[:, 1:2], first[:, 1:2], -1.0, 0.0, ALU.add, ALU.max).then_inc(firsts, 1)
            dve.wait_ge(got_cols, 16)
            prelu("lin", steps[0], lambda m, j: gnn_t[:, m, bass.ts(j, CH)], lin_neg, lambda m: col("lin_a", m), lin_out)
            dve.wait_ge(firsts_row, 1)
            nc.vector.tensor_copy(window_at[:, :], ps[0:1, 7, 0:NW]).then_inc(window_ready, 1)
            dve.wait_ge(window_ready, 1)
            with dve.Fori(0, J) as j:
                columns = first_column("k", j)
                for m in range(KB):
                    windows("k", j, m, KB, columns)
                    wait_full(dve, "t", "k", KB * j + m)
                    nc.vector.tensor_scalar(k_t[:, m, bass.ts(j, CH)], bank("t", m), S_XW, None, ALU.mult, ALU.max,
                                            accum_out=kmax[:, m, bass.ds(j, 1)]).then_inc(free["t", "dve"], 1)
                    if m % 2:
                        low_tile_nat("x", "x0", gnn_nat, S_X, 2 * j + m // 2, m // 2)
            wait_done(dve, "t", "k", 20)
            nc.vector.tensor_reduce(kneg[:, :], kmax[:, :, :], AX.X, ALU.max, negate=True).then_inc(k_max, 1)
            def heads_of(ap):
                return ap.rearrange("p (h d) -> p h d", h=H)

            def per_head(ap):
                return ap.unsqueeze(2).to_broadcast([P, H, DH])

            for i in range(HT + 1):
                for t_ in (2 * i, 2 * i + 1) if i < HT else ():
                    wait_full(dve, "n", "q", t_)
                    then(nc.vector.tensor_reduce(qmax[:, t_, :], heads_of(bank("n", t_ % 2)[0:P, :]), AX.X, ALU.max))
                    nc.vector.tensor_tensor(heads_of(q_nat[:, t_, :]), heads_of(bank("n", t_ % 2)[0:P, :]),
                                            per_head(qmax[:, t_, :]), ALU.subtract).then_inc(free["n", "dve"], 1)
                for t_ in (2 * i - 2, 2 * i - 1) if i else ():
                    low_tile_nat("x", "kn", k_nat, S_K, t_, t_ % 2)
                for t_ in (2 * i, 2 * i + 1) if i < HT else ():
                    dve.wait_ge(q_exp, t_ + 1)
                    then(nc.vector.tensor_reduce(qsum[:, t_, :], heads_of(q_nat[:, t_, :]), AX.X, ALU.add))
                    nc.vector.reciprocal(qsum[:, t_, :], qsum[:, t_, :]).then_inc(q_rec, 1)
            with dve.Fori(0, HT) as i:
                columns = first_column("v", i)
                for c in range(2):
                    windows("v", i, c, 2, columns)
                    low_tile_nat("n", "v", v_nat, 1 / S_W, 2 * i + c, c)
            dve.wait_ge(k_exp, KB)
            nc.vector.reciprocal(krec[:, :], ksum[:, :]).then_inc(k_max, 1)
            dve.wait_ge(k_max, 2)
            for b in range(2):
                wait_high(dve, "x", "ctx", b)
                for hh in range(2):
                    part = slice(hh * DH, hh * DH + DH)
                    last = low(ctx16[part, 1, 2 * b:2 * b + 2, part],
                               bank("x", b)[part, 0:256].rearrange("p (q d) -> p q d", q=2)[:, :, part],
                               ctx16[part, 0, 2 * b:2 * b + 2, part], 1 / (S_X * S_K))
                last.then_inc(free["x", "dve"], 1)
            low_tile_t("qt", q_t, 0, S_Q)
            low_tile_t("qt", q_t, 1, S_Q)
            for p in range(KB):
                wait_high(dve, "n", "m", p)
                low(mm[:, 1, p, :], bank("n", p % 2), mm[:, 0, p, :], krec[:, p:p + 1]).then_inc(free["n", "dve"], 1)
            def add_self(lo, hi):
                for h in range(lo, hi):
                    diagonal = adj[:, h, h * P:(h + 1) * P]
                    last = nc.vector.tensor_tensor(diagonal, diagonal, ident[0:P, 0:P], ALU.add)
                return last

            dve.wait_ge(adj_freed, 2 + first_window("mix"))
            add_self(0, DONE_EARLY)
            low_tile_t("qt", q_t, 2, S_Q)
            low_tile_t("qt", q_t, 3, S_Q)
            dve.wait_ge(got_rows, 16)
            for t in range(T):
                if t % 2 == 0:
                    columns = first_column("mix", t // 2)
                windows("mix", t // 2, t % 2, 2, columns)
                if t + 4 < T:
                    low_tile_t("qt", q_t, t + 4, S_Q)
                wait_full(dve, "n", "mix", t)
                nc.vector.scalar_tensor_tensor(mix_nat[:, t, :], bank("n", t % 2)[0:P, :],
                                               1 / (S_Q * S_M * DH ** 0.5 * N), rows[:, 0, :], ALU.mult, ALU.add
                                               ).then_inc(free["n", "dve"], 1)
            wait_done(dve, "n", "mix", T)

            dve.wait_ge(adj_freed, 2 + NW)
            nc.vector.tensor_reduce(chk[:, 0:1], adj_sum[:, :], AX.X, ALU.add)
            nc.vector.tensor_scalar(stat[0:P, 64:64 + NW], adj_sum[:, :], F16_EXACT, None, ALU.is_ge, ALU.add,
                                    accum_out=chk[:, 1:2]).then_inc(chk_ready, 1)
            dve.wait_ge(chk_sum, 1)
            then(nc.vector.tensor_copy(chk[0:1, 2:4], ps[0:1, 6, 0:2]))
            then(nc.vector.scalar_tensor_tensor(chk[0:1, 2:3], chk[0:1, 2:3], float(EDGES), chk[0:1, 3:4], ALU.not_equal, ALU.add))
            nc.vector.tensor_scalar(rare[:, 0:1], chk[0:1, 2:3], 0.0, None, ALU.is_gt).then_inc(rare_ready, 1)
            dve.wait_ge(rare_ready, 1)
            is_rare = dve.value_load(rare[0:1, 0:1], min_val=0, max_val=1)
            with dve.If(is_rare):
                nc.vector.memset(general[:, 2, :], 0.0).then_inc(g_low, 1)
                nc.vector.memset(rel[:, 0], 0.0).then_inc(g_oh, 1)
                with dve.Fori(0, NW) as w:
                    with dve.Fori(0, COLS // 2) as c:
                        dve.wait_ge(g_used, w * (COLS // 2) + c + 1)
                        for b in range(2):
                            e = 2 * c + b
                            nc.vector.tensor_scalar(general[:, b, P:], iota_mem[:, 0:WK], win_key[:, bass.ds(w, 1)],
                                                    keys[:, bass.ds(e, 1)], ALU.add, ALU.is_equal)
                            last = nc.vector.tensor_tensor(general[:, b, 0:P], iota_mem[:, 0:P], sources[:, bass.ds(e, 1)]
                                                           .to_broadcast([P, P]), ALU.is_equal)
                        last.then_inc(g_oh, 1)
                    dve.wait_ge(g_high, w + 1)
                    counts = ps[0:P, 6, 0:WK].rearrange("p (d h) -> p h d", h=T)
                    part = bass.ts(w, WIN)
                    nc.vector.tensor_tensor(lo_a[:, :, part], counts[:, 0:LO_TILES, :], adj[:, 0:LO_TILES, part], ALU.subtract)
                    nc.vector.tensor_tensor(lo_b[:, :, part], counts[:, LO_TILES:T, :], adj[:, LO_TILES:T, part], ALU.subtract
                                            ).then_inc(g_low, 1)
                dve.wait_ge(g_low, NW + 1)
                for h in range(T):
                    low_ = lo_a[:, h] if h < LO_TILES else lo_b[:, h - LO_TILES]
                    last = nc.vector.tensor_tensor(low_[:, h * P:(h + 1) * P], low_[:, h * P:(h + 1) * P], ident[0:P, 0:P], ALU.add)
                last.then_inc(adj_ready, 1)
            with dve.Else():
                add_self(DONE_EARLY, T).then_inc(adj_ready, 1)

            layer_norm(mix_nat, 0, T, TURN["mix"])

            nc.vector.tensor_scalar(bias_a[:, :], col("b1", 0, 2 * KB), S_H, None, ALU.mult).then_inc(bias_ready, 1)

            def low_hidden(i):
                m, j = divmod(i, J)
                chunk = slice(j * CH, (j + 1) * CH)
                wait_done(dve, "t", "ffn1", i + 1)
                nc.vector.tensor_tensor(hid_t[:, 1, m, chunk], act_tmp[:, i % KB, :], hid_t[:, 0, m, chunk], ALU.subtract
                                        ).then_inc(tmp_free, 1)

            for layer in range(L):
                with dve.Fori(0, J) as j:
                    for m in range(KB):
                        chunk = bass.ts(j, CH)
                        wait_high(dve, "t", f"agg{layer}", KB * j + m)
                        low(h_t[:, 1, m, chunk], bank("t", m), h_t[:, 0, m, chunk], S_H / S_X).then_inc(free["t", "dve"], 1)
                prelu(f"up{layer}", steps[0], lambda m, j: act_tmp[:, m, :], negative, lambda m: col("conv_a", layer), prelu_out)
                with dve.Fori(0, J) as j:
                    for m in range(KB):
                        wait_done(dve, "t", f"down{layer}", KB * j + m + 1)
                        ins = nc.vector.bn_stats(stat[:, :].rearrange("p (m j s) -> p m (j s)", m=KB, j=J)[:, m, bass.ts(j, 6)],
                                                 gnn_t[:, m, bass.ts(j, CH)])
                    ins.then_inc(dve_step, 1)
                steps[0] += J
                dve.wait_ge(dve_step, steps[0])
                for m in range(KB):
                    last = nc.vector.bn_aggr(mv[:, m, :], stat[:, 6 * J * m:6 * J * (m + 1)])
                last.then_inc(var_ready, 1)
                dve.wait_ge(std_ready, TURN["bn"] + layer + 1)
                then(nc.vector.reciprocal(bn_scale[:, :], std[:, 0:KB]))
                then(nc.vector.tensor_tensor(bn_scale[:, :], bn_scale[:, :], col("gamma", KB * layer, KB), ALU.mult))
                then(nc.vector.tensor_tensor(bn_shift[:, :], mv[:, 0:KB, 0], bn_scale[:, :], ALU.mult))
                nc.vector.tensor_tensor(bn_shift[:, :], col("beta", KB * layer, KB), bn_shift[:, :], ALU.subtract
                                        ).then_inc(norm_ready, 1)
                if layer == 0:
                    with dve.Fori(0, HT) as i:
                        for c in range(2):
                            low_tile_nat("x", "x1", gnn_nat, S_X, 2 * i + c, c)

            dve.wait_ge(mixed, T)
            for g in range(HT + 1):
                if g < HT:
                    for t in (2 * g, 2 * g + 1):
                        wait_full(dve, "y", "gnn", t)
                        nc.vector.tensor_tensor(x[:, t, :], bank("y", t % 2)[0:P, :], x[:, t, :], ALU.add
                                                ).then_inc(free["y", "dve"], 1)
                    wait_done(dve, "y", "gnn", 2 * g + 2)
                    pair_statistics(x, g)
                if g:
                    for t in (2 * g - 2, 2 * g - 1):
                        low_tile_t("x2", x2_t, t)
                if g < HT:
                    normalizer(2 * g, 2 * g + 2, TURN["x2"] + g)
            dve.wait_ge(got_ln, 32)
            then(nc.vector.tensor_scalar(rows[:, 0:2, :], rows[:, 0:2, :], 1 - LN_MERGE * E, None, ALU.mult))
            for r in range(2):
                wait_full(dve, "x", "rows", r)
                nc.vector.scalar_tensor_tensor(rows[:, r, :], bank("x", r)[0:P, :], LN_MERGE, rows[:, r, :], ALU.mult, ALU.add
                                               ).then_inc(free["x", "dve"], 1)
            wait_done(dve, "t", "gate", 20)
            then(nc.vector.tensor_reduce(gmean[:, :], gsum[:, :, :], AX.X, ALU.add))
            nc.vector.tensor_scalar(gbc[:, :, :], gmean[:, :].unsqueeze(2).to_broadcast([128, KB, 128]), 1 / N, None, ALU.mult
                                    ).then_inc(g_bc, 1)
            wait_full(dve, "x", "g", 0)
            nc.vector.tensor_tensor(gcol[:, :], bank("x", 0)[:, 0:E], col("gfc2_b", 0, E), ALU.add).then_inc(free["x", "dve"], 1)
            wait_full(dve, "x", "g", 1)
            nc.vector.tensor_scalar(grow[:, :], bank("x", 1)[0:E, 0:P], cols[0:E, COL["gfc2_bc"][0]:COL["gfc2_bc"][0] + 1], None,
                                    ALU.add).then_inc(g_vec, 1)
            wait_done(dve, "x", "g", 1)
            dve.wait_ge(got_wm, 16)
            dve.wait_ge(got_tv, 32)
            half_done = [0]

            def merge(total, task, between=()):
                halves = [(total[:, k:k + n], lambda e, k=k, n=n: task(e)[:, k:k + n])
                          for n in [total.shape[1] // 2] for k in (0, n)]
                for e in range(E):
                    for h, (out, part) in enumerate(halves):
                        if e:
                            dve.wait_ge(merged, half_done[0] + 2 * e + h - 1)
                        nc.vector.scalar_tensor_tensor(out, part(e), gcol[:, e:e + 1], out, ALU.mult, ALU.add).then_inc(merged, 1)
                    for work in between[e:e + 1]:
                        work()
                half_done[0] += 2 * E
                dve.wait_ge(merged, half_done[0])

            def w1_part(ap, part):
                return ap.rearrange("p (k f) -> p k f", k=KB)[:, :, part * 128:(part + 1) * 128]

            for part in range(FB):
                merge(w1_part(wm32[:, 0, :], part), lambda e: w1_part(tv[:, 0, e, :], part))
                if part == 0:
                    scratch = stat[:, 0:FB * E].rearrange("p (f e) -> p f e", f=FB)
                    then(nc.vector.tensor_tensor(scratch, col("tv_b1", 0, FB * E).rearrange("p (f e) -> p f e", f=FB),
                                                 gcol[:, :].unsqueeze(1).to_broadcast([128, FB, E]), ALU.mult))
                    then(nc.vector.tensor_reduce(b1m[:, :], scratch, AX.X, ALU.add))
                    then(nc.vector.tensor_tensor(b1m[:, :], b1m[:, :], col("ffn_b1", 0, FB), ALU.add))
                    nc.vector.tensor_scalar(b1m[:, :], b1m[:, :], S_X, None, ALU.mult).then_inc(b1_done, 1)
                dve.wait_ge(wm_high, part + 1)
                low(w1m[:, 1, :, part * 128:(part + 1) * 128], w1_part(wm32[:, 0, :], part),
                    w1m[:, 0, :, part * 128:(part + 1) * 128], S_W).then_inc(wm_split, 1)
            dve.wait_ge(b2_sum, 1)
            then(nc.vector.tensor_tensor(b2_row, ps[0:P, 7, :], b2_row, ALU.add))

            def rows_of(ap):
                return ap.rearrange("p (k n) -> p k n", k=2)

            merge(rows_of(wm32[:, 1, :]), lambda e: rows_of(tv[:, 1, e, :]), [lambda i=i: low_hidden(i) for i in range(E)])
            dve.wait_ge(wm_high, FB + 1)
            low(wm16[:, 1, 1, :], wm32[:, 1, :], wm16[:, 1, 0, :], S_W).then_inc(wm_split, 1)
            for i in range(E, FB * J):
                low_hidden(i)
            with dve.Fori(0, T) as t_:
                nc.vector.scalar_tensor_tensor(x2_nat[:, t_, :], x2_nat[:, t_, :], 1 / S_X, b2_row, ALU.mult, ALU.add
                                               ).then_inc(dve_step, 1)
            steps[0] += T
            dve.wait_ge(dve_step, steps[0])
            for g in range(HT + 1):
                if g < HT:
                    for t in (2 * g, 2 * g + 1):
                        wait_full(dve, "n", "ffn2", t)
                        nc.vector.scalar_tensor_tensor(x2_nat[:, t, :], bank("n", t % 2)[0:P, :], S_XW, x2_nat[:, t, :],
                                                       ALU.mult, ALU.add).then_inc(free["n", "dve"], 1)
                    wait_done(dve, "n", "ffn2", 2 * g + 2)
                    pair_statistics(x2_nat, g)
                if g:
                    for t in (2 * g - 2, 2 * g - 1):
                        dve.wait_ge(ln_done, 3 * T + t + 1)
                        nc.vector.tensor_tensor(x2_nat[:, t, :], x2_nat[:, t, :], rows[:, 0, :], ALU.mult).then_inc(scaled, 1)
                if g < HT:
                    normalizer(2 * g, 2 * g + 2, TURN["out"] + g)

        @block.gpsimd
        def _(pool):
            steps = [0]

            def then(ins):
                ins.then_inc(pool_step, 1)
                steps[0] += 1
                pool.wait_ge(pool_step, steps[0])

            nc.gpsimd.memset(keys[:, COLS:KEYS], -1.0)
            nc.gpsimd.memset(sources[:, COLS:KEYS], 0.0)
            nc.gpsimd.iota(iota_i[:, 0:WK], pattern=[[1, WK]], base=0, channel_multiplier=0)
            nc.gpsimd.iota(iota_i[:, WK:], pattern=[[WK, NW]], base=0, channel_multiplier=0)
            nc.gpsimd.iota(first_i, pattern=[[0, 1]], base=0, channel_multiplier=WIN).then_inc(iotas, 1)
            nc.gpsimd.memset(eps[:, 0:1], LN_EPS)
            nc.gpsimd.memset(eps[:, 1:2], LN_EPS / (S_X * S_X))
            nc.gpsimd.memset(ones[:, :], 1.0)
            nc.gpsimd.memset(ctx16[:, :, :, :], 0.0)
            then(nc.gpsimd.memset(ident[:, :], 0.0))
            nc.gpsimd.affine_select(out=ident[:, :], in_=ident[:, :], compare_op=ALU.not_equal, fill=1.0, base=0,
                                    pattern=[[-1, 128]], channel_multiplier=1).then_inc(consts, 1)

            def split_weight(name):
                i = WEIGHTS.index(name)
                pool.wait_ge(got_w, 16 * (i + 1))
                nc.gpsimd.tensor_scalar(stage[:, :], stage[:, :], S_W, 1.0, ALU.mult, ALU.mult).then_inc(w_scaled, 1)
                pool.wait_ge(w_high, i + 1)
                nc.gpsimd.tensor_tensor(wslot[:, i % SLOTS, 1].rearrange("p k n -> p (k n)"), stage[:, :],
                                        wslot[:, i % SLOTS, 0].rearrange("p k n -> p (k n)"), ALU.subtract).then_inc(w_split, 1)

            for name in ("k", "q", "v"):
                split_weight(name)
            with pool.Fori(0, T) as t_:
                pool.wait_ge(q_rec, t_ + 1)
                tile = q_nat[:, bass.ds(t_, 1), :].rearrange("p o (h d) -> p (o h) d", h=H)
                nc.gpsimd.tensor_tensor(tile, tile, qsum[:, bass.ds(t_, 1), :].rearrange("p o h -> p (o h)").unsqueeze(2)
                                        .to_broadcast([P, H, DH]), ALU.mult).then_inc(q_soft, 1)
            for name in ("out", "up0", "down0"):
                split_weight(name)
            base = steps[0]
            with pool.Fori(0, T) as t_:
                pool.wait_ge(ln_done, T + t_ + 1)
                tile = mix_nat[:, t_, :]
                nc.gpsimd.tensor_tensor(tile, tile, rows[:, 1, :], ALU.mult).then_inc(pool_step, 1)
                pool.wait_ge(pool_step, t_ + (base + 1))
                nc.gpsimd.tensor_tensor(x[:, t_, :], x[:, t_, :], tile, ALU.add).then_inc(mixed, 1)

            def low_prelu(layer):
                with pool.Fori(0, J) as j:
                    for m in range(KB):
                        pool.wait_ge(hid_high, KB * j + (KB * J * layer + m + 1))
                        nc.gpsimd.tensor_tensor(a_t[:, 1, m, bass.ts(j, CH)], act_tmp[:, m, :], a_t[:, 0, m, bass.ts(j, CH)],
                                                ALU.subtract).then_inc(tmp_free, 1)

            split_weight("up1")
            low_prelu(0)
            split_weight("down1")
            split_weight("gate")
            low_prelu(1)
            pool.wait_ge(ln_done, 3 * T)
            wait_done(pool, "x", "rows", 2)
            with pool.Fori(0, T) as t_:
                nc.gpsimd.tensor_tensor(x[:, t_, :], x[:, t_, :], rows[:, 1, :], ALU.add).then_inc(xb_ready, 1)
            with pool.Fori(0, T) as t_:
                pool.wait_ge(xb_ready, t_ + 1)
                pool.wait_ge(scaled, t_ + 1)
                nc.gpsimd.tensor_tensor(x2_nat[:, t_, :], x2_nat[:, t_, :], x[:, t_, :], ALU.add).then_inc(out_ready, 1)


def kernel(**inputs):
    import numpy as np
    import concourse.bacc as bacc
    from concourse.bass_utils import run_bass_kernel_spmd

    def arr(name):
        return np.asarray(inputs[name])

    def blocks(w):
        return np.ascontiguousarray(w.reshape(-1, 128, w.shape[-1]).transpose(1, 0, 2).reshape(128, -1))

    def columns(v):
        return v.reshape(-1, 128).T

    def spread(v, n):
        return np.broadcast_to(v, (n,) + v.shape)

    g, m, f = "L0_gnn_", "L0_mix_", "L0_ffn_"
    qkv = arr(m + "w_qkv")
    src, dst = (arr(n).reshape(COLS, P) for n in ("src", "dst"))
    gfc2_b = arr(f + "gfc2_b")
    gfc2_col = np.zeros((128, 1), gfc2_b.dtype)
    gfc2_col[:E, 0] = gfc2_b
    weights = {
        "lin": arr(g + "lin_W").T, "q": qkv[:, 0:D], "k": qkv[:, D:2 * D], "v": qkv[:, 2 * D:], "out": arr(m + "w_out"),
        "up0": arr(g + "conv_W1")[0].T, "up1": arr(g + "conv_W1")[1].T, "down0": arr(g + "conv_W2")[0].T,
        "down1": arr(g + "conv_W2")[1].T, "gate": arr(f + "gfc1_w").T,
    }
    arrays = {"w_" + n: blocks(w) for n, w in weights.items()}
    arrays["x"] = np.ascontiguousarray(arr("x").reshape(T, P, D).transpose(1, 0, 2))
    arrays["edges"] = np.ascontiguousarray(np.stack([src.T, dst.T], 1))
    arrays["heads"] = np.ascontiguousarray(spread(dst[:, 0], NW))
    arrays["cols"] = np.ascontiguousarray(np.concatenate([
        columns(arr(g + "lin_b")), columns(arr(g + "lin_a")), columns(arr(g + "conv_b1")), columns(arr(g + "conv_b2")),
        columns(arr(g + "bn_gamma")), columns(arr(g + "bn_beta")), spread(arr(g + "conv_a"), 128),
        columns(arr(f + "gfc1_b")), columns(arr(f + "b1")),
        arr(f + "tv_b1").reshape(E, FB, 128).transpose(2, 1, 0).reshape(128, FB * E), spread(gfc2_b, 128), gfc2_col], 1))
    arrays["mix_rows"] = np.ascontiguousarray(spread(np.stack([arr(m + "b_out"), arr(m + "ln_scale")]), P))
    arrays["ln_rows"] = np.ascontiguousarray(spread(np.stack([arr(f + "ln_g"), arr(f + "ln_b"), arr(f + "b2")]), P))
    arrays["tv_rows"] = np.ascontiguousarray(np.stack([arr(f + "tv_ln_g"), arr(f + "tv_ln_b"), arr(f + "tv_b2")], 1))
    arrays["gfc2"] = blocks(arr(f + "gfc2_w").T).reshape(128, KB, E)
    arrays["w_ffn"] = np.concatenate([blocks(arr(f + "W1").T), blocks(arr(f + "W2").T)], 1)
    arrays["tv"] = np.ascontiguousarray(np.stack(
        [np.stack([blocks(w.T) for w in arr(f + n)], 1) for n in ("tv_W1", "tv_W2")], 1))

    nc = bacc.Bacc("TRN2", target_bir_lowering=False, num_devices=1)
    dram = {n: nc.dram_tensor("in_" + n, a.shape, mybir.dt.from_np(a.dtype), kind="ExternalInput").ap()
            for n, a in arrays.items()}
    dram["out"] = nc.dram_tensor("out_0", (P, T, D), F32, kind="ExternalOutput").ap()
    gps_block(nc, dram)
    result = run_bass_kernel_spmd(nc, [{"in_" + n: a for n, a in arrays.items()}], core_ids=[0])
    return np.ascontiguousarray(result.results[0]["out_0"].transpose(1, 0, 2)).reshape(N, D)
```

```python
from contextlib import ExitStack

import concourse.bass as bass
from concourse import mybir

F32 = mybir.dt.float32
F16 = mybir.dt.float16
I32 = mybir.dt.int32
ALU = mybir.AluOpType
ACT = mybir.ActivationFunctionType
AX = mybir.AxisListType

N, D, H, F, E, L, EDGES = 1250, 512, 8, 256, 8, 2, 41250
DH = D // H
P = 125
T = N // P
KB = D // 128
FB = F // 128
CH = 2 * P
J = N // CH
COLS = EDGES // P
WIN = 25
NW = N // WIN
WC = 9
KEYS = COLS + WC
WK = T * WIN
OHS = 2 * (WC * (P + WK) + 1)
HT = T // 2
LN_EPS, BN_EPS, LN_MERGE = 1e-5, 1e-5, 0.03
F16_EXACT = 2048.0
LO_TILES = 8

TURN = {"xn": 0, "mix": HT, "bn": HT + 1, "x2": HT + 1 + 2 * L, "out": 2 * HT + 1 + 2 * L}
BN_PARTS = ((0, KB - 1), (KB - 1, KB))

S_X, S_W, S_H, S_K, S_Q, S_M = 16.0, 256.0, 1 / 16, 256.0, 1024.0, 256.0
S_XW = 1 / (S_X * S_W)

COL = {}
for _name, _n in (("lin_b", 4), ("lin_a", 4), ("b1", 8), ("b2", 8), ("gamma", 8), ("beta", 8), ("conv_a", 2),
                  ("gfc1_b", 4), ("ffn_b1", 2), ("tv_b1", 16), ("gfc2_b", 8), ("gfc2_bc", 1)):
    COL[_name] = (sum(n for _, n in COL.values()), _n)
NCOL = sum(n for _, n in COL.values())

WEIGHTS = ["lin", "k", "q", "v", "out", "up0", "down0", "up1", "down1", "gate"]
SLOTS = 3
PE_EXPERTS = 4
WINDOWS = {"k": 4, "v": 4, "mix": 2}

USES = {
    "n": [("q", T, "dve", 0), ("v", T, "dve", 1), ("m", KB, "dve", 1), ("mix", T, "dve", 0), ("ffn2", T, "dve", 0)],
    "t": [("lin", 20, "act", 0), ("k", 20, "dve", 0), ("agg0", 20, "dve", 1), ("up0", 20, "act", 0),
          ("down0", 20, "act", 0), ("agg1", 20, "dve", 1), ("up1", 20, "act", 0), ("down1", 20, "act", 0),
          ("gate", 20, "act", 0), ("ffn1", 10, "act", 0)],
    "x": [("xn", T, "dve", 1), ("x0", T, "dve", 1), ("kn", T, "dve", 1),
          ("ctx", 2, "dve", 1), ("qt", T, "dve", 1), ("x1", T, "dve", 1), ("x2", T, "dve", 1),
          ("rows", 2, "dve", 0), ("g", 2, "dve", 0)],
    "y": [("gnn", T, "dve", 0)],
}
RING = {"n": 2, "t": 4, "x": 2, "y": 2}
BANKS_FROM = {"q": ("t", "k", 17), "agg0": ("n", "mix", 9), "ffn2": ("t", "ffn1", 9)}


def before(family, phase, who=None, high=False):
    total = 0
    for name, uses, by, hi in USES[family]:
        if name == phase:
            return total
        if (who is None or by == who) and (hi or not high):
            total += uses
    raise KeyError(phase)


def pool_scales(t):
    return t % 2 == 1 and t < T - 2


def entry(family, phase):
    return next(u for u in USES[family] if u[0] == phase)


def first_window(phase):
    at = 0
    for name, per in WINDOWS.items():
        if name == phase:
            return at
        at += per * J
    raise KeyError(phase)


DONE_EARLY = first_window("mix") * WIN // P


def window_list(phase, i, part=0, parts=1):
    n = WINDOWS.get(phase, 0)
    own = range(n * part // parts, n * (part + 1) // parts)
    first = first_window(phase) if n else 0
    return [(n * i + (first + c), (n * i + first + c if isinstance(i, int) else first + c) % 2) for c in own]


assert sum(WINDOWS.values()) * J == NW and J == HT

READER = {"lin": ("t", "lin"), "k": ("t", "k"), "q": ("n", "q"), "v": ("n", "v"), "out": ("n", "m"), "up0": ("t", "up0"),
          "down0": ("t", "down0"), "up1": ("t", "up1"), "down1": ("t", "down1"), "gate": ("t", "gate")}


def gps_block(nc, dram):
    with ExitStack() as ctx:
        def sb(name, shape, dt=F32):
            return ctx.enter_context(nc.sbuf_tensor(name, shape, dt))

        def sem(name):
            return ctx.enter_context(nc.semaphore(name))

        ps = ctx.enter_context(nc.psum_tensor("ps", [128, 8, 512], F32))

        def bank(family, slot):
            if family == "t":
                return ps[:, slot, 0:CH]
            return ps[:, {"n": 0, "x": 4, "y": 6}[family] + slot, :]

        x = sb("x", [P, T, D])
        r1 = sb("r1", [128, T * D])
        r2 = sb("r2", [128, T * D])
        r3 = sb("r3", [128, T * D])
        late = sb("late", [128, 2 * T * D + N * T // 2])
        r4, r5 = late[:, 0:T * D], late[:, T * D:2 * T * D]
        adj = late[0:P, 2 * T * D:].bitcast(F16).rearrange("p (h d) -> p h d", h=T)

        def nat32(r):
            return r[0:P].rearrange("p (t c) -> p t c", t=T)

        def nat16(r):
            return r[0:P].bitcast(F16).rearrange("p (h t c) -> p h t c", h=2, t=T)

        def tr32(r):
            return r[:, 0:KB * N].rearrange("p (k n) -> p k n", k=KB)

        def tr16(r, blocks=KB):
            return r[:, 0:blocks * N].bitcast(F16).rearrange("p (h k n) -> p h k n", h=2, k=blocks)

        xn_nat, xn_t = nat32(r5), tr16(r1)
        gnn_t, gnn_nat = tr32(r3), nat16(r2)
        k_t, k_nat = tr32(r4), nat16(r5)
        q_nat, q_t = nat32(r3), tr16(r1)
        v_nat = nat16(r4)
        mm = r5[:, 0:KB * D].bitcast(F16).rearrange("p (h k n) -> p h k n", h=2, k=KB)
        mix_nat = nat32(r3)
        h_t, a_t = tr16(r4), tr16(r5)
        x2_nat, x2_t = nat32(r2), tr16(r1)
        hid_t = tr16(r3, FB)
        tv = late[:, 0:2 * E * KB * F].rearrange("p (w e n) -> p w e n", w=2, e=E)

        stage = sb("stage", [128, KB * D])
        wm32 = stage[:, :].rearrange("p (w n) -> p w n", w=2)
        wslot = sb("wslot", [128, SLOTS, 2, KB, D], F16)
        wm16 = wslot[:, 2].rearrange("p h k n -> p (h k n)").rearrange("p (w h n) -> p w h n", w=2, h=2)
        w1m = wm16[:, 0].rearrange("p h (k f) -> p h k f", k=KB)
        w2m = wm16[:, 1].rearrange("p h (k c) -> p h k c", k=FB)
        assert WEIGHTS.index("gate") % SLOTS == 0

        ohs = sb("ohs", [128, OHS], F16)
        oh_s = ohs[0:P, 0:2 * (WC * P + 1)].rearrange("p (b n) -> p b n", b=2)[:, :, 0:WC * P].rearrange(
            "p b (s w) -> p b s w", w=WC)
        oh_d = ohs[0:P, 2 * (WC * P + 1):].rearrange("p (b d w h) -> p b d w h", b=2, w=WC, h=T)
        act_tmp = ohs[:, 0:2 * KB * CH].bitcast(F32).rearrange("p (m n) -> p m n", m=KB)
        negative = ohs[:, 2 * KB * CH:4 * KB * CH].bitcast(F32).rearrange("p (m n) -> p m n", m=KB)
        tvrow = ohs[0:E, 2 * KB * CH:2 * KB * CH + 6 * D].bitcast(F32).rearrange("e (r c) -> e r c", r=3)
        g_diag = ohs[:, 2 * KB * CH + 6 * D:2 * KB * CH + 6 * D + PE_EXPERTS * 256].bitcast(F32).rearrange(
            "p (e n) -> p e n", e=PE_EXPERTS)
        general = ohs[0:P, 0:3 * (P + WK)].rearrange("p (b n) -> p b n", b=3)
        lo_a = r1[0:P, 0:LO_TILES * N // 2].bitcast(F16).rearrange("p (h d) -> p h d", h=LO_TILES)
        lo_b = ohs[0:P, OHS - (T - LO_TILES) * N:].rearrange("p (h d) -> p h d", h=T - LO_TILES)

        ident = sb("ident", [128, 128])
        cols = sb("cols", [128, NCOL])
        rows = sb("rows", [P, 2, D])
        keys = sb("keys", [P, KEYS])
        sources = sb("sources", [P, KEYS], F16)
        iota_mem = sb("iota", [P, WK + P * WC + 1], F16)
        iota_d = iota_mem[:, 0:WK].rearrange("p (d h) -> p d h", h=T)
        iota_s = iota_mem[:, WK:WK + P * WC].rearrange("p (s w) -> p s w", w=WC)
        b2_row = iota_mem[:, 0:2 * D].bitcast(F32)
        win_key = sb("win_key", [P, NW])
        rel = sb("rel", [P, 2, WC, T], F16)
        window_at = sb("window_at", [1, NW], I32)
        adj_sum = sb("adj_sum", [P, NW])
        chk = sb("chk", [P, 4])
        ones = sb("ones", [128, 128])
        rare = sb("rare", [1, 2], I32)
        stat = sb("stat", [128, KB * J * 6])
        mv = sb("mv", [128, T, 2])
        std = sb("std", [128, T])
        eps = sb("eps", [128, 3])
        rstd = sb("rstd", [128, T])
        shift = sb("shift", [128, T])
        bn_scale, bn_shift = sb("bn_scale", [128, KB]), sb("bn_shift", [128, KB])
        kmax = sb("kmax", [128, KB, J])
        kneg = sb("kneg", [128, KB])
        ksum = sb("ksum", [128, KB])
        krec = sb("krec", [128, KB])
        qmax = sb("qmax", [P, T, H])
        qsum = sb("qsum", [P, T, H])
        ctx16 = sb("ctx16", [128, 2, KB, 128], F16)
        bias_a = sb("bias_a", [128, 2 * KB])
        gsum = sb("gsum", [128, KB, J])
        gmean = sb("gmean", [128, KB])
        gbc = ctx16[:, :, :, :].rearrange("p h k n -> p (h k n)").bitcast(F32).rearrange("p (k n) -> p k n", k=KB)
        gcol = sb("gcol", [128, E])
        grow = sb("grow", [E, P])
        b1m = sb("b1m", [128, FB])
        gfc2 = sb("gfc2", [128, KB, E])

        ints = r2[0:P, 0:2 * COLS].bitcast(I32).rearrange("p (a c) -> p a c", a=2)
        heads_i = r2[0:NW, 700:700 + COLS].bitcast(I32)
        heads = r2[0:NW, 1100:1100 + COLS]
        heads_lt = r2[0:NW, 1500:1500 + COLS]
        iota_i = r2[0:P, 1900:1900 + WK + NW].bitcast(I32)
        src_tile = r2[0:P, 2400:2400 + COLS]
        first = r2[0:NW, 2800:2802]
        lin_neg = r2[:, 3000:3000 + KB * CH].rearrange("p (m n) -> p m n", m=KB)
        first_i = r2[0:NW, 2802:2803].bitcast(I32)

        def col(name, i=0, n=1):
            return cols[:, COL[name][0] + i:COL[name][0] + i + n]

        got_edges, got_cols, got_rows, got_w = sem("got_edges"), sem("got_cols"), sem("got_rows"), sem("got_w")
        got_x = [sem(f"got_x{i}") for i in range(HT)]
        got_tvrow, got_wm, got_tv, got_ln = sem("got_tvrow"), sem("got_wm"), sem("got_tv"), sem("got_ln")
        stored = sem("stored")
        full = {f: sem(f"{f}_full") for f in USES}
        high = {f: sem(f"{f}_high") for f in USES}
        free = {(f, e): sem(f"{f}_free_{e}") for f in USES for e in ("act", "dve")}
        def sems(*names):
            return (sem(n) for n in names)

        w_scaled, w_high, w_split = sems("w_scaled", "w_high", "w_split")
        consts, iotas = sems("consts", "iotas")
        dve_step, pool_step = sems("dve_step", "pool_step")
        firsts, firsts_row, window_ready = sems("firsts", "firsts_row", "window_ready")
        rel_ready, oh_ready, adj_full, adj_freed, self_early = sems("rel_ready", "oh_ready", "adj_full", "adj_freed", "self_early")
        chk_ready, chk_sum, rare_ready, adj_ready = sems("chk_ready", "chk_sum", "rare_ready", "adj_ready")
        g_oh, g_used, g_full, g_high, g_low = sems("g_oh", "g_used", "g_full", "g_high", "g_low")
        var_ready, std_ready, norm_ready, ln_done = sems("var_ready", "std_ready", "norm_ready", "ln_done")
        k_max, k_exp, q_exp, q_rec, q_soft, mixed = sems("k_max", "k_exp", "q_exp", "q_rec", "q_soft", "mixed")
        lin_out, prelu_out, hid_high, tmp_free, bias_ready, layer_out = sems(
            "lin_out", "prelu_out", "hid_high", "tmp_free", "bias_ready", "layer_out")
        g_bc, g_vec, diag_ready, b1_done, b2_sum, b2_ready = sems("g_bc", "g_vec", "diag_ready", "b1_done", "b2_sum", "b2_ready")
        merged, w2_part, wm_high, wm_split = sems("merged", "w2_part", "wm_high", "wm_split")
        xb_ready, b2_added, scaled, out_ready, last_ready = sems("xb_ready", "b2_added", "scaled", "out_ready", "last_ready")

        def wait_full(eng, family, phase, i):
            eng.wait_ge(full[family], before(family, phase) + i + 1)

        def wait_high(eng, family, phase, i):
            eng.wait_ge(high[family], before(family, phase, high=True) + i + 1)

        def wait_done(eng, family, phase, n):
            who = entry(family, phase)[2]
            eng.wait_ge(free[family, who], RING[family] + before(family, phase, who) + n)

        def wait_bank(pe, family, phase, i, slot):
            names = [u[0] for u in USES[family]]
            _, _, who, _ = entry(family, phase)
            pe.wait_ge(free[family, who], before(family, phase, who) + i + 1)
            if names.index(phase):
                last, uses, by, _ = USES[family][names.index(phase) - 1]
                if by != who:
                    pe.wait_ge(free[family, by], before(family, last, by) + uses + slot + 1)
            if phase in BANKS_FROM and slot < 2:
                family, last, uses = BANKS_FROM[phase]
                wait_done(pe, family, last, uses + slot)

        def wait_slot(eng, i):
            if i >= SLOTS:
                family, phase = READER[WEIGHTS[i - SLOTS]]
                eng.wait_ge(full[family], before(family, phase) + entry(family, phase)[1])

        def weight(name):
            return wslot[:, WEIGHTS.index(name) % SLOTS]

        def wait_weight(pe, name):
            pe.wait_ge(w_split, WEIGHTS.index(name) + 1)

        block = ctx.enter_context(nc.Block())

        @block.sync
        def _(sp):
            for pair in (0, 2):
                sp.dma_start(x[:, 2 * pair:2 * pair + 2, :], dram["x"][:, 2 * pair:2 * pair + 2, :]).then_inc(got_x[pair], 16)
            sp.dma_start(stage[:, :], dram["w_lin"]).then_inc(got_w, 16)
            sp.dma_start(x[:, 8:10, :], dram["x"][:, 8:10, :]).then_inc(got_x[4], 16)
            sp.dma_start(ints, dram["edges"]).then_inc(got_edges, 16)
            sp.dma_start(heads_i, dram["heads"]).then_inc(got_edges, 16)
            sp.dma_start(cols[:, :], dram["cols"]).then_inc(got_cols, 16)
            sp.dma_start(rows[:, 0:2, :], dram["mix_rows"]).then_inc(got_rows, 16)
            sp.dma_start(gfc2[:, :, :], dram["gfc2"]).then_inc(got_tvrow, 16)
            for i, name in enumerate(WEIGHTS[1:], 1):
                sp.wait_ge(w_split, i)
                sp.dma_start(stage[:, :], dram["w_" + name]).then_inc(got_w, 16)
            sp.wait_ge(mixed, T)
            sp.dma_start(rows[:, :, :], dram["ln_rows"][:, 0:2]).then_inc(got_ln, 16)
            sp.wait_ge(adj_ready, 1)
            sp.dma_start(b2_row, dram["ln_rows"][:, 2]).then_inc(got_ln, 16)
            sp.wait_ge(w_split, len(WEIGHTS))
            sp.dma_start(stage[:, :], dram["w_ffn"]).then_inc(got_wm, 16)
            sp.wait_ge(full["t"], before("t", "gate"))
            sp.dma_start(tvrow, dram["tv_rows"]).then_inc(got_tvrow, 16)
            for w in range(2):
                sp.dma_start(tv[:, w], dram["tv"][:, w]).then_inc(got_tv, 16)
            for t in range(T):
                if t < T - 1:
                    sp.wait_ge(out_ready, t + 1)
                else:
                    sp.wait_ge(last_ready, 1)
                sp.dma_start(dram["out"][:, t, :], x2_nat[:, t, :]).then_inc(stored, 16)
            sp.wait_ge(stored, 16 * T)

        @block.tensor
        def _(pe):
            for f in USES:
                pe.sem_inc(free[f, "act"], RING[f])
                pe.sem_inc(free[f, "dve"], RING[f])
            pe.sem_inc(adj_full, 2)
            pe.sem_inc(adj_freed, 2)
            pe.sem_inc(g_used, 1)
            pe.sem_inc(tmp_free, KB)

            def window(w, slot):
                pe.wait_ge(oh_ready, w + 1)
                pe.wait_ge(adj_freed, w + 1)
                for c in range(WC):
                    mm_ = nc.tensor.matmul(ps[0:P, 6 + slot, 0:WK], oh_s[:, slot, :, c], oh_d[:, slot, :, c, :],
                                           start=(c == 0), stop=(c == WC - 1))
                mm_.then_inc(adj_full, 1)

            def windows(phase, i, part=0, parts=1):
                for w, slot in window_list(phase, i, part, parts):
                    window(w, slot)

            def passes(out, stat_, mov, blocks, start=True, stop=True):
                n = 0
                for b in range(blocks):
                    for hs, hm in ((0, 0), (0, 1), (1, 0)):
                        last = nc.tensor.matmul(out, stat_(hs, b), mov(hm, b), start=start and n == 0,
                                                stop=stop and n == 3 * blocks - 1)
                        n += 1
                return last

            def product(phase, i, slot, w, m, mov, chunk):
                wait_bank(pe, "t", phase, i, slot)
                passes(bank("t", slot), lambda h, b: w[:, h, b, m * 128:(m + 1) * 128],
                       lambda h, b: mov[:, h, b, chunk], KB).then_inc(full["t"], 1)

            def product_chunk(phase, w, mov, j, chunk):
                for m in range(KB):
                    product(phase, KB * j + m, m, w, m, mov, chunk)

            def transposed(phase, w, mov, ready=None, chunks=J):
                with pe.Fori(0, chunks) as j:
                    if ready:
                        ready(j)
                    product_chunk(phase, w, mov, j, bass.ts(j, CH))

            def natural_tile(phase, mov, w, t):
                wait_bank(pe, "n", phase, t, t % 2)
                passes(bank("n", t % 2)[0:P, :], lambda h, b: mov[:, h, b, t * P:(t + 1) * P], lambda h, b: w[:, h, b, :], KB
                       ).then_inc(full["n"], 1)

            def natural(phase, mov, w, blocks=KB, ready=None):
                with pe.Fori(0, HT) as i:
                    if ready:
                        ready(i)
                    for c in range(2):
                        wait_bank(pe, "n", phase, 2 * i + c, c)
                        passes(bank("n", c)[0:P, :], lambda h, b: mov[:, h, b, bass.ts(2 * i + c, P)],
                               lambda h, b: w[:, h, b, :], blocks).then_inc(full["n"], 1)

            def flip_tile_to_t(family, phase, src, t):
                wait_bank(pe, family, phase, t, t % 2)
                for m in range(KB):
                    mm_ = nc.tensor.transpose(bank(family, t % 2)[:, m * P:(m + 1) * P],
                                              src[:, t, m * 128:(m + 1) * 128], ident[0:P, 0:P])
                mm_.then_inc(full[family], 1)

            def flip_tile_to_nat(family, phase, src, t, ready=None):
                wait_bank(pe, family, phase, t, t % 2)
                for m in range(KB):
                    if ready:
                        ready(m)
                    mm_ = nc.tensor.transpose(bank(family, t % 2)[0:P, m * 128:(m + 1) * 128],
                                              src[:, m, t * P:(t + 1) * P], ident[:, :])
                mm_.then_inc(full[family], 1)

            pe.wait_ge(consts, 1)
            for t in range(T):
                pe.wait_ge(ln_done, t + 1)
                flip_tile_to_t("x", "xn", xn_nat, t)
            wait_weight(pe, "lin")
            transposed("lin", weight("lin"), xn_t, ready=lambda j: wait_done(pe, "x", "xn", 2 * j + 2), chunks=J - 1)
            pe.wait_ge(firsts, 1)
            nc.tensor.matmul(ps[0:1, 7, 0:NW], first[:, 1:2], ident[0:NW, 0:NW], start=True, stop=True).then_inc(firsts_row, 1)
            wait_done(pe, "x", "xn", T)
            product_chunk("lin", weight("lin"), xn_t, J - 1, slice((J - 1) * CH, N))
            wait_weight(pe, "k")
            for j in range(J):
                for m in range(KB):
                    product("k", KB * j + m, m, weight("k"), m, xn_t, slice(j * CH, (j + 1) * CH))
                    if KB * j + m:
                        windows("k", *divmod(KB * j + m - 1, KB), KB)
                    if m % 2 == 0:
                        pe.wait_ge(lin_out, KB * j + KB)
                        flip_tile_to_nat("x", "x0", gnn_t, 2 * j + m // 2)
            windows("k", J - 1, KB - 1, KB)
            wait_weight(pe, "q")
            for t in range(T + 2):
                if t < T:
                    natural_tile("q", xn_t, weight("q"), t)
                if t >= 2:
                    pe.wait_ge(k_exp, KB)
                    flip_tile_to_nat("x", "kn", k_t, t - 2)
            wait_weight(pe, "v")
            for t in range(T):
                natural_tile("v", xn_t, weight("v"), t)
                if t:
                    windows("v", (t - 1) // 2, (t - 1) % 2, 2)
            windows("v", HT - 1, 1, 2)
            wait_done(pe, "n", "v", T)
            wait_done(pe, "x", "kn", T)
            for b in range(2):
                wait_bank(pe, "x", "ctx", b, b)
                for q in range(2):
                    part = slice((2 * b + q) * 128, (2 * b + q + 1) * 128)
                    last = passes(bank("x", b)[:, q * 128:(q + 1) * 128], lambda h, t: v_nat[:, h, t, part],
                                  lambda h, t: k_nat[:, h, t, part], T)
                last.then_inc(full["x"], 1)

            def flip_q(t):
                pe.wait_ge(q_soft, t + 1)
                flip_tile_to_t("x", "qt", q_nat, t)

            flip_q(0)
            flip_q(1)
            wait_weight(pe, "out")
            wait_done(pe, "x", "ctx", 2)
            for p in range(KB):
                wait_bank(pe, "n", "m", p, p % 2)
                passes(bank("n", p % 2), lambda h, b: ctx16[:, h, p, :], lambda h, b: weight("out")[:, h, p, :], 1
                       ).then_inc(full["n"], 1)
            flip_q(2)
            flip_q(3)
            wait_done(pe, "n", "m", KB)
            for t in range(T):
                if t + 4 < T:
                    flip_q(t + 4)
                wait_done(pe, "x", "qt", t + 1)
                natural_tile("mix", q_t, mm, t)
                if t:
                    windows("mix", (t - 1) // 2, (t - 1) % 2, 2)
            windows("mix", HT - 1, 1, 2)

            def low_count(h):
                return lo_a[:, h] if h < LO_TILES else lo_b[:, h - LO_TILES]

            def add_tiles(m, tiles, counts, chunk, start=False, stop=False):
                for h in tiles:
                    for p in range(2):
                        last = nc.tensor.matmul(bank("t", m), gnn_nat[:, p, h, m * 128:(m + 1) * 128], counts(h)[:, chunk],
                                                start=(start and h == 0 and p == 0), stop=(stop and h == tiles[-1] and p == 1))
                return last

            def first_sums(blocks):
                for m in blocks:
                    wait_bank(pe, "t", "agg0", m, m)
                    add_tiles(m, range(T - 1), lambda h: adj[:, h], slice(0, CH), start=True)

            wait_done(pe, "x", "x0", T)
            pe.wait_ge(self_early, 1)
            first_sums((0, 1))
            pe.wait_ge(chk_ready, 1)
            nc.tensor.matmul(ps[0:1, 6, 0:2], ones[0:P, 0:1], chk[:, 0:2], start=True, stop=True).then_inc(chk_sum, 1)
            first_sums((2, 3))
            pe.wait_ge(rare_ready, 1)
            is_rare = pe.value_load(rare[0:1, 0:1], min_val=0, max_val=1)

            with pe.If(is_rare):
                for m in range(KB):
                    add_tiles(m, [T - 1], lambda h: adj[:, h], slice(0, CH), stop=True)
                with pe.Fori(0, NW) as w:
                    pe.wait_ge(g_low, w + 1)
                    nc.tensor.matmul(ps[0:P, 6, 0:WK], general[:, 2, 0:P], general[:, 2, P:], start=True, stop=False)
                    with pe.Fori(0, COLS // 2) as c:
                        pe.wait_ge(g_oh, w * (COLS // 2) + c + 2)
                        for b in range(2):
                            mm_ = nc.tensor.matmul(ps[0:P, 6, 0:WK], general[:, b, 0:P], general[:, b, P:],
                                                   start=False, stop=False)
                        mm_.then_inc(g_used, 1)
                    nc.tensor.matmul(ps[0:P, 6, 0:WK], general[:, 2, 0:P], general[:, 2, P:], start=False, stop=True
                                     ).then_inc(g_full, 1)

            def gather(phase, general, first_done):
                def chunk_sums(j, chunk, tiles):
                    for m in range(KB):
                        if len(tiles) == T:
                            wait_bank(pe, "t", phase, KB * j + m, m)
                        last = add_tiles(m, tiles, lambda h: adj[:, h], chunk, start=True, stop=not general)
                        if general:
                            last = add_tiles(m, range(T), low_count, chunk, stop=True)
                        last.then_inc(full["t"], 1)

                if first_done:
                    chunk_sums(0, slice(0, CH), [T - 1])
                with pe.Fori(int(first_done), J) as j:
                    chunk_sums(j, bass.ts(j, CH), range(T))

            for layer in range(L):
                if layer == 0:
                    pe.wait_ge(adj_ready, 1)
                else:
                    for t in range(T + 2):
                        if t < T:
                            flip_tile_to_nat("x", "x1", gnn_t, t, lambda m: pe.wait_ge(layer_out, KB * (t // 2) + m + 1))
                        if t >= 2:
                            wait_done(pe, "x", "x1", t - 1)
                            for m in range(KB if t < T + 1 else 0):
                                if t == 2:
                                    wait_bank(pe, "t", "agg1", m, m)
                                add_tiles(m, [t - 2], lambda h: adj[:, h], slice(0, CH), start=True)
                with pe.If(is_rare):
                    gather(f"agg{layer}", True, layer > 0)
                with pe.Else():
                    gather(f"agg{layer}", False, True)
                wait_weight(pe, f"up{layer}")
                transposed(f"up{layer}", weight(f"up{layer}"), h_t,
                           ready=lambda j: wait_done(pe, "t", f"agg{layer}", KB * j + KB))
                wait_weight(pe, f"down{layer}")
                transposed(f"down{layer}", weight(f"down{layer}"), a_t,
                           ready=lambda j: pe.wait_ge(tmp_free, KB + 20 * layer + KB * j + KB))

            wait_weight(pe, "gate")
            for g in range(HT + 2):
                for t in (2 * g, 2 * g + 1):
                    if g < HT:
                        flip_tile_to_nat("y", "gnn", gnn_t, t, lambda m: pe.wait_ge(layer_out, KB * J + KB * g + m + 1))
                for t in (2 * g - 2, 2 * g - 1):
                    if 1 <= g <= HT:
                        pe.wait_ge(ln_done, T + T + t + 1)
                        flip_tile_to_t("x", "x2", x2_nat, t)
                if g >= 2:
                    wait_done(pe, "x", "x2", 2 * g - 2)
                    product_chunk("gate", weight("gate"), x2_t, g - 2, slice((g - 2) * CH, (g - 1) * CH))
            pe.wait_ge(got_tvrow, 32)
            for r in range(2):
                wait_bank(pe, "x", "rows", r, r)
                nc.tensor.matmul(bank("x", r)[0:P, :], ones[0:E, 0:P], tvrow[:, r, :], start=True, stop=True
                                 ).then_inc(full["x"], 1)
            pe.wait_ge(g_bc, 1)
            wait_bank(pe, "x", "g", 0, 0)
            for m in range(KB):
                mm_ = nc.tensor.matmul(bank("x", 0)[:, 0:E], gbc[:, m, :], gfc2[:, m, :], start=(m == 0), stop=(m == KB - 1))
            mm_.then_inc(full["x"], 1)
            wait_bank(pe, "x", "g", 1, 1)
            for m in range(KB):
                mm_ = nc.tensor.matmul(bank("x", 1)[0:E, 0:P], gfc2[:, m, :], gbc[:, m, 0:P], start=(m == 0), stop=(m == KB - 1))
            mm_.then_inc(full["x"], 1)
            pe.wait_ge(g_vec, 1)
            nc.tensor.matmul(ps[0:P, 7, :], grow[:, :], tvrow[:, 2, :], start=True, stop=True).then_inc(b2_sum, 1)
            pe.wait_ge(got_tv, 32)
            for k in range(PE_EXPERTS):
                pe.wait_ge(diag_ready, k + 1)
                for h in range(2):
                    last = nc.tensor.matmul(ps[:, 4 + h, :], g_diag[:, k, :], tv[:, 1, E - PE_EXPERTS + k, h * D:(h + 1) * D],
                                            start=(k == 0), stop=(k == PE_EXPERTS - 1))
            last.then_inc(w2_part, 1)
            for m in range(FB):
                pe.wait_ge(wm_split, m + 1)
                for j in range(J):
                    product("ffn1", J * m + j, (J * m + j) % 4, w1m, m, x2_t, slice(j * CH, (j + 1) * CH))
            pe.wait_ge(wm_split, FB + 2)
            natural("ffn2", hid_t, w2m, blocks=FB, ready=lambda i: pe.wait_ge(tmp_free, KB + 2 * KB * J + J + i + 1))

        @block.scalar
        def _(act):
            nc.scalar.preload_act_table(ACT.Sqrt)
            for pair in (1, 3):
                act.dma_start(x[:, 2 * pair:2 * pair + 2, :], dram["x"][:, 2 * pair:2 * pair + 2, :]).then_inc(got_x[pair], 16)

            def split_weight(name):
                i = WEIGHTS.index(name)
                act.wait_ge(w_scaled, i + 1)
                wait_slot(act, i)
                nc.scalar.activation(wslot[:, i % SLOTS, 0].rearrange("p k n -> p (k n)"), stage[:, :], ACT.Copy
                                     ).then_inc(w_high, 1)

            def windows(phase, i, part=0, parts=1):
                for w, slot in window_list(phase, i, part, parts):
                    act.wait_ge(adj_full, w + 3)
                    nc.scalar.activation(adj[:, :, bass.ts(w, WIN)], ps[0:P, 6 + slot, 0:WK].rearrange("p (d h) -> p h d", h=T),
                                         ACT.Copy, accum_out=adj_sum[:, bass.ds(w, 1)]).then_inc(adj_freed, 1)

            def deviations(lo, hi, turn, rows_=P, scaled=0):
                act.wait_ge(var_ready, turn + 1)
                nc.scalar.activation(std[0:rows_, lo:hi], mv[0:rows_, lo:hi, 1], ACT.Sqrt,
                                     bias=eps[0:rows_, scaled:scaled + 1], scale=S_X ** -2 if scaled == 1 else 1.0
                                     ).then_inc(std_ready, 1)

            def high_tile_nat(family, phase, dst, scale, t, slot):
                wait_full(act, family, phase, t)
                nc.scalar.activation(dst[:, 0, t, :], bank(family, slot)[0:P, :], ACT.Copy, scale=scale
                                     ).then_inc(high[family], 1)

            def normalize(dst, src, t):
                nc.scalar.activation(dst[:, t, :], src[:, t, :], ACT.Identity, bias=shift[0:P, t:t + 1],
                                     scale=rstd[0:P, t:t + 1]).then_inc(ln_done, 1)

            def high_tile_t(phase, dst, t, scale=1.0):
                wait_full(act, "x", phase, t)
                nc.scalar.activation(dst[:, 0, :, t * P:(t + 1) * P],
                                     bank("x", t % 2)[:, 0:KB * P].rearrange("p (k n) -> p k n", k=KB), ACT.Copy,
                                     scale=scale).then_inc(high["x"], 1)

            act.wait_ge(consts, 1)
            for g in range(-2, HT + 1):
                if g + 2 < HT:
                    deviations(2 * g + 4, 2 * g + 6, TURN["xn"] + g + 2, scaled=1)
                for c in range(2):
                    if 0 <= g < HT:
                        act.wait_ge(norm_ready, TURN["xn"] + g + 1)
                        normalize(xn_nat, x, 2 * g + c)
                    if g > 0:
                        high_tile_t("xn", xn_t, 2 * g - 2 + c)
            act.wait_ge(got_cols, 16)
            nc.scalar.preload_act_table(ACT.Exp)
            with act.Fori(0, J) as j:
                for m in range(KB):
                    wait_full(act, "t", "lin", KB * j + m)
                    nc.scalar.activation(gnn_t[:, m, bass.ts(j, CH)], bank("t", m), ACT.Identity, bias=col("lin_b", m),
                                         scale=S_XW).then_inc(free["t", "act"], 1)
            split_weight("q")
            with act.Fori(0, J) as j:
                for m in range(KB):
                    windows("k", j, m, KB)
                    if m % 2 == 0:
                        high_tile_nat("x", "x0", gnn_nat, S_X, 2 * j + m // 2, m // 2)
            act.wait_ge(k_max, 1)
            for m in range(KB):
                nc.scalar.activation(k_t[:, m, :], k_t[:, m, :], ACT.Exp, bias=kneg[:, m:m + 1],
                                     accum_out=ksum[:, m:m + 1]).then_inc(k_exp, 1)
            split_weight("v")
            for t in range(T + 2):
                if t < T:
                    wait_done(act, "n", "q", t + 1)
                    nc.scalar.activation(q_nat[:, t, :], q_nat[:, t, :], ACT.Exp, scale=S_XW).then_inc(q_exp, 1)
                if t >= 2:
                    high_tile_nat("x", "kn", k_nat, S_K, t - 2, t % 2)
            split_weight("out")
            for t in range(T):
                high_tile_nat("n", "v", v_nat, 1 / S_W, t, t % 2)
                windows("v", t // 2, t % 2, 2)
            split_weight("up0")
            act.wait_ge(consts, 1)
            for b in range(2):
                wait_full(act, "x", "ctx", b)
                for hh in range(2):
                    part = slice(hh * DH, hh * DH + DH)
                    last = nc.scalar.activation(ctx16[part, 0, 2 * b:2 * b + 2, part],
                                                bank("x", b)[part, 0:256].rearrange("p (q d) -> p q d", q=2)[:, :, part],
                                                ACT.Copy, scale=1 / (S_X * S_K))
                last.then_inc(high["x"], 1)
            high_tile_t("qt", q_t, 0, S_Q)
            high_tile_t("qt", q_t, 1, S_Q)
            act.wait_ge(k_max, 2)
            for p in range(KB):
                wait_full(act, "n", "m", p)
                nc.scalar.activation(mm[:, 0, p, :], bank("n", p % 2), ACT.Identity, scale=krec[:, p:p + 1]).then_inc(high["n"], 1)
            high_tile_t("qt", q_t, 2, S_Q)
            high_tile_t("qt", q_t, 3, S_Q)
            for t in range(T):
                if t + 4 < T:
                    high_tile_t("qt", q_t, t + 4, S_Q)
                windows("mix", t // 2, t % 2, 2)
            split_weight("down0")
            act.wait_ge(rare_ready, 1)
            is_rare = act.value_load(rare[0:1, 0:1], min_val=0, max_val=1)
            with act.If(is_rare):
                with act.Fori(0, NW) as w:
                    act.wait_ge(g_full, w + 1)
                    nc.scalar.activation(adj[:, :, bass.ts(w, WIN)], ps[0:P, 6, 0:WK].rearrange("p (d h) -> p h d", h=T),
                                         ACT.Copy).then_inc(g_high, 1)
            nc.scalar.preload_act_table(ACT.Sqrt)
            act.wait_ge(bias_ready, 1)

            def prelu(phase, turn, dst, bias):
                def product(i, m):
                    wait_full(act, "t", phase, i + m)
                    act.wait_ge(tmp_free, i + (turn + m + 1))
                    nc.scalar.activation(act_tmp[:, m, :], bank("t", m), ACT.Identity, bias=bias(m), scale=1 / S_W
                                         ).then_inc(free["t", "act"], 1)

                def top(j, m):
                    act.wait_ge(prelu_out, KB * j + (turn + m + 1))
                    nc.scalar.activation(dst[:, 0, m, bass.ts(j, CH)], act_tmp[:, m, :], ACT.Copy).then_inc(hid_high, 1)

                with act.Fori(0, J) as j:
                    for m in range(KB):
                        product(KB * j, m)
                        if m:
                            top(j, m - 1)
                    top(j, KB - 1)

            def hidden(i):
                m, j = divmod(i, J)
                wait_full(act, "t", "ffn1", i)
                act.wait_ge(tmp_free, 2 * KB * J + i + 1)
                for out in (hid_t[:, 0, m, j * CH:(j + 1) * CH], act_tmp[:, i % KB, :]):
                    last = nc.scalar.activation(out, bank("t", i % KB), ACT.Relu, bias=b1m[:, m:m + 1], scale=1 / S_W)
                last.then_inc(free["t", "act"], 1)

            def relu_chunk(layer, chunk, lo=0, hi=KB):
                for m in range(lo, hi):
                    nc.scalar.activation(gnn_t[:, m, chunk], gnn_t[:, m, chunk], ACT.Relu, bias=bn_shift[:, m:m + 1],
                                         scale=bn_scale[:, m:m + 1]).then_inc(layer_out, 1)

            for layer in range(L):
                def high_sums(i, chunk):
                    for m in range(KB):
                        wait_full(act, "t", f"agg{layer}", i + m)
                        nc.scalar.activation(h_t[:, 0, m, chunk], bank("t", m), ACT.Copy, scale=S_H / S_X
                                             ).then_inc(high["t"], 1)

                high_sums(0, slice(0, CH))
                high_sums(KB, slice(CH, 2 * CH))
                if layer == 0:
                    deviations(0, T, TURN["mix"])
                    act.wait_ge(norm_ready, TURN["mix"] + 1)
                    for t in range(4):
                        normalize(mix_nat, mix_nat, t)
                with act.Fori(2, J) as j:
                    high_sums(KB * j, bass.ts(j, CH))
                    for t_ in (2 * j, 2 * j + 1) if layer == 0 else ():
                        nc.scalar.activation(mix_nat[:, t_, :], mix_nat[:, t_, :], ACT.Identity, bias=shift[0:P, bass.ds(t_, 1)],
                                             scale=rstd[0:P, bass.ds(t_, 1)]).then_inc(ln_done, 1)
                prelu(f"up{layer}", 20 * layer, a_t, lambda m: bias_a[:, KB * layer + m:KB * layer + m + 1])
                if layer == 0:
                    act.wait_ge(mixed, T)
                def down_out(i, m, chunk):
                    wait_full(act, "t", f"down{layer}", i + m)
                    nc.scalar.activation(gnn_t[:, m, chunk], bank("t", m), ACT.Identity,
                                         bias=col("b2", KB * layer + m), scale=1 / (S_W * S_H)).then_inc(free["t", "act"], 1)

                with act.Fori(0, J - 1) as j:
                    for m in range(KB):
                        down_out(KB * j, m, bass.ts(j, CH))
                turn = TURN["bn"] + 2 * layer
                for m in range(KB - 1):
                    down_out(KB * (J - 1), m, slice((J - 1) * CH, N))
                deviations(0, KB - 1, turn, rows_=128)
                down_out(KB * (J - 1), KB - 1, slice((J - 1) * CH, N))
                act.wait_ge(norm_ready, turn + 1)
                relu_chunk(layer, slice(0, CH), 0, KB - 1)
                deviations(KB - 1, KB, turn + 1, rows_=128)
                act.wait_ge(norm_ready, turn + 2)
                relu_chunk(layer, slice(0, CH), KB - 1, KB)
                if layer == 0:
                    with act.Fori(0, J - 1) as j:
                        for c in range(2):
                            relu_chunk(layer, bass.ts(j + 1, CH), 2 * c, 2 * c + 2)
                            high_tile_nat("x", "x1", gnn_nat, S_X, 2 * j + c, c)
                    for t in (T - 2, T - 1):
                        high_tile_nat("x", "x1", gnn_nat, S_X, t, t % 2)

            def gate_chunk(j):
                for m in range(KB):
                    wait_full(act, "t", "gate", KB * j + m)
                    nc.scalar.activation(bank("t", m), bank("t", m), ACT.Relu, bias=col("gfc1_b", m), scale=S_XW,
                                         accum_out=gsum[:, m, j:j + 1]).then_inc(free["t", "act"], 1)

            for g in range(HT + 2):
                if g + 1 < HT:
                    relu_chunk(L - 1, slice((g + 1) * CH, (g + 2) * CH))
                if g < HT:
                    deviations(2 * g, 2 * g + 2, TURN["x2"] + g, scaled=1)
                if 1 <= g <= HT:
                    for t in (2 * g - 2, 2 * g - 1):
                        high_tile_t("x2", x2_t, t)
                if g < HT:
                    act.wait_ge(norm_ready, TURN["x2"] + g + 1)
                    for t in (2 * g, 2 * g + 1):
                        normalize(x2_nat, x, t)
                if g >= 2:
                    gate_chunk(g - 2)

            act.wait_ge(g_vec, 1)
            for k in range(PE_EXPERTS):
                e = E - PE_EXPERTS + k
                nc.scalar.activation(g_diag[:, k, :], ident[:, :], ACT.Copy, scale=gcol[:, e:e + 1]).then_inc(diag_ready, 1)
            for part in range(FB):
                act.wait_ge(merged, 2 * E * (part + 1))
                nc.scalar.activation(w1m[:, 0, :, part * 128:(part + 1) * 128], wm32[:, 0, :].rearrange("p (k f) -> p k f", k=KB)
                                     [:, :, part * 128:(part + 1) * 128], ACT.Copy, scale=S_W).then_inc(wm_high, 1)
            act.wait_ge(b1_done, 1)
            for i in range(FB * J - 2):
                hidden(i)
            for h in range(2):
                act.wait_ge(merged, 2 * E * FB + 2 * (E - PE_EXPERTS) + h + 1)
                part = slice(h * D, (h + 1) * D)
                nc.scalar.activation(wm16[:, 1, 0, part], wm32[:, 1, part], ACT.Copy, scale=S_W).then_inc(wm_high, 1)
            for i in range(FB * J - 2, FB * J):
                hidden(i)
            for g in range(HT):
                deviations(2 * g, 2 * g + 2, TURN["out"] + g, scaled=2)
                act.wait_ge(norm_ready, TURN["out"] + g + 1)
                for t in (2 * g, 2 * g + 1):
                    normalize(x2_nat, x2_nat, t)

        @block.vector
        def _(dve):
            steps = [0]

            def then(ins):
                ins.then_inc(dve_step, 1)
                steps[0] += 1
                dve.wait_ge(dve_step, steps[0])

            def first_column(w):
                return dve.value_load(window_at[0:1, w:w + 1], min_val=0, max_val=COLS)

            column = []

            def windows(phase, i, part, parts):
                for w, slot in window_list(phase, i, part, parts):
                    at = column.pop() if column else first_column(w)
                    dve.wait_ge(adj_full, w + 1)
                    nc.vector.tensor_tensor(rel[:, slot], keys[:, bass.ds(at, WC)].unsqueeze(2).to_broadcast([P, WC, T]),
                                            win_key[:, w:w + 1].unsqueeze(2).to_broadcast([P, WC, T]),
                                            ALU.subtract).then_inc(rel_ready, 1)
                    nc.vector.tensor_tensor(oh_s[:, slot], iota_s, sources[:, bass.ds(at, WC)].unsqueeze(1)
                                            .to_broadcast([P, P, WC]), ALU.is_equal)
                    dve.wait_ge(rel_ready, w + 1)
                    nc.vector.tensor_tensor(oh_d[:, slot], iota_d.unsqueeze(2).to_broadcast([P, WIN, WC, T]),
                                            rel[:, slot].unsqueeze(1).to_broadcast([P, WIN, WC, T]), ALU.is_equal
                                            ).then_inc(oh_ready, 1)
                    if w + 1 < NW:
                        column.append(first_column(w + 1))

            def low(out, src, hi, scale=1.0):
                if isinstance(scale, float) and scale == 1.0:
                    return nc.vector.tensor_tensor(out, src, hi, ALU.subtract)
                return nc.vector.scalar_tensor_tensor(out, src, scale, hi, ALU.mult, ALU.subtract)

            def low_tile_nat(family, phase, dst, scale, t, slot):
                wait_high(dve, family, phase, t)
                low(dst[:, 1, t, :], bank(family, slot)[0:P, :], dst[:, 0, t, :], scale).then_inc(free[family, "dve"], 1)

            def aggregate(lo, hi):
                for t_ in range(lo, hi):
                    last = nc.vector.bn_aggr(mv[0:P, t_, :], stat[0:P, 6 * t_:6 * t_ + 6])
                last.then_inc(var_ready, 1)

            def normalizer(lo, hi, turn):
                dve.wait_ge(std_ready, turn + 1)
                then(nc.vector.reciprocal(rstd[0:P, lo:hi], std[0:P, lo:hi]))
                nc.vector.scalar_tensor_tensor(shift[0:P, lo:hi], mv[0:P, lo:hi, 0], -1.0, rstd[0:P, lo:hi], ALU.mult,
                                               ALU.mult).then_inc(norm_ready, 1)

            def pair_statistics(src, g):
                for t in (2 * g, 2 * g + 1):
                    last = nc.vector.bn_stats(stat[0:P, 6 * t:6 * t + 6], src[:, t, :])
                then(last)
                aggregate(2 * g, 2 * g + 2)

            def low_tile_t(phase, dst, t, scale=1.0):
                wait_high(dve, "x", phase, t)
                tile = slice(t * P, (t + 1) * P)
                low(dst[:, 1, :, tile], bank("x", t % 2)[:, 0:KB * P].rearrange("p (k n) -> p k n", k=KB), dst[:, 0, :, tile],
                    scale).then_inc(free["x", "dve"], 1)

            def high_weight(name):
                i = WEIGHTS.index(name)
                dve.wait_ge(w_scaled, i + 1)
                wait_slot(dve, i)
                nc.vector.tensor_copy(wslot[:, i % SLOTS, 0].rearrange("p k n -> p (k n)"), stage[:, :]).then_inc(w_high, 1)

            for g in range(-2, HT + 1):
                if g + 2 < HT:
                    dve.wait_ge(got_x[g + 2], 16)
                    pair_statistics(x, g + 2)
                if 0 <= g + 1 < HT:
                    normalizer(2 * g + 2, 2 * g + 4, TURN["xn"] + g + 1)
                if g > 0:
                    for t in (2 * g - 2, 2 * g - 1):
                        low_tile_t("xn", xn_t, t)
                if g == 1:
                    high_weight("lin")

            def prelu(phase, base, src, neg, alpha, done):
                with dve.Fori(0, J) as j:
                    for m in range(0, KB, 2):
                        for q in (m, m + 1):
                            wait_done(dve, "t", phase, KB * j + q + 1)
                            nc.vector.tensor_scalar(neg[:, q, :], src(q, j), 0.0, alpha(q), ALU.min, ALU.mult
                                                    ).then_inc(dve_step, 1)
                        for q in (m, m + 1):
                            dve.wait_ge(dve_step, KB * j + (base + q + 1))
                            nc.vector.scalar_tensor_tensor(src(q, j), src(q, j), 0.0, neg[:, q, :], ALU.max, ALU.add
                                                           ).then_inc(done, 1)
                steps[0] += KB * J

            dve.wait_ge(got_edges, 32)
            then(nc.vector.tensor_scalar(src_tile, ints[:, 0, :], float(P), None, ALU.is_ge))
            for h in range(2, T):
                then(nc.vector.scalar_tensor_tensor(src_tile, ints[:, 0, :], float(P * h), src_tile, ALU.is_ge, ALU.add))
            dve.wait_ge(iotas, 1)
            nc.vector.scalar_tensor_tensor(keys[:, 0:COLS], ints[:, 1, :], float(T), src_tile, ALU.mult, ALU.add)
            nc.vector.scalar_tensor_tensor(sources[:, 0:COLS], src_tile, -float(P), ints[:, 0, :], ALU.mult, ALU.add)
            nc.vector.tensor_copy(iota_mem[:, 0:WK], iota_i[:, 0:WK])
            nc.vector.tensor_copy(iota_s, iota_i[:, 0:P].unsqueeze(2).to_broadcast([P, P, WC]))
            nc.vector.tensor_copy(win_key[:, :], iota_i[:, WK:])
            nc.vector.tensor_copy(heads, heads_i)
            then(nc.vector.tensor_copy(first[:, 0:1], first_i))
            then(nc.vector.tensor_scalar(heads_lt, heads, first[:, 0:1], None, ALU.is_lt, ALU.add, accum_out=first[:, 1:2]))
            nc.vector.tensor_scalar(first[:, 1:2], first[:, 1:2], -1.0, 0.0, ALU.add, ALU.max).then_inc(firsts, 1)
            high_weight("k")
            dve.wait_ge(got_cols, 16)
            prelu("lin", steps[0], lambda m, j: gnn_t[:, m, bass.ts(j, CH)], lin_neg, lambda m: col("lin_a", m), lin_out)
            dve.wait_ge(firsts_row, 1)
            nc.vector.tensor_copy(window_at[:, :], ps[0:1, 7, 0:NW]).then_inc(window_ready, 1)
            dve.wait_ge(window_ready, 1)
            for j in range(J):
                for m in range(KB):
                    windows("k", j, m, KB)
                    wait_full(dve, "t", "k", KB * j + m)
                    nc.vector.tensor_scalar(k_t[:, m, j * CH:(j + 1) * CH], bank("t", m), S_XW, None, ALU.mult, ALU.max,
                                            accum_out=kmax[:, m, j:j + 1]).then_inc(free["t", "dve"], 1)
                    if m % 2:
                        low_tile_nat("x", "x0", gnn_nat, S_X, 2 * j + m // 2, m // 2)
            wait_done(dve, "t", "k", 20)
            nc.vector.tensor_reduce(kneg[:, :], kmax[:, :, :], AX.X, ALU.max, negate=True).then_inc(k_max, 1)
            def heads_of(ap):
                return ap.rearrange("p (h d) -> p h d", h=H)

            def per_head(ap):
                return ap.unsqueeze(2).to_broadcast([P, H, DH])

            for i in range(HT + 1):
                for t_ in (2 * i, 2 * i + 1) if i < HT else ():
                    wait_full(dve, "n", "q", t_)
                    then(nc.vector.tensor_reduce(qmax[:, t_, :], heads_of(bank("n", t_ % 2)[0:P, :]), AX.X, ALU.max))
                    nc.vector.tensor_tensor(heads_of(q_nat[:, t_, :]), heads_of(bank("n", t_ % 2)[0:P, :]),
                                            per_head(qmax[:, t_, :]), ALU.subtract).then_inc(free["n", "dve"], 1)
                for t_ in (2 * i - 2, 2 * i - 1) if i else ():
                    low_tile_nat("x", "kn", k_nat, S_K, t_, t_ % 2)
                for t_ in (2 * i, 2 * i + 1) if i < HT else ():
                    dve.wait_ge(q_exp, t_ + 1)
                    then(nc.vector.tensor_reduce(qsum[:, t_, :], heads_of(q_nat[:, t_, :]), AX.X, ALU.add))
                    nc.vector.reciprocal(qsum[:, t_, :], qsum[:, t_, :]).then_inc(q_rec, 1)
            for t in range(T):
                windows("v", t // 2, t % 2, 2)
                low_tile_nat("n", "v", v_nat, 1 / S_W, t, t % 2)
            dve.wait_ge(k_exp, KB)
            nc.vector.reciprocal(krec[:, :], ksum[:, :]).then_inc(k_max, 1)
            dve.wait_ge(k_max, 2)
            for b in range(2):
                wait_high(dve, "x", "ctx", b)
                for hh in range(2):
                    part = slice(hh * DH, hh * DH + DH)
                    last = low(ctx16[part, 1, 2 * b:2 * b + 2, part],
                               bank("x", b)[part, 0:256].rearrange("p (q d) -> p q d", q=2)[:, :, part],
                               ctx16[part, 0, 2 * b:2 * b + 2, part], 1 / (S_X * S_K))
                last.then_inc(free["x", "dve"], 1)
            low_tile_t("qt", q_t, 0, S_Q)
            low_tile_t("qt", q_t, 1, S_Q)
            for p in range(KB):
                wait_high(dve, "n", "m", p)
                low(mm[:, 1, p, :], bank("n", p % 2), mm[:, 0, p, :], krec[:, p:p + 1]).then_inc(free["n", "dve"], 1)
            def add_self(lo, hi):
                for h in range(lo, hi):
                    diagonal = adj[:, h, h * P:(h + 1) * P]
                    last = nc.vector.tensor_tensor(diagonal, diagonal, ident[0:P, 0:P], ALU.add)
                return last

            dve.wait_ge(adj_freed, 2 + first_window("mix"))
            low_tile_t("qt", q_t, 2, S_Q)
            low_tile_t("qt", q_t, 3, S_Q)
            add_self(0, DONE_EARLY).then_inc(self_early, 1)
            dve.wait_ge(got_rows, 16)
            for t in range(T):
                windows("mix", t // 2, t % 2, 2)
                if t + 4 < T:
                    low_tile_t("qt", q_t, t + 4, S_Q)
                wait_full(dve, "n", "mix", t)
                nc.vector.scalar_tensor_tensor(mix_nat[:, t, :], bank("n", t % 2)[0:P, :],
                                               1 / (S_Q * S_M * DH ** 0.5 * N), rows[:, 0, :], ALU.mult, ALU.add
                                               ).then_inc(free["n", "dve"], 1)
            wait_done(dve, "n", "mix", T)

            dve.wait_ge(adj_freed, 2 + NW)
            nc.vector.tensor_reduce(chk[:, 0:1], adj_sum[:, :], AX.X, ALU.add)
            nc.vector.tensor_scalar(stat[0:P, 64:64 + NW], adj_sum[:, :], F16_EXACT, None, ALU.is_ge, ALU.add,
                                    accum_out=chk[:, 1:2]).then_inc(chk_ready, 1)
            dve.wait_ge(chk_sum, 1)
            then(nc.vector.tensor_copy(chk[0:1, 2:4], ps[0:1, 6, 0:2]))
            then(nc.vector.scalar_tensor_tensor(chk[0:1, 2:3], chk[0:1, 2:3], float(EDGES), chk[0:1, 3:4], ALU.not_equal, ALU.add))
            nc.vector.tensor_scalar(rare[:, 0:1], chk[0:1, 2:3], 0.0, None, ALU.is_gt).then_inc(rare_ready, 1)
            dve.wait_ge(rare_ready, 1)
            is_rare = dve.value_load(rare[0:1, 0:1], min_val=0, max_val=1)
            with dve.If(is_rare):
                nc.vector.memset(general[:, 2, :], 0.0).then_inc(g_low, 1)
                nc.vector.memset(rel[:, 0], 0.0).then_inc(g_oh, 1)
                with dve.Fori(0, NW) as w:
                    with dve.Fori(0, COLS // 2) as c:
                        dve.wait_ge(g_used, w * (COLS // 2) + c + 1)
                        for b in range(2):
                            e = 2 * c + b
                            nc.vector.tensor_scalar(general[:, b, P:], iota_mem[:, 0:WK], win_key[:, bass.ds(w, 1)],
                                                    keys[:, bass.ds(e, 1)], ALU.add, ALU.is_equal)
                            last = nc.vector.tensor_tensor(general[:, b, 0:P], iota_mem[:, 0:P], sources[:, bass.ds(e, 1)]
                                                           .to_broadcast([P, P]), ALU.is_equal)
                        last.then_inc(g_oh, 1)
                    dve.wait_ge(g_high, w + 1)
                    counts = ps[0:P, 6, 0:WK].rearrange("p (d h) -> p h d", h=T)
                    part = bass.ts(w, WIN)
                    nc.vector.tensor_tensor(lo_a[:, :, part], counts[:, 0:LO_TILES, :], adj[:, 0:LO_TILES, part], ALU.subtract)
                    nc.vector.tensor_tensor(lo_b[:, :, part], counts[:, LO_TILES:T, :], adj[:, LO_TILES:T, part], ALU.subtract
                                            ).then_inc(g_low, 1)
                dve.wait_ge(g_low, NW + 1)
                for h in range(T):
                    low_ = lo_a[:, h] if h < LO_TILES else lo_b[:, h - LO_TILES]
                    last = nc.vector.tensor_tensor(low_[:, h * P:(h + 1) * P], low_[:, h * P:(h + 1) * P], ident[0:P, 0:P], ALU.add)
                last.then_inc(adj_ready, 1)
            with dve.Else():
                add_self(DONE_EARLY, T).then_inc(adj_ready, 1)

            nc.vector.tensor_scalar(bias_a[:, :], col("b1", 0, 2 * KB), S_H, None, ALU.mult).then_inc(bias_ready, 1)


            for layer in range(L):
                def mix_statistics(m):
                    tiles = range(m * T // KB, (m + 1) * T // KB)
                    for t in tiles:
                        ins = nc.vector.bn_stats(stat[0:P, 6 * t:6 * t + 6], mix_nat[:, t, :])
                    if m == KB - 1:
                        then(ins)

                def low_sums(i, chunk, between=lambda m: None):
                    for m in range(KB):
                        wait_high(dve, "t", f"agg{layer}", i + m)
                        low(h_t[:, 1, m, chunk], bank("t", m), h_t[:, 0, m, chunk], S_H / S_X).then_inc(free["t", "dve"], 1)
                        between(m)

                low_sums(0, slice(0, CH))
                low_sums(KB, slice(CH, 2 * CH), mix_statistics if layer == 0 else lambda m: None)
                if layer == 0:
                    aggregate(0, T)
                    normalizer(0, T, TURN["mix"])
                with dve.Fori(2, J) as j:
                    low_sums(KB * j, bass.ts(j, CH))
                if layer:
                    high_weight("down1")
                prelu(f"up{layer}", steps[0], lambda m, j: act_tmp[:, m, :], negative, lambda m: col("conv_a", layer), prelu_out)
                high_weight("gate" if layer else "up1")
                bn_stat = stat[:, :].rearrange("p (m j s) -> p m (j s)", m=KB, j=J)
                with dve.Fori(0, J - 1) as j:
                    for m in range(KB):
                        wait_done(dve, "t", f"down{layer}", KB * j + m + 1)
                        ins = nc.vector.bn_stats(bn_stat[:, m, bass.ts(j, 6)], gnn_t[:, m, bass.ts(j, CH)])
                    ins.then_inc(dve_step, 1)
                steps[0] += J - 1
                for part, (lo, hi) in enumerate(BN_PARTS):
                    for m in range(lo, hi):
                        wait_done(dve, "t", f"down{layer}", KB * (J - 1) + m + 1)
                        ins = nc.vector.bn_stats(bn_stat[:, m, 6 * (J - 1):], gnn_t[:, m, (J - 1) * CH:])
                    then(ins)
                    for m in range(lo, hi):
                        last = nc.vector.bn_aggr(mv[:, m, :], bn_stat[:, m, :])
                    last.then_inc(var_ready, 1)
                    dve.wait_ge(std_ready, TURN["bn"] + 2 * layer + part + 1)
                    scale, shift_ = bn_scale[:, lo:hi], bn_shift[:, lo:hi]
                    then(nc.vector.reciprocal(scale, std[:, lo:hi]))
                    then(nc.vector.tensor_tensor(scale, scale, col("gamma", KB * layer + lo, hi - lo), ALU.mult))
                    then(nc.vector.tensor_tensor(shift_, mv[:, lo:hi, 0], scale, ALU.mult))
                    nc.vector.tensor_tensor(shift_, col("beta", KB * layer + lo, hi - lo), shift_, ALU.subtract
                                            ).then_inc(norm_ready, 1)
                if layer == 0:
                    with dve.Fori(0, HT) as i:
                        for c in range(2):
                            low_tile_nat("x", "x1", gnn_nat, S_X, 2 * i + c, c)

            dve.wait_ge(mixed, T)
            for g in range(HT + 1):
                if g < HT:
                    for t in (2 * g, 2 * g + 1):
                        wait_full(dve, "y", "gnn", t)
                        nc.vector.tensor_tensor(x[:, t, :], bank("y", t % 2)[0:P, :], x[:, t, :], ALU.add
                                                ).then_inc(free["y", "dve"], 1)
                    wait_done(dve, "y", "gnn", 2 * g + 2)
                    pair_statistics(x, g)
                if g:
                    for t in (2 * g - 2, 2 * g - 1):
                        low_tile_t("x2", x2_t, t)
                if g < HT:
                    normalizer(2 * g, 2 * g + 2, TURN["x2"] + g)
            dve.wait_ge(got_ln, 32)
            then(nc.vector.tensor_scalar(b2_row, b2_row, S_X, None, ALU.mult))
            then(nc.vector.tensor_scalar(rows[:, 0:2, :], rows[:, 0:2, :], 1 - LN_MERGE * E, None, ALU.mult))
            for r in range(2):
                wait_full(dve, "x", "rows", r)
                nc.vector.scalar_tensor_tensor(rows[:, r, :], bank("x", r)[0:P, :], LN_MERGE, rows[:, r, :], ALU.mult, ALU.add
                                               ).then_inc(free["x", "dve"], 1)
            wait_done(dve, "t", "gate", 20)
            then(nc.vector.tensor_reduce(gmean[:, :], gsum[:, :, :], AX.X, ALU.add))
            nc.vector.tensor_scalar(gbc[:, :, :], gmean[:, :].unsqueeze(2).to_broadcast([128, KB, 128]), 1 / N, None, ALU.mult
                                    ).then_inc(g_bc, 1)
            wait_full(dve, "x", "g", 0)
            nc.vector.tensor_tensor(gcol[:, :], bank("x", 0)[:, 0:E], col("gfc2_b", 0, E), ALU.add).then_inc(free["x", "dve"], 1)
            wait_full(dve, "x", "g", 1)
            nc.vector.tensor_scalar(grow[:, :], bank("x", 1)[0:E, 0:P], cols[0:E, COL["gfc2_bc"][0]:COL["gfc2_bc"][0] + 1], None,
                                    ALU.add).then_inc(g_vec, 1)
            wait_done(dve, "x", "g", 1)
            dve.wait_ge(got_wm, 16)
            dve.wait_ge(got_tv, 32)
            half_done = [0]

            def merge(total, task, experts=E):
                halves = [(total[:, k:k + n], lambda e, k=k, n=n: task(e)[:, k:k + n])
                          for n in [total.shape[1] // 2] for k in (0, n)]
                for e in range(experts):
                    for h, (out, part) in enumerate(halves):
                        if e:
                            dve.wait_ge(merged, half_done[0] + 2 * e + h - 1)
                        nc.vector.scalar_tensor_tensor(out, part(e), gcol[:, e:e + 1], out, ALU.mult, ALU.add).then_inc(merged, 1)
                half_done[0] += 2 * experts
                dve.wait_ge(merged, half_done[0])

            def w1_part(ap, part):
                return ap.rearrange("p (k f) -> p k f", k=KB)[:, :, part * 128:(part + 1) * 128]

            for part in range(FB):
                merge(w1_part(wm32[:, 0, :], part), lambda e: w1_part(tv[:, 0, e, :], part))
                if part == 0:
                    dve.wait_ge(b2_sum, 1)
                    nc.vector.scalar_tensor_tensor(b2_row, ps[0:P, 7, :], S_X, b2_row, ALU.mult, ALU.add).then_inc(b2_ready, 1)
                    scratch = stat[:, 0:FB * E].rearrange("p (f e) -> p f e", f=FB)
                    then(nc.vector.tensor_tensor(scratch, col("tv_b1", 0, FB * E).rearrange("p (f e) -> p f e", f=FB),
                                                 gcol[:, :].unsqueeze(1).to_broadcast([128, FB, E]), ALU.mult))
                    then(nc.vector.tensor_reduce(b1m[:, :], scratch, AX.X, ALU.add))
                    then(nc.vector.tensor_tensor(b1m[:, :], b1m[:, :], col("ffn_b1", 0, FB), ALU.add))
                    nc.vector.tensor_scalar(b1m[:, :], b1m[:, :], S_X, None, ALU.mult).then_inc(b1_done, 1)
                dve.wait_ge(wm_high, part + 1)
                low(w1m[:, 1, :, part * 128:(part + 1) * 128], w1_part(wm32[:, 0, :], part),
                    w1m[:, 0, :, part * 128:(part + 1) * 128], S_W).then_inc(wm_split, 1)

            def rows_of(ap):
                return ap.rearrange("p (k n) -> p k n", k=2)

            merge(rows_of(wm32[:, 1, :]), lambda e: rows_of(tv[:, 1, e, :]), E - PE_EXPERTS)
            dve.wait_ge(w2_part, 1)
            for h in range(2):
                part = wm32[:, 1, h * D:(h + 1) * D]
                nc.vector.tensor_tensor(part, ps[:, 4 + h, :], part, ALU.add).then_inc(merged, 1)
            for h in range(2):
                dve.wait_ge(merged, half_done[0] + h + 1)
                dve.wait_ge(wm_high, FB + h + 1)
                part = slice(h * D, (h + 1) * D)
                low(wm16[:, 1, 1, part], wm32[:, 1, part], wm16[:, 1, 0, part], S_W).then_inc(wm_split, 1)
            for g in range(HT + 1):
                if g < HT:
                    for t in (2 * g, 2 * g + 1):
                        wait_full(dve, "n", "ffn2", t)
                        dve.wait_ge(b2_added, t + 1)
                        nc.vector.scalar_tensor_tensor(x2_nat[:, t, :], bank("n", t % 2)[0:P, :], S_XW * S_X, x2_nat[:, t, :],
                                                       ALU.mult, ALU.add).then_inc(free["n", "dve"], 1)
                    wait_done(dve, "n", "ffn2", 2 * g + 2)
                    pair_statistics(x2_nat, g)
                if g:
                    for t in (2 * g - 2, 2 * g - 1):
                        if not pool_scales(t):
                            dve.wait_ge(ln_done, 3 * T + t + 1)
                            nc.vector.tensor_tensor(x2_nat[:, t, :], x2_nat[:, t, :], rows[:, 0, :], ALU.mult).then_inc(scaled, 1)
                if g < HT:
                    normalizer(2 * g, 2 * g + 2, TURN["out"] + g)

            dve.wait_ge(scaled, sum(not pool_scales(t) for t in range(T)))
            dve.wait_ge(xb_ready, T)
            nc.vector.tensor_tensor(x2_nat[:, T - 1, :], x2_nat[:, T - 1, :], x[:, T - 1, :], ALU.add).then_inc(last_ready, 1)

        @block.gpsimd
        def _(pool):
            steps = [0]

            def then(ins):
                ins.then_inc(pool_step, 1)
                steps[0] += 1
                pool.wait_ge(pool_step, steps[0])

            nc.gpsimd.memset(keys[:, COLS:KEYS], -1.0)
            nc.gpsimd.memset(sources[:, COLS:KEYS], 0.0)
            nc.gpsimd.iota(iota_i[:, 0:WK], pattern=[[1, WK]], base=0, channel_multiplier=0)
            nc.gpsimd.iota(iota_i[:, WK:], pattern=[[WK, NW]], base=0, channel_multiplier=0)
            nc.gpsimd.iota(first_i, pattern=[[0, 1]], base=0, channel_multiplier=WIN).then_inc(iotas, 1)
            nc.gpsimd.memset(eps[:, 0:1], LN_EPS)
            nc.gpsimd.memset(eps[:, 1:2], LN_EPS / (S_X * S_X))
            nc.gpsimd.memset(eps[:, 2:3], LN_EPS * (S_X * S_X))
            nc.gpsimd.memset(ones[:, :], 1.0)
            nc.gpsimd.memset(ctx16[:, :, :, :], 0.0)
            then(nc.gpsimd.memset(ident[:, :], 0.0))
            nc.gpsimd.affine_select(out=ident[:, :], in_=ident[:, :], compare_op=ALU.not_equal, fill=1.0, base=0,
                                    pattern=[[-1, 128]], channel_multiplier=1).then_inc(consts, 1)

            def split_weight(name):
                i = WEIGHTS.index(name)
                pool.wait_ge(got_w, 16 * (i + 1))
                nc.gpsimd.tensor_scalar(stage[:, :], stage[:, :], S_W, 1.0, ALU.mult, ALU.mult).then_inc(w_scaled, 1)
                pool.wait_ge(w_high, i + 1)
                nc.gpsimd.tensor_tensor(wslot[:, i % SLOTS, 1].rearrange("p k n -> p (k n)"), stage[:, :],
                                        wslot[:, i % SLOTS, 0].rearrange("p k n -> p (k n)"), ALU.subtract).then_inc(w_split, 1)

            for name in ("lin", "k", "q", "v"):
                split_weight(name)
            with pool.Fori(0, T) as t_:
                pool.wait_ge(q_rec, t_ + 1)
                tile = q_nat[:, bass.ds(t_, 1), :].rearrange("p o (h d) -> p (o h) d", h=H)
                nc.gpsimd.tensor_tensor(tile, tile, qsum[:, bass.ds(t_, 1), :].rearrange("p o h -> p (o h)").unsqueeze(2)
                                        .to_broadcast([P, H, DH]), ALU.mult).then_inc(q_soft, 1)
            for name in ("out", "up0", "down0"):
                split_weight(name)
            base = steps[0]
            with pool.Fori(0, T) as t_:
                pool.wait_ge(ln_done, T + t_ + 1)
                tile = mix_nat[:, t_, :]
                nc.gpsimd.tensor_tensor(tile, tile, rows[:, 1, :], ALU.mult).then_inc(pool_step, 1)
                pool.wait_ge(pool_step, t_ + (base + 1))
                nc.gpsimd.tensor_tensor(x[:, t_, :], x[:, t_, :], tile, ALU.add).then_inc(mixed, 1)
            steps[0] += T

            def low_prelu(layer):
                with pool.Fori(0, J) as j:
                    for m in range(KB):
                        pool.wait_ge(hid_high, KB * j + (KB * J * layer + m + 1))
                        nc.gpsimd.tensor_tensor(a_t[:, 1, m, bass.ts(j, CH)], act_tmp[:, m, :], a_t[:, 0, m, bass.ts(j, CH)],
                                                ALU.subtract).then_inc(tmp_free, 1)

            low_prelu(0)
            split_weight("up1")
            split_weight("down1")
            low_prelu(1)
            split_weight("gate")
            pool.wait_ge(ln_done, 3 * T)
            wait_done(pool, "x", "rows", 2)
            def add_ln_b(t):
                nc.gpsimd.tensor_tensor(x[:, t, :], x[:, t, :], rows[:, 1, :], ALU.add).then_inc(xb_ready, 1)

            def add_b2(t):
                nc.gpsimd.tensor_tensor(x2_nat[:, t, :], x2_nat[:, t, :], b2_row, ALU.add).then_inc(b2_added, 1)

            def low_hidden(i):
                m, j = divmod(i, J)
                chunk = slice(j * CH, (j + 1) * CH)
                wait_done(pool, "t", "ffn1", i + 1)
                nc.gpsimd.tensor_tensor(hid_t[:, 1, m, chunk], act_tmp[:, i % KB, :], hid_t[:, 0, m, chunk], ALU.subtract
                                        ).then_inc(tmp_free, 1)

            for t in range(T - 2):
                add_ln_b(t)
            pool.wait_ge(b2_ready, 1)
            for t in range(HT + 1):
                add_b2(t)
            for i in range(FB * J):
                low_hidden(i)
                if i % 2 and HT + 1 + i // 2 < T:
                    add_b2(HT + 1 + i // 2)
            for t in range(T - 2, T):
                add_ln_b(t)
            pool.wait_ge(xb_ready, T)
            for t in range(T - 1):
                if pool_scales(t):
                    pool.wait_ge(ln_done, 3 * T + t + 1)
                    then(nc.gpsimd.tensor_tensor(x2_nat[:, t, :], x2_nat[:, t, :], rows[:, 0, :], ALU.mult))
                else:
                    pool.wait_ge(scaled, sum(not pool_scales(u) for u in range(t + 1)))
                nc.gpsimd.tensor_tensor(x2_nat[:, t, :], x2_nat[:, t, :], x[:, t, :], ALU.add).then_inc(out_ready, 1)


def kernel(**inputs):
    import numpy as np
    import concourse.bacc as bacc
    from concourse.bass_utils import run_bass_kernel_spmd

    def arr(name):
        return np.asarray(inputs[name])

    def blocks(w):
        return np.ascontiguousarray(w.reshape(-1, 128, w.shape[-1]).transpose(1, 0, 2).reshape(128, -1))

    def columns(v):
        return v.reshape(-1, 128).T

    def spread(v, n):
        return np.broadcast_to(v, (n,) + v.shape)

    g, m, f = "L0_gnn_", "L0_mix_", "L0_ffn_"
    qkv = arr(m + "w_qkv")
    src, dst = (arr(n).reshape(COLS, P) for n in ("src", "dst"))
    gfc2_b = arr(f + "gfc2_b")
    gfc2_col = np.zeros((128, 1), gfc2_b.dtype)
    gfc2_col[:E, 0] = gfc2_b
    weights = {
        "lin": arr(g + "lin_W").T, "q": qkv[:, 0:D], "k": qkv[:, D:2 * D], "v": qkv[:, 2 * D:], "out": arr(m + "w_out"),
        "up0": arr(g + "conv_W1")[0].T, "up1": arr(g + "conv_W1")[1].T, "down0": arr(g + "conv_W2")[0].T,
        "down1": arr(g + "conv_W2")[1].T, "gate": arr(f + "gfc1_w").T,
    }
    arrays = {"w_" + n: blocks(w) for n, w in weights.items()}
    arrays["x"] = np.ascontiguousarray(arr("x").reshape(T, P, D).transpose(1, 0, 2))
    arrays["edges"] = np.ascontiguousarray(np.stack([src.T, dst.T], 1))
    arrays["heads"] = np.ascontiguousarray(spread(dst[:, 0], NW))
    arrays["cols"] = np.ascontiguousarray(np.concatenate([
        columns(arr(g + "lin_b")), columns(arr(g + "lin_a")), columns(arr(g + "conv_b1")), columns(arr(g + "conv_b2")),
        columns(arr(g + "bn_gamma")), columns(arr(g + "bn_beta")), spread(arr(g + "conv_a"), 128),
        columns(arr(f + "gfc1_b")), columns(arr(f + "b1")),
        arr(f + "tv_b1").reshape(E, FB, 128).transpose(2, 1, 0).reshape(128, FB * E), spread(gfc2_b, 128), gfc2_col], 1))
    arrays["mix_rows"] = np.ascontiguousarray(spread(np.stack([arr(m + "b_out"), arr(m + "ln_scale")]), P))
    arrays["ln_rows"] = np.ascontiguousarray(spread(np.stack([arr(f + "ln_g"), arr(f + "ln_b"), arr(f + "b2")]), P))
    arrays["tv_rows"] = np.ascontiguousarray(np.stack([arr(f + "tv_ln_g"), arr(f + "tv_ln_b"), arr(f + "tv_b2")], 1))
    arrays["gfc2"] = blocks(arr(f + "gfc2_w").T).reshape(128, KB, E)
    arrays["w_ffn"] = np.concatenate([blocks(arr(f + "W1").T), blocks(arr(f + "W2").T)], 1)
    arrays["tv"] = np.ascontiguousarray(np.stack(
        [np.stack([blocks(w.T) for w in arr(f + n)], 1) for n in ("tv_W1", "tv_W2")], 1))

    nc = bacc.Bacc("TRN2", target_bir_lowering=False, num_devices=1)
    dram = {n: nc.dram_tensor("in_" + n, a.shape, mybir.dt.from_np(a.dtype), kind="ExternalInput").ap()
            for n, a in arrays.items()}
    dram["out"] = nc.dram_tensor("out_0", (P, T, D), F32, kind="ExternalOutput").ap()
    gps_block(nc, dram)
    result = run_bass_kernel_spmd(nc, [{"in_" + n: a for n, a in arrays.items()}], core_ids=[0])
    return np.ascontiguousarray(result.results[0]["out_0"].transpose(1, 0, 2)).reshape(N, D)
```
